# Optimizing a Trainium2 kernel written in Bass

```python
import numpy as np
import jax
import jax.numpy as jnp

def _softmax(x, axis=-1):
    return jax.nn.softmax(x, axis=axis)

def _gelu(x):
    return jax.nn.gelu(x, approximate=True)

def _silu(x):
    return jax.nn.silu(x)

def _sigmoid(x):
    return jax.nn.sigmoid(x)

def _layernorm(x, axis=-1, eps=1e-05):
    m = jnp.mean(x, axis=axis, keepdims=True)
    v = jnp.var(x, axis=axis, keepdims=True)
    return (x - m) / jnp.sqrt(v + eps)

def _scatter_add(tgt, idx, src, axis=0):
    return tgt.at[idx].add(src)

def _segment_sum(src, seg, n):
    return jax.ops.segment_sum(src, seg, n)
kernel_name = 'mk_adaln_d1_jaxref_r8_ed8d82'

def setup_inputs(seed: int=0):
    np.random.seed(seed)
    _w = jnp.asarray

    def _L0_attn_setup():
        import math
        import jax, jax.numpy as jnp
        import numpy as np
        B, T, E, H = (2, 256, 256, 16)
        D = E // H

        def _alibi_slopes(n):
            start = 2.0 ** (-2.0 ** (-(math.log2(n) - 3)))
            return np.array([start * start ** i for i in range(n)], dtype=np.float32)
        key = jax.random.key(seed)
        ks = jax.random.split(key, 5)
        w_scale = 0.02
        return {'x': jax.random.normal(ks[0], (B, T, E), dtype=jnp.float32), 'Wq': jax.random.normal(ks[1], (E, E), dtype=jnp.float32) * w_scale, 'bq': jnp.zeros((E,), jnp.float32), 'Wk': jax.random.normal(ks[2], (E, E), dtype=jnp.float32) * w_scale, 'bk': jnp.zeros((E,), jnp.float32), 'Wv': jax.random.normal(ks[3], (E, E), dtype=jnp.float32) * w_scale, 'bv': jnp.zeros((E,), jnp.float32), 'Wo': jax.random.normal(ks[4], (E, E), dtype=jnp.float32) * w_scale, 'bo': jnp.zeros((E,), jnp.float32), 'slopes': jnp.asarray(_alibi_slopes(H))}
    _L0_attn_in = _L0_attn_setup()

    def _L0_ffn_setup():
        import jax, jax.numpy as jnp
        import numpy as np
        TOP_K = 4
        NUM_EXPERTS = 16
        key = jax.random.key(seed)
        ks = jax.random.split(key, 6)
        B, S, H, I, E = (2, 128, 256, 224, NUM_EXPERTS)
        return {'x': jax.random.normal(ks[0], (B, S, H), dtype=jnp.float32), 'router_w': jax.random.normal(ks[1], (E, H), dtype=jnp.float32) * 0.02, 'expert_bias': jnp.zeros((E,), dtype=jnp.float32), 'gate_proj': jax.random.normal(ks[2], (E, H, I), dtype=jnp.float32) * 0.02, 'up_proj': jax.random.normal(ks[3], (E, H, I), dtype=jnp.float32) * 0.02, 'down_proj': jax.random.normal(ks[4], (E, I, H), dtype=jnp.float32) * 0.02}
    _L0_ffn_in = _L0_ffn_setup()
    _L0_c = _w((lambda *s: np.random.randn(*s).astype(np.float32) * 0.05)(1, 256))
    _L0_wmod = _w((lambda *s: np.random.randn(*s).astype(np.float32) * 0.05)(256, 6 * 256) * 256 ** (-0.5))
    _d = {'L0_attn_x': _L0_attn_in['x'], 'L0_attn_Wq': _L0_attn_in['Wq'], 'L0_attn_bq': _L0_attn_in['bq'], 'L0_attn_Wk': _L0_attn_in['Wk'], 'L0_attn_bk': _L0_attn_in['bk'], 'L0_attn_Wv': _L0_attn_in['Wv'], 'L0_attn_bv': _L0_attn_in['bv'], 'L0_attn_Wo': _L0_attn_in['Wo'], 'L0_attn_bo': _L0_attn_in['bo'], 'L0_attn_slopes': _L0_attn_in['slopes'], 'L0_ffn_router_w': _L0_ffn_in['router_w'], 'L0_ffn_expert_bias': _L0_ffn_in['expert_bias'], 'L0_ffn_gate_proj': _L0_ffn_in['gate_proj'], 'L0_ffn_up_proj': _L0_ffn_in['up_proj'], 'L0_ffn_down_proj': _L0_ffn_in['down_proj'], 'L0_c': _L0_c, 'L0_wmod': _L0_wmod}
    _x0 = _d['L0_attn_x']
    _d['L0_attn_x'] = jax.random.normal(jax.random.fold_in(jax.random.key(seed), 1), (1, 1024, 256), dtype=_x0.dtype)
    del _x0
    return _d

def reference(L0_attn_x, L0_attn_Wq, L0_attn_bq, L0_attn_Wk, L0_attn_bk, L0_attn_Wv, L0_attn_bv, L0_attn_Wo, L0_attn_bo, L0_attn_slopes, L0_ffn_router_w, L0_ffn_expert_bias, L0_ffn_gate_proj, L0_ffn_up_proj, L0_ffn_down_proj, L0_c, L0_wmod):

    def _L0_attn_ref(x, Wq, bq, Wk, bk, Wv, bv, Wo, bo, slopes):
        import math
        import jax, jax.numpy as jnp
        import numpy as np
        B, T, E, H = (2, 256, 256, 16)
        D = E // H

        def _alibi_slopes(n):
            start = 2.0 ** (-2.0 ** (-(math.log2(n) - 3)))
            return np.array([start * start ** i for i in range(n)], dtype=np.float32)
        b, t, e = x.shape
        h, d = (H, e // H)
        scaling = d ** (-0.5)
        q = (jnp.einsum('bte,fe->btf', x, Wq) + bq) * scaling
        k = jnp.einsum('bte,fe->btf', x, Wk) + bk
        v = jnp.einsum('bte,fe->btf', x, Wv) + bv
        q = q.reshape(b, t, h, d)
        k = k.reshape(b, t, h, d)
        v = v.reshape(b, t, h, d)
        scores = jnp.einsum('bihd,bjhd->bhij', q, k)
        pos = jnp.arange(t)
        alibi = -jnp.abs(pos[None, :] - pos[:, None]).astype(scores.dtype)
        scores = scores + slopes[:, None, None] * alibi
        probs = jax.nn.softmax(scores.astype(jnp.float32), axis=-1).astype(scores.dtype)
        out = jnp.einsum('bhij,bjhd->bihd', probs, v).reshape(b, t, e)
        return jnp.einsum('bte,fe->btf', out, Wo) + bo

    def _L0_ffn_ref(x, router_w, expert_bias, gate_proj, up_proj, down_proj):
        import jax, jax.numpy as jnp
        import numpy as np
        TOP_K = 4
        NUM_EXPERTS = 16
        logits = jnp.einsum('bsh,eh->bse', x, router_w) + expert_bias
        scores = jax.nn.softmax(logits, axis=-1)
        top_w, top_idx = jax.lax.top_k(scores, TOP_K)
        top_w = top_w / jnp.sum(top_w, axis=-1, keepdims=True)
        g = jnp.einsum('bsh,khe->bske', x, gate_proj)
        u = jnp.einsum('bsh,khe->bske', x, up_proj)
        act = jax.nn.silu(g) * u
        out = jnp.einsum('bske,keh->bskh', act, down_proj)
        sel = jnp.take_along_axis(out, top_idx[..., None], axis=2)
        return jnp.sum(sel * top_w[..., None], axis=2)
    x = L0_attn_x
    mod = (_silu(L0_c) @ L0_wmod).reshape(L0_c.shape[0], 6, 1, -1)
    sa, ca, ga, sb, cb, gb = (mod[:, 0], mod[:, 1], mod[:, 2], mod[:, 3], mod[:, 4], mod[:, 5])
    ga = (2 * (ga >= 0) - 1) * jnp.maximum(jnp.abs(ga), 0.25)
    gb = (2 * (gb >= 0) - 1) * jnp.maximum(jnp.abs(gb), 0.25)
    h = _layernorm(x, axis=-1) * (1 + ca) + sa
    x = x + ga * _L0_attn_ref(h, L0_attn_Wq, L0_attn_bq, L0_attn_Wk, L0_attn_bk, L0_attn_Wv, L0_attn_bv, L0_attn_Wo, L0_attn_bo, L0_attn_slopes)
    h = _layernorm(x, axis=-1) * (1 + cb) + sb
    x = x + gb * _L0_ffn_ref(h, L0_ffn_router_w, L0_ffn_expert_bias, L0_ffn_gate_proj, L0_ffn_up_proj, L0_ffn_down_proj)
    return x

_drawn_inputs = setup_inputs


def setup_inputs(seed=0):
    import zlib

    import numpy as np

    out = dict(_drawn_inputs(seed))
    spreads = {'L0_attn_bq': (0.0, 0.8),
     'L0_attn_bk': (0.0, 0.8),
     'L0_attn_bv': (0.0, 0.8),
     'L0_attn_bo': (0.0, 0.331),
     'L0_ffn_expert_bias': (0.0, 0.8)}
    factors = {'L0_attn_Wq': 8.0,
     'L0_attn_Wk': 8.0,
     'L0_attn_Wv': 8.0,
     'L0_attn_Wo': 6.051,
     'L0_attn_slopes': 8.0,
     'L0_ffn_router_w': 8.0,
     'L0_ffn_gate_proj': 8.0,
     'L0_ffn_up_proj': 8.0,
     'L0_ffn_down_proj': 8.0}
    for name, (base, spread) in spreads.items():
        noise = np.random.default_rng([zlib.crc32(name.encode()), seed]).standard_normal(out[name].shape)
        drawn = base * np.exp(spread * noise) if base else spread * noise
        out[name] = jnp.asarray(drawn.astype(out[name].dtype))
    for name, factor in factors.items():
        out[name] = (out[name] * factor).astype(out[name].dtype)
    return out
```

```python
from contextlib import ExitStack

import numpy as np

import concourse.bass as bass
from concourse import mybir

F32 = mybir.dt.float32
BF16 = mybir.dt.bfloat16
U32 = mybir.dt.uint32
I32 = mybir.dt.int32
ALU = mybir.AluOpType
ACT = mybir.ActivationFunctionType
AX_X = mybir.AxisListType.X

P = 128
T = 1024
NT = T // P
E = 256
KE = E // P
H = 16
D = E // H
VW = D + 1
CH = 512
NCH = T // CH
TC = CH // P
LN_EPS = 1e-5
GATE_MIN = 0.25
HT = P // D

Q_PARTS = (0, 0, 1, 0, 1, 2)
K_PARTS = (0, 1, 0, 2, 1, 0)
R_QK = 6 * D
R_AL = 6 * TC
R_M = 3
R_ALL = R_QK + R_AL + R_M

W_DIST = T + (NT - 1) * P
DIST0 = (NT - 1) * P

SLOTS = 4
NX = 16
TOPK = 4
INTER = 224
IH = INTER // 2
NTAB = 48
MAX_TILES = (T * TOPK + NX * (P - 1)) // P


def host_constants():
    def bf16_bits(a):
        return (np.ascontiguousarray(a, np.float32).view(np.uint32) >> 16).astype(np.uint16)

    i = np.arange(P)[:, None]
    dist = -np.abs(i - (np.arange(W_DIST)[None, :] - DIST0)).astype(np.float32)
    c = (np.arange(P) % NT)[:, None]
    j = np.arange(T)[None, :]
    same = (j // P) == c
    alibi_key = np.where(same, 0, -np.abs(j - P * c)).astype(np.float32)
    alibi_sign = np.sign(np.arange(NT)[None, :] - c).astype(np.float32)
    t = np.arange(T)
    rows = [((t // P) % TC == k) * 1.0 for k in range(TC)]
    qrows = np.stack(rows * 3 + [r * (t % P) for r in rows] * 3)
    merge = np.zeros((P, NCH * VW), np.float32)
    for g in range(4):
        for d in range(VW):
            merge[32 * g + d, (g % NCH) * VW + d] = 1.0
    return {
        "ident": np.eye(P, dtype=np.float32),
        "dist": dist,
        "alibi_key": alibi_key,
        "alibi_sign": alibi_sign,
        "query_rows": bf16_bits(qrows),
        "one_rows": bf16_bits(np.ones((R_M, T))),
        "merge": merge,
        "triangle": bf16_bits(np.concatenate([np.triu(np.ones((P, P)), 1), np.ones((P, P))], 1)),
        "route": np.concatenate([np.broadcast_to(r, (P, r.shape[-1])) for r in (
            np.arange(NX), P * np.arange(NT), np.arange(NTAB), np.arange(P),
            1 + T * np.arange(TOPK)[None, None, :] + P * np.arange(NT)[None, :, None] + np.arange(P)[:, None, None])
            for r in [np.asarray(r).reshape(-1 if np.ndim(r) == 1 else P, *([] if np.ndim(r) == 1 else [-1]))]],
            1).astype(np.float32),
    }


def on_partitions(ap, n):
    return bass.AP(ap.tensor, ap.offset, [[0, n]] + [list(a) for a in ap.ap])


def adaln_block(nc, a, out):
    with ExitStack() as ctx:
        def sb(name, shape, dt=F32):
            return ctx.enter_context(nc.sbuf_tensor(name, shape, dt))

        def sem(name):
            return ctx.enter_context(nc.semaphore(name))

        def dram(name, shape, dt):
            return nc.dram_tensor(name, shape, dt, kind="Internal").ap()

        q_rows = dram("q_rows", [H, R_QK, T], BF16)
        k_rows = dram("k_rows", [H, R_QK, T], BF16)
        al_rows = dram("al_rows", [H, NCH, R_AL, T], BF16)
        m_rows = dram("m_rows", [H, R_M, NT, P], BF16)
        xn_rows = dram("xn_rows", [T, E], F32)
        z_rows = dram("z_rows", [TOPK * T, E], F32)

        w_gu = sb("w_gu", [P, NX, KE, 2 * INTER])
        w_dn = sb("w_dn", [P, NX, 2, E])
        flat_gu = w_gu[:].rearrange("p x k n -> p (x k n)")
        flat_dn = w_dn[:].rearrange("p x k n -> p (x k n)")

        def carver(flat):
            used = [0]

            def carve(shape, dt=F32):
                n = int(np.prod(shape[1:])) * (1 if dt in (F32, U32, I32) else 2) // (1 if dt in (F32, U32, I32) else 4)
                v = flat[0:shape[0], used[0]:used[0] + n]
                used[0] += n
                assert used[0] <= flat.shape[1]
                v = v if dt == F32 else v.bitcast(dt)
                names = "abcdef"[:len(shape) - 1]
                return v.rearrange(f"p ({' '.join(names)}) -> p {' '.join(names)}",
                                   **{c: m for c, m in zip(names[1:], shape[2:])}) if len(shape) > 2 else v
            return carve

        early = carver(flat_gu)
        qk_part = early([P, 2, KE, 3, T], BF16)
        wmod = early([P, KE, 6 * E])
        al_part = early([P, 6, T], BF16)
        xh = early([P, NT, E])
        early = carver(flat_dn)
        w_raw = early([P, 4, KE, E])
        wT = early([P, 4, KE, E])
        al_key = early([P, T])
        qk_f = early([P, CH])
        qk_r = early([P, CH])
        gsign = early([P, 2, E])
        rw_raw = early([NX, E])

        x_sb = sb("x_sb", [P, NT, E])
        hT = sb("hT", [P, KE, T])
        wo_sb = sb("wo_sb", [P, KE, E])
        cond = sb("cond", [P, KE])
        cond_silu = sb("cond_silu", [P, KE])
        cond_bc = sb("cond_bc", [P, KE, P])
        modc = sb("modc", [P, 6, KE])
        gates = sb("gates", [P, 2, E])
        qk_bias = sb("qk_bias", [P, 2, KE])
        q_bias_s = sb("q_bias_s", [P, KE])
        v_bias = sb("v_bias", [P, E])
        o_bias = sb("o_bias", [P, E])
        x_bias = sb("x_bias", [P, NX])
        rwT = sb("rwT", [P, KE, NX])
        slopes = sb("slopes", [P, H])
        slope_hc = sb("slope_hc", [P, 1])
        ident = sb("ident", [P, P])
        merge = sb("merge", [P, NCH * VW])
        triangle = sb("triangle", [P, 2, P], BF16)
        route = sb("route", [P, NX + NT + NTAB + P + NT * TOPK])
        dist = sb("dist", [P, W_DIST])
        stats = sb("stats", [P, NT, 6])
        mv = sb("mv", [P, NT, 2])
        std = sb("std", [P, NT])
        rstd = sb("rstd", [P, NT])
        al_sign = sb("al_sign", [P, NT])
        v_all = sb("v_all", [P, NT, E])
        q_st = sb("q_st", [P, SLOTS, T], BF16)
        k_st = sb("k_st", [P, NCH, SLOTS, T], BF16)
        v_st = sb("v_st", [P, 2, NT, 32])
        bias_t = sb("bias_t", [P, 2, W_DIST])
        bias_d = sb("bias_d", [P, SLOTS, P])
        slope_now = sb("slope_now", [P, 2, 1])
        junk = sb("junk", [P, 2, CH], BF16)
        mx = sb("mx", [P, 2, NT, NCH])
        negm = sb("negm", [P, 2, NT])
        m_f = sb("m_f", [NT, P])
        m_r = sb("m_r", [NT, P])
        m_part = sb("m_part", [NT, R_M, P], BF16)
        probs = sb("probs", [P, 4, T])
        o_sb = sb("o_sb", [P, CH])
        rsum = sb("rsum", [P, TC, NCH])
        attn = sb("attn", [P, NCH, TC, E])

        xn = v_all
        late = carver(bias_t[:].rearrange("p s n -> p (s n)"))
        attT = late([P, 2, KE, P])
        logits = late([P, NT, NX])
        top8 = late([P, NT, 8])
        top8_i = late([P, NT, 8], U32)
        top_i = late([P, NT, TOPK])
        top_w = late([P, NT, TOPK])
        top_e = late([P, NT, TOPK])
        top_s = late([P, NT])
        hot = late([P, NT, TOPK, NX])
        hot_a = late([P, NT, TOPK, NX])
        mask = late([P, NT, NX], BF16)
        before = late([P, NT, NX])
        over = late([P, NX, NT])
        n_tiles = late([P, NX])
        ends = late([P, NX])
        starts = late([P, NX])
        pos = late([P, NT, TOPK])
        pos_i = late([P, NT, TOPK], I32)
        lo_i = late([P, NT, TOPK], I32)
        hi_i = late([P, NT, TOPK], I32)
        lo_f = late([P, NT, TOPK])
        hi_f = late([P, NT, TOPK])
        hot_lo = late([P, 2, P])
        hot_hi = late([P, 2, NTAB])
        tab_f = late([P, NTAB])
        tab_e = late([P, NTAB])
        tab_i = late([P, NTAB, 2], I32)
        exp_f = late([1, NTAB])
        exp_i = late([1, NTAB], I32)
        late = carver(probs[:].rearrange("p s n -> p (s n)"))
        xg = late([P, 4, E])
        xT = late([P, 2, KE, P])
        silu = late([P, 2, INTER])
        hid = late([P, 2, INTER])
        hidT = late([P, 2, 2, P])
        y_sb = late([P, 4, E])
        idx = late([P, 4, 2], I32)
        idx_s = late([P, 4, 1], I32)
        ended = xg.rearrange("p s e -> p (s e)")[0:1, 0:NTAB * NX]
        z_sb = [k_st[:, s // 2].rearrange("p s n -> p (s n)").bitcast(F32)[:, (s % 2) * 1024:(s % 2) * 1024 + 1024]
                for s in range(4)] + [q_st[:].rearrange("p s n -> p (s n)").bitcast(F32)[:, s * 1024:s * 1024 + 1024]
                                      for s in range(2)]
        z_sb = [z.rearrange("p (j e) -> p j e", j=TOPK) for z in z_sb]

        ps = ctx.enter_context(nc.psum_tensor("ps", [P, 8, CH], F32))
        ps_max = [ps[:, 0, :], ps[:, 1, :]]
        ps_st = [ps[:, 2:4, :], ps[:, 4:6, :]]
        ps_o = ps[:, 6, :]
        ps_misc = ps[:, 7, :]
        ps_ot = ps_misc[:, 0:TC * NCH * VW].rearrange("p (t c d) -> p t c d", t=TC, c=NCH)

        x_in = [sem("x_in0"), sem("x_in1")]
        cond_in = sem("cond_in")
        wmod_in = sem("wmod_in")
        w_in = sem("w_in")
        ident_in = sem("ident_in")
        consts_in = sem("consts_in")
        dist_in = sem("dist_in")
        al_in = sem("al_in")
        rows_in = sem("rows_in")
        silu_done = sem("silu_done")
        bc_done = sem("bc_done")
        var_done = sem("var_done")
        std_done = sem("std_done")
        xh_done = sem("xh_done")
        pe_group = sem("pe_group")
        dve_evac = sem("dve_evac")
        act_evac = sem("act_evac")
        mod_done = sem("mod_done")
        dve_chain = sem("dve_chain")
        q_bias_done = sem("q_bias_done")
        qk_split = sem("qk_split")
        qk_stored = [sem("qk_stored0"), sem("qk_stored1")]
        al_done = sem("al_done")
        al_stored = sem("al_stored")
        v_done = sem("v_done")
        st_in = [sem(f"st_in{s}") for s in range(SLOTS)]
        v_init = sem("v_init")
        slope_cp = sem("slope_cp")
        bias_done = sem("bias_done")
        v_staged = sem("v_staged")
        max_ready = sem("max_ready")
        max_used = sem("max_used")
        negm_done = sem("negm_done")
        mT_ready = sem("mT_ready")
        m_chain = sem("m_chain")
        m_stored = sem("m_stored")
        m_in = sem("m_in")
        st_ready = sem("st_ready")
        exp_done = sem("exp_done")
        pv_done = sem("pv_done")
        o_evac = sem("o_evac")
        ot_ready = sem("ot_ready")
        ot_recip = sem("ot_recip")
        ot_used = sem("ot_used")
        settled = sem("settled")
        fin = sem("fin")
        late_in = sem("late_in")
        wo_done = sem("wo_done")
        xg_done = sem("xg_done")
        w_stage = sem("w_stage")
        w_done = sem("w_done")
        attT_ready = sem("attT_ready")
        attT_evac = sem("attT_evac")
        y1_ready = sem("y1_ready")
        x2_done = sem("x2_done")
        var2_done = sem("var2_done")
        std2_done = sem("std2_done")
        xn_done = sem("xn_done")
        xn_stored = sem("xn_stored")
        xnT_ready = sem("xnT_ready")
        xnT_evac = sem("xnT_evac")
        logits_ready = sem("logits_ready")
        top_shift = sem("top_shift")
        top_exp = sem("top_exp")
        mask_done = sem("mask_done")
        before_ready = sem("before_ready")
        hot_done = sem("hot_done")
        hot_used = sem("hot_used")
        tab_done = sem("tab_done")
        idx_cp = sem("idx_cp")
        idx_s_cp = sem("idx_s_cp")
        gathered = [sem(f"gathered{s}") for s in range(4)]
        xgT_ready = sem("xgT_ready")
        xT_act = sem("xT_act")
        xT_dve = sem("xT_dve")
        gu_ready = sem("gu_ready")
        silu2_done = sem("silu2_done")
        hid_done = sem("hid_done")
        hidT_ready = sem("hidT_ready")
        hidT_evac = sem("hidT_evac")
        y_ready = sem("y_ready")
        y_evac = sem("y_evac")
        scattered = [sem(f"scattered{s}") for s in range(4)]
        z_in = [sem(f"z_in{s}") for s in range(6)]
        z_used = sem("z_used")
        acc_done = sem("acc_done")
        out_stored = sem("out_stored")

        block = ctx.enter_context(nc.Block())

        WT0, MODC, GATE, XT0, Q0, K0, V0, Q1, K1 = 0, 4, 5, 6, 10, 12, 14, 18, 20
        N_GROUPS = 22
        emptied_by = ["dve"] * 6 + ["act"] * 4 + ["act"] * 4 + ["dve"] * 4 + ["act"] * 4

        def count(group, engine):
            return sum(e == engine for e in emptied_by[:group + 1])

        def wait_emptied(eng, group):
            s = dve_evac if emptied_by[group] == "dve" else act_evac
            eng.wait_ge(s, count(group, emptied_by[group]))

        def settle(eng):
            eng.sem_inc(settled, 1)

        def at(i, c, per=SLOTS, k=1):
            return k * (4 * i + c)

        def is0(i):
            return isinstance(i, int) and i == 0

        def steps(eng, step):
            for c in (-2, -1, 0):
                step(0, c)
            with eng.Fori(0, 3) as i:
                for c in range(1, 1 + SLOTS):
                    step(i, c)
            for c in (1, 2, 3):
                step(3, c)

        def tiles(eng, tile, first, last):
            for k in range(first, 8):
                tile(0, k)
            with eng.Fori(2, MAX_TILES // 4) as i:
                for c in range(4):
                    tile(i, c)
            for k in range(MAX_TILES // 4 * 4, last):
                tile(MAX_TILES // 4, k - MAX_TILES // 4 * 4)

        def kind(i, c):
            if isinstance(i, int):
                h = 4 * i + c
                return h + 2 < H, 0 <= h + 1 < H, h >= 0, h >= 1
            return True, True, True, True

        @block.sync
        def _(sp):
            for k in range(2):
                sp.dma_start(x_sb[:, 4 * k:4 * k + 4, :],
                             a["x"].rearrange("(t p) e -> p t e", p=P)[:, 4 * k:4 * k + 4, :]).then_inc(x_in[k], 16)
            sp.dma_start(ident[:], a["ident"]).then_inc(ident_in, 16)
            for n, w in enumerate(("Wq", "Wk", "Wv", "Wo")):
                sp.dma_start(w_raw[:, n], a[w].rearrange("(k p) e -> p k e", p=P)).then_inc(w_in, 16)
            sp.dma_start(al_key[:], a["alibi_key"]).then_inc(al_in, 16)
            sp.dma_start(al_sign[:], a["alibi_sign"]).then_inc(al_in, 16)
            sp.dma_start(slope_hc[:], bass.AP(a["slopes"].tensor, a["slopes"].offset, [[1, H], [0, NT], [1, 1]])).then_inc(al_in, 16)
            sp.dma_start(rw_raw, a["router_w"]).then_inc(late_in, 16)
            sp.dma_start(dist[:], a["dist"]).then_inc(dist_in, 16)
            sp.dma_start(slopes[:], on_partitions(a["slopes"], P)).then_inc(dist_in, 16)
            for s in range(SLOTS):
                sp.dma_start(q_st[R_QK:R_QK + R_AL, s, :], a["query_rows"].bitcast(BF16)).then_inc(rows_in, 16)
                for ch in range(NCH):
                    sp.dma_start(k_st[R_QK + R_AL:R_ALL, ch, s, :], a["one_rows"].bitcast(BF16)).then_inc(rows_in, 16)

            sp.wait_ge(al_done, 1)
            for g in range(6):
                sp.dma_start(al_rows[:, :, TC * g:TC * g + TC, :], al_part[:, g, :]).then_inc(al_stored, 16)

            def store_qk(f):
                for w, (rows, parts) in enumerate(((q_rows, Q_PARTS), (k_rows, K_PARTS))):
                    sp.wait_ge(qk_split, 4 * f + 2 * w + 2)
                    for g, part in enumerate(parts):
                        sp.dma_start(rows[HT * f:HT * f + HT, D * g:D * g + D, :],
                                     qk_part[:, w, f, part, :]).then_inc(qk_stored[f], 16)

            def load_head(i, c):
                s, h = c % SLOTS, at(i, c)
                sp.dma_start(q_st[0:R_QK, s, :], q_rows[h]).then_inc(st_in[s], 16)
                for ch in range(NCH):
                    sp.dma_start(k_st[0:R_QK, ch, s, :], k_rows[h]).then_inc(st_in[s], 16)
                    sp.dma_start(k_st[R_QK:R_QK + R_AL, ch, s, :], al_rows[h, ch]).then_inc(st_in[s], 16)

            store_qk(0)
            sp.wait_ge(qk_stored[0], 16 * 12)
            sp.wait_ge(al_stored, 16 * 6)
            load_head(0, 0)
            load_head(0, 1)

            def step(i, c):
                _, rows, _, _ = kind(i, c)
                if not isinstance(i, int) or 2 <= 4 * i + c + 3 < H:
                    if not isinstance(i, int) or 4 * i + c >= 1:
                        sp.wait_ge(st_ready, at(i, c, k=NT))
                    load_head(i, c + 3)
                if rows:
                    g = c + 1
                    sp.wait_ge(m_chain, at(i, g, k=5) + 5)
                    sp.dma_start(m_rows[at(i, g)].rearrange("r i x -> i r x"), m_part[:]).then_inc(m_stored, 16)
                    sp.wait_ge(m_stored, at(i, g, k=16) + 16)
                    sp.dma_start(q_st[R_QK + R_AL:R_ALL, g % SLOTS, :],
                                 m_rows[at(i, g)].rearrange("r i x -> r (i x)")).then_inc(m_in, 16)
                if is0(i) and c == -1:
                    store_qk(1)
                    sp.wait_ge(qk_stored[1], 16 * 12)

            steps(sp, step)

            for hf in range(NCH):
                sp.wait_ge(xn_done, TC * hf + TC)
                sp.dma_start(xn_rows.rearrange("(t p) e -> p t e", p=P)[:, TC * hf:TC * hf + TC, :],
                             xn[:, TC * hf:TC * hf + TC, :]).then_inc(xn_stored, 16)
            for s in range(4):
                sp.wait_ge(scattered[s], 16 * len(range(s, MAX_TILES, 4)))
            for t in range(NT):
                s = t % 6
                if t >= 6:
                    sp.wait_ge(acc_done, t - 6 + 1)
                sp.dma_start(z_sb[s], z_rows.rearrange("(j t p) e -> p t j e", p=P, j=TOPK)[:, t]).then_inc(z_in[s], 16)
            for t in range(NT):
                sp.wait_ge(acc_done, t + 1)
                sp.dma_start(out[P * t:P * t + P, :], x_sb[:, t, :]).then_inc(out_stored, 16)
            sp.wait_ge(out_stored, 16 * NT)

        @block.scalar
        def _(act):
            act.dma_start(cond[:], a["c"].rearrange("o (k p) -> p (o k)", p=P), allow_slow_non_contiguous=True).then_inc(cond_in, 16)
            act.dma_start(wmod[:], a["wmod"].rearrange("(k p) m -> p k m", p=P)).then_inc(wmod_in, 16)
            for n, b in enumerate(("bq", "bk")):
                act.dma_start(qk_bias[:, n, :], a[b].rearrange("(k p) -> p k", p=P), allow_slow_non_contiguous=True).then_inc(consts_in, 16)
            act.dma_start(v_bias[:], on_partitions(a["bv"], P)).then_inc(consts_in, 16)
            act.dma_start(o_bias[:], on_partitions(a["bo"], P)).then_inc(consts_in, 16)
            act.dma_start(merge[:], a["merge"]).then_inc(consts_in, 16)
            act.dma_start(x_bias[:], on_partitions(a["expert_bias"], P)).then_inc(late_in, 16)
            act.dma_start(triangle[:].rearrange("p a b -> p (a b)"), a["triangle"].bitcast(BF16)).then_inc(late_in, 16)
            act.dma_start(route[:], a["route"]).then_inc(late_in, 16)
            act.wait_ge(cond_in, 16)
            act.activation(cond_silu[:], cond[:], ACT.Silu).then_inc(silu_done, 1)
            act.wait_ge(var_done, 1)
            act.activation(std[:], std[:], ACT.Sqrt).then_inc(std_done, 1)
            act.wait_ge(mod_done, 1)
            for g in range(4):
                ch, k = g // KE, g % KE
                act.wait_ge(pe_group, XT0 + g + 1)
                act.activation(hT[:, k, CH * ch:CH * ch + CH], ps[:, (XT0 + g) % 8, :], ACT.Identity,
                               bias=modc[:, 0, k:k + 1], scale=modc[:, 1, k:k + 1]).then_inc(act_evac, 1)
            act.wait_ge(consts_in, 16 * 5)
            act.wait_ge(q_bias_done, 1)
            n = 0
            for g0, w, f in ((Q0, 0, 0), (K0, 1, 0), (Q1, 0, 1), (K1, 1, 1)):
                for ch in range(NCH):
                    g = g0 + ch
                    act.wait_ge(pe_group, g + 1)
                    if n:
                        act.wait_ge(qk_split, n)
                    bias = q_bias_s[:, f:f + 1] if w == 0 else qk_bias[:, 1, f:f + 1]
                    act.activation(qk_f[:], ps[:, g % 8, :], ACT.Identity, bias=bias,
                                   scale=D ** -0.5 if w == 0 else 1.0).then_inc(act_evac, 1)
                    n += 1

            def step(i, c):
                _, _, probabilities, output = kind(i, c)
                for j in range(NT):
                    if probabilities:
                        first = is0(i) and c == 0
                        act.wait_ge(st_ready, at(i, c, k=NT) + j + 1)
                        if not first or j >= 4:
                            act.wait_ge(pv_done, at(i, c, k=4) + (j - 4) // 2 + 1)
                        act.activation(probs[:, j % 4, :], ps_st[j % 2].rearrange("p b n -> p (b n)"),
                                       ACT.Exp).then_inc(exp_done, 1)
                    if output and j == 2:
                        evac_o(i, c - 1)

            def evac_o(i, c):
                act.wait_ge(pv_done, at(i, c, k=4) + 4)
                if not (is0(i) and c == 0):
                    act.wait_ge(ot_ready, at(i, c) + 1)
                act.copy(o_sb[:], ps_o).then_inc(o_evac, 1)

            steps(act, step)
            evac_o(3, 3)

            for t in range(NT):
                act.wait_ge(attT_ready, t + 1)
                if t >= 2:
                    act.wait_ge(y1_ready, t - 1)
                act.copy(attT[:, t % 2], ps[:, t % 2, 0:E].rearrange("p (k n) -> p k n", k=KE)).then_inc(attT_evac, 1)
                if t % TC == TC - 1:
                    hf = t // TC
                    act.wait_ge(var2_done, hf + 1)
                    act.activation(std[:, TC * hf:TC * hf + TC], std[:, TC * hf:TC * hf + TC], ACT.Sqrt).then_inc(std2_done, 1)
            for g in range(4):
                hf, k = g // KE, g % KE
                act.wait_ge(xnT_ready, g + 1)
                act.activation(hT[:, k, CH * hf:CH * hf + CH], ps[:, 4 + g, :], ACT.Identity,
                               bias=modc[:, 3, k:k + 1], scale=modc[:, 4, k:k + 1]).then_inc(xnT_evac, 1)
            act.wait_ge(top_shift, 1)
            act.activation(top_e, top_w, ACT.Exp).then_inc(top_exp, 1)

            def tile(i, c):
                k = 4 * i + c if isinstance(i, int) else None
                if k is None or 0 <= k < MAX_TILES:
                    act.wait_ge(gu_ready, at(i, c) + 1)
                    if k is None or k >= 2:
                        act.wait_ge(hid_done, at(i, c) - 1)
                    act.activation(silu[:, c % 2, :], ps[:, 2 + c % 2, 0:INTER], ACT.Silu).then_inc(silu2_done, 1)
                if k is None or 0 <= k - 1 < MAX_TILES:
                    act.wait_ge(hidT_ready, at(i, c - 1) + 1)
                    if k is None or k - 1 >= 2:
                        act.wait_ge(y_ready, at(i, c - 1) - 1)
                    act.copy(hidT[0:IH, (c - 1) % 2], ps[0:IH, 4 + (c - 1) % 2, 0:2 * P].rearrange("p (a n) -> p a n", a=2)).then_inc(hidT_evac, 1)
                if k is None or k + 1 < MAX_TILES:
                    act.wait_ge(xgT_ready, at(i, c + 1) + 1)
                    if k is None or k + 1 >= 2:
                        act.wait_ge(gu_ready, at(i, c + 1) - 1)
                    act.activation(xT[:, (c + 1) % 2, 0, :], ps[:, 0, 0:P], ACT.Identity,
                                   bias=modc[:, 3, 0:1], scale=modc[:, 4, 0:1]).then_inc(xT_act, 1)

            tiles(act, tile, -1, MAX_TILES + 1)

        @block.gpsimd
        def _(pool):
            pool.memset(v_st[:], 0.0).then_inc(v_init, 1)
            pool.wait_ge(v_init, 1)
            pool.memset(v_st[:, :, :, D:D + 1], 1.0).then_inc(v_init, 1)

            def make_bias(i, c):
                s = c % 2
                first = isinstance(i, int) and 4 * i + c < 2
                if not first:
                    pool.wait_ge(bias_done, at(i, c, k=2) - 2)
                pool.tensor_copy(slope_now[:, s, :], slopes[:, bass.ds(at(i, c), 1)]).then_inc(slope_cp, 1)
                pool.wait_ge(slope_cp, at(i, c) + 1)
                if not first:
                    pool.wait_ge(max_used, at(i, c - 1, k=16))
                settle(pool)
                pool.tensor_scalar(bias_t[:, s, :], dist[:], slope_now[:, s, :], None, ALU.mult).then_inc(bias_done, 1)
                if not isinstance(i, int) or 4 * i + c >= SLOTS:
                    pool.wait_ge(st_ready, at(i, c - 3, k=NT))
                settle(pool)
                pool.tensor_scalar(bias_d[:, c % SLOTS, :], dist[:, DIST0:DIST0 + P], slope_now[:, s, :], None,
                                   ALU.mult).then_inc(bias_done, 1)

            def stage_v(i, c):
                if not isinstance(i, int) or 4 * i + c >= 2:
                    pool.wait_ge(pv_done, at(i, c - 1, k=4))
                pool.tensor_copy(v_st[:, c % 2, :, 0:D], v_all[:, :, bass.ds(at(i, c, k=D), D)]).then_inc(v_staged, 1)

            pool.wait_ge(dist_in, 32)
            make_bias(0, 0)
            def load_expert(i, c):
                n = at(i, c)
                for half, name in enumerate(("gate_proj", "up_proj")):
                    pool.dma_start(w_gu[:, bass.ds(n, 1), :, INTER * half:INTER * half + INTER],
                                   a[name][bass.ds(n, 1)].rearrange("x (k p) n -> p x k n", p=P)).then_inc(w_done, 16)
                pool.dma_start(w_dn[0:IH, bass.ds(n, 1), :, :],
                               a["down_proj"][bass.ds(n, 1)].rearrange("x (k p) n -> p x k n", p=IH)).then_inc(w_done, 16)

            def step(i, c):
                static = isinstance(i, int)
                h = 4 * i + c if static else None
                if static and h == 0:
                    for f in range(KE):
                        pool.wait_ge(qk_stored[f], 16 * 12)
                    pool.wait_ge(al_stored, 16 * 6)
                    pool.wait_ge(wo_done, 2)
                    pool.wait_ge(pe_group, N_GROUPS)
                if not static or h >= 0:
                    load_expert(i, c)
                if not static or h + 3 < H:
                    make_bias(i, c + 3)
                if is0(i) and c == -1:
                    pool.wait_ge(v_init, 2)
                    pool.wait_ge(v_done, 4)
                if not static or 0 <= h + 1 < H:
                    stage_v(i, c + 1)

            steps(pool, step)

            pool.wait_ge(tab_done, 1)
            pool.wait_ge(xn_stored, 32)

            def tile(i, c):
                k = 4 * i + c if isinstance(i, int) else None
                if k is None or 0 <= k + 3 < MAX_TILES:
                    s = (c + 3) % 4
                    if k is None or k + 3 >= 4:
                        pool.wait_ge(xgT_ready, at(i, c + 3) - 3)
                        pool.wait_ge(idx_cp, at(i, c + 3))
                    settle(pool)
                    pool.tensor_copy(idx[:, s, :].unsqueeze(1), tab_i[:, bass.ds(at(i, c + 3), 1), :]).then_inc(idx_cp, 1)
                    pool.wait_ge(idx_cp, at(i, c + 3) + 1)
                    settle(pool)
                    pool.indirect_dma_start(xg[:, s, :], None, xn_rows,
                                            bass.IndirectOffsetOnAxis(ap=idx[:, s, 0:1].bitcast(U32), axis=0),
                                            bounds_check=T - 1, oob_is_err=False).then_inc(gathered[s], 16)
                if k is None or 0 <= k - 3 < MAX_TILES:
                    s = (c - 3) % 4
                    pool.wait_ge(y_evac, at(i, c - 3) + 1)
                    settle(pool)
                    pool.tensor_copy(idx_s[:, s, :].unsqueeze(1), tab_i[:, bass.ds(at(i, c - 3), 1), 1:2]).then_inc(idx_s_cp, 1)
                    pool.wait_ge(idx_s_cp, at(i, c - 3) + 1)
                    settle(pool)
                    pool.indirect_dma_start(z_rows, bass.IndirectOffsetOnAxis(ap=idx_s[:, s, :].bitcast(U32), axis=0),
                                            y_sb[:, s, :], None, bounds_check=TOPK * T - 1,
                                            oob_is_err=False).then_inc(scattered[s], 16)

            tiles(pool, tile, -3, MAX_TILES + 3)

        @block.vector
        def _(dve):
            chain = [0]
            dve.sem_inc(ot_used, 1)

            def link(ins):
                chain[0] += 1
                ins.then_inc(dve_chain, 1)
                dve.wait_ge(dve_chain, chain[0])

            for t in range(NT):
                if t % 4 == 0:
                    dve.wait_ge(x_in[t // 4], 16)
                last = dve.bn_stats(stats[:, t, :], x_sb[:, t, :])
            link(last)
            for t in range(NT):
                last = dve.bn_aggr(mv[:, t, :], stats[:, t, :])
            link(last)
            dve.tensor_scalar(std[:], mv[:, :, 1], LN_EPS, None, ALU.add).then_inc(var_done, 1)
            dve.wait_ge(silu_done, 1)
            dve.tensor_copy(cond_bc[:], cond_silu[:].unsqueeze(2).broadcast_to([P, KE, P])).then_inc(bc_done, 1)
            dve.wait_ge(std_done, 1)
            link(dve.reciprocal(rstd[:], std[:]))
            for t in range(NT):
                dve.tensor_scalar(xh[:, t, :], x_sb[:, t, :], mv[:, t, 0:1], rstd[:, t:t + 1],
                                  ALU.subtract, ALU.mult).then_inc(xh_done, 1)
            for w in range(4):
                dve.wait_ge(pe_group, WT0 + w + 1)
                dve.tensor_copy(wT[:, w].rearrange("p k f -> p (k f)"), ps[:, WT0 + w, :]).then_inc(dve_evac, 1)
            dve.wait_ge(pe_group, MODC + 1)
            dve.tensor_copy(modc[:].rearrange("p m k -> p (m k)"), ps[:, MODC, 0:6 * KE]).then_inc(dve_evac, 1)
            dve.wait_ge(dve_evac, MODC + 1)
            dve.tensor_copy(rwT[:].rearrange("p k n -> p (k n)"), ps[:, MODC, 32:32 + KE * NX]).then_inc(wo_done, 1)
            for m in (1, 4):
                last = dve.tensor_scalar(modc[:, m, :], modc[:, m, :], 1.0, None, ALU.add)
            last.then_inc(mod_done, 1)
            dve.wait_ge(pe_group, GATE + 1)
            link(dve.tensor_copy(gates[:].rearrange("p g e -> p (g e)"), ps[:, GATE, :]))
            link(dve.tensor_scalar(gsign[:], gates[:], 0.0, 2.0, ALU.is_ge, ALU.mult))
            dve.wait_ge(dve_chain, chain[0])
            dve.tensor_scalar(gsign[:], gsign[:], -1.0, None, ALU.add).then_inc(dve_evac, 1)
            dve.wait_ge(dve_evac, GATE + 1)
            link(dve.scalar_tensor_tensor(out=gates[:], in0=gates[:], scalar=-1.0, in1=gates[:],
                                          op0=ALU.mult, op1=ALU.max))
            link(dve.scalar_tensor_tensor(out=gates[:], in0=gates[:], scalar=GATE_MIN, in1=gsign[:],
                                          op0=ALU.max, op1=ALU.mult))
            dve.wait_ge(consts_in, 16 * 5)
            dve.tensor_tensor(wo_sb[:], wT[:, 3], gates[:, 0:1, :].broadcast_to([P, KE, E]), ALU.mult).then_inc(wo_done, 1)
            link(dve.tensor_tensor(o_bias[:], o_bias[:], gates[:, 0, :], ALU.mult))
            dve.tensor_scalar(q_bias_s[:], qk_bias[:, 0, :], D ** -0.5, None, ALU.mult).then_inc(q_bias_done, 1)

            def split(parts, full, rest):
                link(dve.tensor_copy(parts[0], full))
                link(dve.tensor_tensor(rest, full, parts[0], ALU.subtract))
                link(dve.tensor_copy(parts[1], rest))
                return dve.tensor_tensor(parts[2], rest, parts[1], ALU.subtract)

            dve.wait_ge(al_in, 16 * 3)
            link(dve.tensor_scalar(al_key[:], al_key[:], slope_hc[:, 0:1], None, ALU.mult))
            spare = attn[:].rearrange("p c t e -> p (c t e)")[:, 0:T]
            link(split([al_part[:, g, :] for g in range(3)], al_key[:], spare))
            link(dve.tensor_scalar(al_sign[:], al_sign[:], slope_hc[:, 0:1], None, ALU.mult))
            link(dve.tensor_copy(al_key[:].rearrange("p (j n) -> p j n", n=P),
                                 al_sign[:].unsqueeze(2).broadcast_to([P, NT, P])))
            split([al_part[:, 3 + g, :] for g in range(3)], al_key[:], spare).then_inc(al_done, 1)

            def split_qk(n, w, f, ch):
                dve.wait_ge(act_evac, 4 + n + 1)
                part = [qk_part[:, w, f, g, CH * ch:CH * ch + CH] for g in range(3)]
                split(part, qk_f[:], qk_r[:]).then_inc(qk_split, 1)
                dve.wait_ge(qk_split, n + 1)

            for n in range(4):
                split_qk(n, n // 2, 0, n % 2)
            for g in range(4):
                dve.wait_ge(pe_group, V0 + g + 1)
                dve.tensor_tensor(v_all[:, 2 * g:2 * g + 2, :],
                                  ps[:, (V0 + g) % 8, :].rearrange("p (t e) -> p t e", t=2),
                                  v_bias[:].unsqueeze(1).broadcast_to([P, 2, E]), ALU.add).then_inc(dve_evac, 1)
            dve.wait_ge(dve_evac, count(N_GROUPS - 1, "dve"))
            dve.tensor_copy(rsum[0:1, 0, 0:1], v_all[0:1, 0, 0:1]).then_inc(v_done, 4)
            for n in range(4, 8):
                split_qk(n, (n - 4) // 2, 1, n % 2)
            dve.tensor_tensor(x_sb[:], x_sb[:], o_bias[:].unsqueeze(1).broadcast_to([P, NT, E]), ALU.add).then_inc(xg_done, 1)

            def step(i, c):
                maxima, rows, _, output = kind(i, c)
                g = c + 2
                for q in range(NT):
                    if maxima:
                        if q == 0:
                            dve.wait_ge(bias_done, at(i, g, k=2) + 1)
                        for half in range(NCH):
                            n = 2 * q + half
                            dve.wait_ge(max_ready, at(i, g, k=16) + n + 1)
                            if n >= 2 or not (is0(i) and g == 0):
                                dve.wait_ge(max_used, at(i, g, k=16) + n - 1)
                            if n == 0 and not (is0(i) and g < 2):
                                dve.wait_ge(negm_done, at(i, g) - 1)
                            settle(dve)
                            off = DIST0 + CH * half - P * q
                            dve.tensor_tensor_reduce(
                                junk[:, half, :], ps_max[half], bias_t[:, g % 2, off:off + CH], 1.0, -3.0e38,
                                ALU.add, ALU.max, mx[:, g % 2, q, half:half + 1]).then_inc(max_used, 1)
                    if rows and q == 2:
                        split_rows(i, c + 1)
                    if output and q == 6:
                        normalise(i, c - 1)
                if maxima:
                    dve.wait_ge(max_used, at(i, g, k=16) + 16)
                    if not (is0(i) and g < 2):
                        dve.wait_ge(mT_ready, at(i, g) - 1)
                    dve.tensor_reduce(negm[:, g % 2, :], mx[:, g % 2], AX_X, ALU.max, negate=True).then_inc(negm_done, 1)

            def split_rows(i, g):
                n = at(i, g, k=5)
                dve.wait_ge(mT_ready, at(i, g) + 1)
                if not (is0(i) and g == 0):
                    dve.wait_ge(m_stored, at(i, g, k=16))
                dve.tensor_copy(m_f[:], ps_misc[0:NT, 256:256 + P]).then_inc(m_chain, 1)
                dve.wait_ge(m_chain, n + 1)
                dve.tensor_copy(m_part[:, 0, :], m_f[:]).then_inc(m_chain, 1)
                dve.wait_ge(m_chain, n + 2)
                dve.tensor_tensor(m_r[:], m_f[:], m_part[:, 0, :], ALU.subtract).then_inc(m_chain, 1)
                dve.wait_ge(m_chain, n + 3)
                dve.tensor_copy(m_part[:, 1, :], m_r[:]).then_inc(m_chain, 1)
                dve.wait_ge(m_chain, n + 4)
                dve.tensor_tensor(m_part[:, 2, :], m_r[:], m_part[:, 1, :], ALU.subtract).then_inc(m_chain, 1)

            def normalise(i, c):
                dve.wait_ge(ot_ready, at(i, c) + 2)
                if not (is0(i) and c == 0):
                    dve.wait_ge(ot_used, at(i, c) + 1)
                dve.reciprocal(rsum[:], ps_ot[:, :, :, D]).then_inc(ot_recip, 1)
                dve.wait_ge(ot_recip, at(i, c) + 1)
                dve.tensor_tensor(attn[:, :, :, bass.ds(at(i, c, k=D), D)].rearrange("p c t d -> p t c d"),
                                  ps_ot[:, :, :, 0:D], rsum[:].unsqueeze(3).broadcast_to([P, TC, NCH, D]),
                                  ALU.mult).then_inc(ot_used, 1)

            steps(dve, step)
            normalise(3, 3)

            for t in range(NT):
                hf = t // TC
                dve.wait_ge(y1_ready, t + 1)
                dve.wait_ge(xg_done, 1)
                dve.tensor_tensor(x_sb[:, t, :], ps[:, 2 + t % 2, 0:E], x_sb[:, t, :], ALU.add).then_inc(x2_done, 1)
                dve.wait_ge(x2_done, t + 1)
                last = dve.bn_stats(stats[:, t, :], x_sb[:, t, :])
                if t % TC == TC - 1:
                    link(last)
                    for n in range(TC * hf, TC * hf + TC):
                        last = dve.bn_aggr(mv[:, n, :], stats[:, n, :])
                    link(last)
                    dve.tensor_scalar(std[:, TC * hf:TC * hf + TC], mv[:, TC * hf:TC * hf + TC, 1], LN_EPS, None,
                                      ALU.add).then_inc(var2_done, 1)
                    dve.wait_ge(std2_done, hf + 1)
                    link(dve.reciprocal(rstd[:, TC * hf:TC * hf + TC], std[:, TC * hf:TC * hf + TC]))
                    for n in range(TC * hf, TC * hf + TC):
                        dve.tensor_scalar(xn[:, n, :], x_sb[:, n, :], mv[:, n, 0:1], rstd[:, n:n + 1],
                                          ALU.subtract, ALU.mult).then_inc(xn_done, 1)
            dve.wait_ge(late_in, 16 * 4)
            for hf in range(NCH):
                dve.wait_ge(logits_ready, hf + 1)
                link(dve.tensor_tensor(logits[:, TC * hf:TC * hf + TC, :],
                                       ps[:, hf, 0:TC * NX].rearrange("p (t x) -> p t x", t=TC),
                                       x_bias[:].unsqueeze(1).broadcast_to([P, TC, NX]), ALU.add))
                for t in range(TC * hf, TC * hf + TC):
                    last = dve.max(top8[:, t, :], logits[:, t, :])
                link(last)
                for t in range(TC * hf, TC * hf + TC):
                    last = dve.max_index(top8_i[:, t, :], top8[:, t, :], logits[:, t, :])
            link(last)
            col = [0]

            def consts(n):
                col[0] += n
                return route[:, col[0] - n:col[0]]
            c_experts, c_sizes, c_tiles, c_slots, c_rows = (consts(n) for n in (NX, NT, NTAB, P, NT * TOPK))
            link(dve.tensor_copy(top_i, top8_i[:, :, 0:TOPK]))
            link(dve.tensor_tensor(hot, top_i.unsqueeze(3).broadcast_to([P, NT, TOPK, NX]),
                                   c_experts.unsqueeze(1).unsqueeze(1).broadcast_to([P, NT, TOPK, NX]), ALU.is_equal))
            link(dve.tensor_reduce(before, hot.rearrange("p t j x -> p t x j"), AX_X, ALU.add))
            dve.tensor_copy(mask, before).then_inc(mask_done, 1)
            dve.tensor_tensor(top_w, top8[:, :, 0:TOPK], top8[:, :, 0:1].broadcast_to([P, NT, TOPK]),
                              ALU.subtract).then_inc(top_shift, 1)
            dve.wait_ge(top_exp, 1)
            link(dve.tensor_reduce(top_s, top_e, AX_X, ALU.add))
            link(dve.reciprocal(top_s, top_s))
            dve.tensor_tensor(top_w, top_e, top_s.unsqueeze(2).broadcast_to([P, NT, TOPK]), ALU.mult)
            dve.wait_ge(before_ready, 1)
            counts = ps[:, 3, 0:NX]
            link(dve.tensor_tensor(over, counts.unsqueeze(2).broadcast_to([P, NX, NT]),
                                   c_sizes.unsqueeze(1).broadcast_to([P, NX, NT]), ALU.is_gt))
            link(dve.tensor_reduce(n_tiles, over, AX_X, ALU.add))
            dve.memset(starts, 1.0)
            link(dve.tensor_copy(before, ps[:, 2, 0:P].rearrange("p (t x) -> p t x", t=NT)))
            link(dve.tensor_tensor_scan(ends, starts, n_tiles, 0.0, ALU.mult, ALU.add))
            link(dve.tensor_tensor(starts, ends, n_tiles, ALU.subtract))
            link(dve.tensor_scalar(starts, starts, float(P), None, ALU.mult))
            link(dve.tensor_tensor(before, before, starts.unsqueeze(1).broadcast_to([P, NT, NX]), ALU.add))
            link(dve.tensor_tensor(hot_a, hot, before.unsqueeze(2).broadcast_to([P, NT, TOPK, NX]), ALU.mult))
            link(dve.tensor_reduce(pos, hot_a, AX_X, ALU.add))
            link(dve.tensor_copy(pos_i, pos))
            dve.tensor_scalar(hi_i, pos_i, 7, None, ALU.logical_shift_right)
            link(dve.tensor_scalar(lo_i, pos_i, P - 1, None, ALU.bitwise_and))
            dve.tensor_copy(hi_f, hi_i)
            link(dve.tensor_copy(lo_f, lo_i))
            for n in range(NT * TOPK):
                t, j = n // TOPK, n % TOPK
                if n >= 2:
                    dve.wait_ge(hot_used, n - 1)
                dve.tensor_scalar(hot_lo[:, n % 2, :], c_slots, lo_f[:, t, j:j + 1], None, ALU.is_equal).then_inc(hot_done, 1)
                dve.tensor_scalar(hot_hi[:, n % 2, :], c_tiles, hi_f[:, t, j:j + 1], c_rows[:, n:n + 1],
                                  ALU.is_equal, ALU.mult).then_inc(hot_done, 1)
            link(dve.tensor_tensor(ended.rearrange("p (k x) -> p k x", k=NTAB), ends[0:1].unsqueeze(1).broadcast_to([1, NTAB, NX]),
                                   c_tiles[0:1].unsqueeze(2).broadcast_to([1, NTAB, NX]), ALU.is_le))
            link(dve.tensor_reduce(exp_f, ended.rearrange("p (k x) -> p k x", k=NTAB), AX_X, ALU.add))
            link(dve.tensor_scalar(exp_f, exp_f, float(NX - 1), None, ALU.min))
            link(dve.tensor_copy(exp_i, exp_f))
            dve.wait_ge(hot_used, NT * TOPK)
            link(dve.tensor_copy(tab_f, ps[:, 4, 0:NTAB]))
            link(dve.tensor_scalar(tab_e, tab_f, 0.0, 2.0 * TOPK * T, ALU.is_equal, ALU.mult))
            link(dve.scalar_tensor_tensor(out=tab_f, in0=tab_f, scalar=-1.0, in1=tab_e, op0=ALU.add, op1=ALU.add))
            link(dve.tensor_copy(tab_i[:, :, 1], tab_f))
            dve.tensor_scalar(tab_i[:, :, 0], tab_i[:, :, 1], T - 1, None, ALU.bitwise_and).then_inc(tab_done, 1)

            def tile(i, c):
                k = 4 * i + c if isinstance(i, int) else None
                if k is None or 0 <= k < MAX_TILES:
                    dve.wait_ge(silu2_done, at(i, c) + 1)
                    if k is None or k >= 2:
                        dve.wait_ge(hidT_ready, at(i, c) - 1)
                    dve.tensor_tensor(hid[:, c % 2, :], silu[:, c % 2, :], ps[:, 2 + c % 2, INTER:2 * INTER],
                                      ALU.mult).then_inc(hid_done, 1)
                if k is None or k + 1 < MAX_TILES:
                    dve.wait_ge(xgT_ready, at(i, c + 1) + 1)
                    if k is None or k + 1 >= 2:
                        dve.wait_ge(gu_ready, at(i, c + 1) - 1)
                    dve.tensor_scalar(xT[:, (c + 1) % 2, 1, :], ps[:, 1, 0:P], modc[:, 4, 1:2], modc[:, 3, 1:2],
                                      ALU.mult, ALU.add).then_inc(xT_dve, 1)
                if k is None or 0 <= k - 2 < MAX_TILES:
                    s = (c - 2) % 4
                    dve.wait_ge(y_ready, at(i, c - 2) + 1)
                    if k is None or k - 2 >= 4:
                        dve.wait_ge(scattered[s], (i + (c - 2) // 4) * 16)
                    dve.tensor_tensor(y_sb[:, s, :], ps[:, 6 + c % 2, 0:E], gates[:, 1, :], ALU.mult).then_inc(y_evac, 1)

            tiles(dve, tile, -1, MAX_TILES + 2)

            for t in range(NT):
                s = t % 6
                dve.wait_ge(z_in[s], 16 * (t // 6 + 1))
                for j in range(TOPK):
                    ins = dve.scalar_tensor_tensor(out=x_sb[:, t, :], in0=z_sb[s][:, j, :], scalar=top_w[:, t, j:j + 1],
                                                   in1=x_sb[:, t, :], op0=ALU.mult, op1=ALU.add)
                    if j < TOPK - 1:
                        link(ins)
                ins.then_inc(acc_done, 1)

        @block.tensor
        def _(pe):
            def group(g):
                if g >= 8:
                    wait_emptied(pe, g - 8)
                return ps[:, g % 8, :]

            pe.wait_ge(ident_in, 16)
            for w in range(4):
                pe.wait_ge(w_in, 16 * 4)
                b = group(WT0 + w)
                for k in range(KE):
                    for f in range(KE):
                        last = pe.transpose(b[:, k * E + f * P:k * E + f * P + P],
                                            w_raw[:, w, f, k * P:k * P + P], ident[:])
                last.then_inc(pe_group, 1)
            pe.wait_ge(wmod_in, 16)
            pe.wait_ge(silu_done, 1)
            b = group(MODC)
            for m in range(6 * KE):
                for k in range(KE):
                    last = pe.matmul(b[:, m:m + 1], wmod[:, k, m * P:m * P + P], cond_silu[:, k:k + 1],
                                     start=(k == 0), stop=(k == KE - 1))
            pe.wait_ge(late_in, 16 * 4)
            for k in range(KE):
                last = pe.transpose(b[:, 32 + k * NX:32 + k * NX + NX], rw_raw[:, k * P:k * P + P], ident[0:NX, 0:NX])
            last.then_inc(pe_group, 1)
            pe.wait_ge(bc_done, 1)
            b = group(GATE)
            for n, m in enumerate((2, 5)):
                for k in range(KE):
                    last = pe.matmul(b[:, n * E:n * E + E], cond_bc[:, k, :], wmod[:, k, m * E:m * E + E],
                                     start=(k == 0), stop=(k == KE - 1))
            last.then_inc(pe_group, 1)
            for g in range(4):
                ch, k = g // KE, g % KE
                pe.wait_ge(xh_done, TC * ch + TC)
                b = group(XT0 + g)
                for t in range(TC):
                    last = pe.transpose(b[:, t * P:t * P + P], xh[:, TC * ch + t, k * P:k * P + P], ident[:])
                last.then_inc(pe_group, 1)

            pe.wait_ge(dve_evac, 4)

            def project_t(g0, w, f):
                for ch in range(NCH):
                    pe.wait_ge(act_evac, 2 * ch + 2)
                    b = group(g0 + ch)
                    for k in range(KE):
                        last = pe.matmul(b, wT[:, w, k, f * P:f * P + P], hT[:, k, CH * ch:CH * ch + CH],
                                         start=(k == 0), stop=(k == KE - 1))
                    last.then_inc(pe_group, 1)

            project_t(Q0, 0, 0)
            project_t(K0, 1, 0)
            for g in range(4):
                b = group(V0 + g)
                for n in range(2):
                    t = 2 * g + n
                    for k in range(KE):
                        last = pe.matmul(b[:, n * E:n * E + E], hT[:, k, t * P:t * P + P], wT[:, 2, k, :],
                                         start=(k == 0), stop=(k == KE - 1))
                last.then_inc(pe_group, 1)
            project_t(Q1, 0, 1)
            project_t(K1, 1, 1)
            pe.wait_ge(act_evac, count(N_GROUPS - 1, "act"))
            pe.wait_ge(dve_evac, count(N_GROUPS - 1, "dve"))
            pe.wait_ge(rows_in, 16 * 3 * SLOTS)

            def step(i, c):
                maxima, rows, probabilities, output = kind(i, c)
                for j in range(NT):
                    if probabilities:
                        scores_t(i, c, j)
                        if j % 2 == 1 and j >= 3:
                            sum_pv(i, c, (j - 3) // 2)
                    if maxima:
                        scores(i, c + 2, j)
                    if output and j == 1:
                        sum_pv(i, c - 1, 3)
                    if rows and j == 1:
                        rows_t(i, c + 1)
                    if output and j == 5:
                        merge_o(i, c - 1)

            def loaded(i, c):
                pe.wait_ge(st_in[c % SLOTS], 80 * (i + c // SLOTS) + 80)

            def scores(i, c, q):
                s = c % SLOTS
                if q == 0:
                    loaded(i, c)
                for half in range(NCH):
                    n = 2 * q + half
                    if n >= 2 or not (is0(i) and c == 0):
                        pe.wait_ge(max_used, at(i, c, k=16) + n - 1)
                    pe.matmul(ps_max[half], q_st[0:R_QK, s, q * P:q * P + P],
                              k_st[0:R_QK, 0, s, CH * half:CH * half + CH], start=True, stop=True).then_inc(max_ready, 1)

            def scores_t(i, c, j):
                s = c % SLOTS
                if j == 0:
                    pe.wait_ge(m_in, at(i, c, k=16) + 16)
                    pe.wait_ge(bias_done, at(i, c, k=2) + 2)
                if j >= 2 or not (is0(i) and c == 0):
                    pe.wait_ge(exp_done, at(i, c, k=NT) + j - 1)
                for ch in range(NCH):
                    bank = ps_st[j % 2][:, ch, :]
                    own = j // TC == ch
                    last = pe.matmul(bank, k_st[0:R_ALL, ch, s, j * P:j * P + P], q_st[0:R_ALL, s, CH * ch:CH * ch + CH],
                                     start=True, stop=not own)
                    if own:
                        t = j % TC
                        last = pe.matmul(bank[:, t * P:t * P + P], ident[:], bias_d[:, s, :], start=False, stop=True)
                last.then_inc(st_ready, 1)

            def sum_pv(i, c, pair):
                if pair == 0:
                    pe.wait_ge(v_staged, at(i, c) + 1)
                    if not (is0(i) and c == 0):
                        pe.wait_ge(o_evac, at(i, c))
                pe.wait_ge(exp_done, at(i, c, k=NT) + 2 * pair + 2)
                for n in range(2):
                    j = 2 * pair + n
                    for ch in range(NCH):
                        r = 32 * (2 * n + ch)
                        last = pe.matmul(ps_o[r:r + 32], v_st[:, c % 2, j, :], probs[:, j % 4, CH * ch:CH * ch + CH],
                                         start=(pair == 0), stop=(pair == 3))
                last.then_inc(pv_done, 1)

            def rows_t(i, g):
                pe.wait_ge(negm_done, at(i, g) + 1)
                if not (is0(i) and g < 2):
                    pe.wait_ge(ot_used, at(i, g) - 1)
                pe.transpose(ps_misc[0:NT, 256:256 + P], negm[:, g % 2, :], ident[:]).then_inc(mT_ready, 1)

            def merge_o(i, c):
                pe.wait_ge(o_evac, at(i, c) + 1)
                if not (is0(i) and c == 0):
                    pe.wait_ge(ot_used, at(i, c) + 1)
                nr = c + 2
                if not (isinstance(i, int) and 4 * i + nr >= H):
                    pe.wait_ge(m_chain, at(i, nr, k=5) + 1)
                for t in range(TC):
                    last = pe.matmul(ps_ot[:, t].rearrange("p c d -> p (c d)"), o_sb[:, t * P:t * P + P], merge[:],
                                     start=True, stop=True)
                last.then_inc(ot_ready, 1)

            pe.wait_ge(consts_in, 16 * 5)
            pe.sem_inc(ot_ready, 1)
            steps(pe, step)
            sum_pv(3, 3, 3)
            merge_o(3, 3)

            pe.wait_ge(wo_done, 2)
            for t in range(NT + 1):
                if t < NT:
                    pe.wait_ge(ot_used, H + 1)
                    if t >= 2:
                        pe.wait_ge(attT_evac, t - 1)
                    for k in range(KE):
                        last = pe.transpose(ps[:, t % 2, k * P:k * P + P], attn[:, t // TC, t % TC, k * P:k * P + P], ident[:])
                    last.then_inc(attT_ready, 1)
                if t >= 1:
                    n = t - 1
                    pe.wait_ge(attT_evac, n + 1)
                    if n >= 2:
                        pe.wait_ge(x2_done, n - 1)
                    for k in range(KE):
                        last = pe.matmul(ps[:, 2 + n % 2, 0:E], attT[:, n % 2, k, :], wo_sb[:, k, :],
                                         start=(k == 0), stop=(k == KE - 1))
                    last.then_inc(y1_ready, 1)
            for g in range(4):
                hf, k = g // KE, g % KE
                pe.wait_ge(xn_done, TC * hf + TC)
                for t in range(TC):
                    last = pe.transpose(ps[:, 4 + g, t * P:t * P + P], xn[:, TC * hf + t, k * P:k * P + P], ident[:])
                last.then_inc(xnT_ready, 1)
            for hf in range(NCH):
                pe.wait_ge(xnT_evac, KE * hf + KE)
                for t in range(TC):
                    for k in range(KE):
                        last = pe.matmul(ps[:, hf, t * NX:t * NX + NX], hT[:, k, (TC * hf + t) * P:(TC * hf + t) * P + P],
                                         rwT[:, k, :], start=(k == 0), stop=(k == KE - 1))
                last.then_inc(logits_ready, 1)
            pe.wait_ge(mask_done, 1)
            flat_mask = mask.rearrange("p t x -> p (t x)")
            for n in range(1, NT):
                pe.matmul(ps[:, 2, n * NX:P], triangle[:, 1, :], flat_mask[:, 0:P - n * NX], start=(n == 1), stop=False,
                          skip_group_check=True)
            pe.matmul(ps[:, 2, 0:P], triangle[:, 0, :], flat_mask, start=False, stop=True, skip_group_check=True)
            for n in range(NT):
                last = pe.matmul(ps[:, 3, 0:NX], triangle[:, 1, :], mask[:, n, :], start=(n == 0), stop=(n == NT - 1))
            last.then_inc(before_ready, 1)
            for n in range(NT * TOPK):
                pe.wait_ge(hot_done, 2 * n + 2)
                pe.matmul(ps[:, 4, 0:NTAB], hot_lo[:, n % 2, :], hot_hi[:, n % 2, :], start=(n == 0),
                          stop=(n == NT * TOPK - 1)).then_inc(hot_used, 1)
            pe.wait_ge(tab_done, 1)
            pe.wait_ge(w_done, 16 * 3 * NX)

            def expert(i, c):
                return pe.value_load(exp_i[0:1, bass.ds(at(i, c), 1)], min_val=0, max_val=NX - 1)

            def tile(i, c):
                k = 4 * i + c if isinstance(i, int) else None
                if k is None or 0 <= k < MAX_TILES:
                    e = expert(i, c)
                    pe.wait_ge(xT_act, at(i, c) + 1)
                    pe.wait_ge(xT_dve, at(i, c) + 1)
                    if k is None or k >= 2:
                        pe.wait_ge(hid_done, at(i, c) - 1)
                    for kk in range(KE):
                        last = pe.matmul(ps[:, 2 + c % 2, 0:2 * INTER], xT[:, c % 2, kk, :],
                                         w_gu[:, bass.ds(e, 1), kk, :].rearrange("p x n -> p (x n)"),
                                         start=(kk == 0), stop=(kk == KE - 1))
                    last.then_inc(gu_ready, 1)
                if k is None or 0 <= k - 1 < MAX_TILES:
                    pe.wait_ge(hid_done, at(i, c - 1) + 1)
                    if k is None or k - 1 >= 2:
                        pe.wait_ge(hidT_evac, at(i, c - 1) - 1)
                    for kk in range(2):
                        last = pe.transpose(ps[0:IH, 4 + (c - 1) % 2, kk * P:kk * P + P],
                                            hid[:, (c - 1) % 2, kk * IH:kk * IH + IH], ident[:])
                    last.then_inc(hidT_ready, 1)
                if k is None or k + 1 < MAX_TILES:
                    s = (c + 1) % 4
                    pe.wait_ge(gathered[s], (i + (c + 1) // 4) * 16 + 16)
                    if k is None or k + 1 >= 1:
                        pe.wait_ge(xT_act, at(i, c + 1))
                        pe.wait_ge(xT_dve, at(i, c + 1))
                    for kk in range(KE):
                        last = pe.transpose(ps[:, kk, 0:P], xg[:, s, kk * P:kk * P + P], ident[:])
                    last.then_inc(xgT_ready, 1)
                if k is None or 0 <= k - 2 < MAX_TILES:
                    e = expert(i, c - 2)
                    pe.wait_ge(hidT_evac, at(i, c - 2) + 1)
                    if k is None or k - 2 >= 2:
                        pe.wait_ge(y_evac, at(i, c - 2) - 1)
                    for kk in range(2):
                        last = pe.matmul(ps[:, 6 + c % 2, 0:E], hidT[0:IH, c % 2, kk, :],
                                         w_dn[0:IH, bass.ds(e, 1), kk, :].rearrange("p x n -> p (x n)"),
                                         start=(kk == 0), stop=(kk == 1))
                    last.then_inc(y_ready, 1)

            tiles(pe, tile, -1, MAX_TILES + 2)


_INPUTS = {"x": "L0_attn_x", "Wq": "L0_attn_Wq", "Wk": "L0_attn_Wk", "Wv": "L0_attn_Wv", "Wo": "L0_attn_Wo",
           "bq": "L0_attn_bq", "bk": "L0_attn_bk", "bv": "L0_attn_bv", "bo": "L0_attn_bo",
           "slopes": "L0_attn_slopes", "router_w": "L0_ffn_router_w", "expert_bias": "L0_ffn_expert_bias",
           "gate_proj": "L0_ffn_gate_proj", "up_proj": "L0_ffn_up_proj", "down_proj": "L0_ffn_down_proj",
           "c": "L0_c", "wmod": "L0_wmod"}


def kernel(**inputs):
    import concourse.bacc as bacc
    from concourse.bass_utils import run_bass_kernel_spmd

    nc = bacc.Bacc("TRN2", target_bir_lowering=False, num_devices=1)
    arrays = {short: np.ascontiguousarray(inputs[name]) for short, name in _INPUTS.items()}
    arrays["x"] = arrays["x"].reshape(T, E)
    arrays.update(host_constants())
    aps = {n: nc.dram_tensor(f"in_{n}", v.shape, mybir.dt.from_np(v.dtype), kind="ExternalInput").ap()
           for n, v in arrays.items()}
    out = nc.dram_tensor("out_0", (T, E), F32, kind="ExternalOutput").ap()
    adaln_block(nc, aps, out)
    r = run_bass_kernel_spmd(nc, [{f"in_{n}": v for n, v in arrays.items()}], core_ids=[0])
    return r.results[0]["out_0"].reshape(1, T, E)
```

```python
from contextlib import ExitStack

import numpy as np

import concourse.bass as bass
from concourse import mybir

F32 = mybir.dt.float32
BF16 = mybir.dt.bfloat16
U32 = mybir.dt.uint32
I32 = mybir.dt.int32
ALU = mybir.AluOpType
ACT = mybir.ActivationFunctionType
AX_X = mybir.AxisListType.X

P = 128
T = 1024
NT = T // P
E = 256
KE = E // P
H = 16
D = E // H
VW = D + 1
CH = 512
NCH = T // CH
TC = CH // P
LN_EPS = 1e-5
GATE_MIN = 0.25
HT = P // D

Q_PARTS = (0, 1, 2, 0, 1, 0)
K_PARTS = (0, 0, 0, 1, 1, 2)
R_QK = 6 * D
R_AL = 6 * TC
R_M = 3
R_ALL = R_QK + R_AL + R_M

W_DIST = T + (NT - 1) * P
DIST0 = (NT - 1) * P

SLOTS = 4
NX = 16
TOPK = 4
INTER = 224
IH = INTER // 2
NTAB = 48
MAX_TILES = (T * TOPK + NX * (P - 1)) // P


def host_constants():
    def bf16_bits(a):
        return (np.ascontiguousarray(a, np.float32).view(np.uint32) >> 16).astype(np.uint16)

    i = np.arange(P)[:, None]
    dist = -np.abs(i - (np.arange(W_DIST)[None, :] - DIST0)).astype(np.float32)
    c = (np.arange(P) % NT)[:, None]
    j = np.arange(T)[None, :]
    same = (j // P) == c
    alibi_key = np.where(same, 0, -np.abs(j - P * c)).astype(np.float32)
    alibi_sign = np.sign(np.arange(NT)[None, :] - c).astype(np.float32)
    t = np.arange(T)
    rows = [((t // P) % TC == k) * 1.0 for k in range(TC)]
    qrows = np.stack(rows * 3 + [r * (t % P) for r in rows] * 3)
    merge = np.zeros((P, NCH * VW), np.float32)
    for g in range(4):
        for d in range(VW):
            merge[32 * g + d, (g % NCH) * VW + d] = 1.0
    return {
        "ident": np.eye(P, dtype=np.float32),
        "dist": dist,
        "alibi_key": alibi_key,
        "alibi_sign": alibi_sign,
        "query_rows": bf16_bits(qrows),
        "one_rows": bf16_bits(np.ones((R_M, T))),
        "triangle": bf16_bits(np.concatenate([np.triu(np.ones((P, P)), 1), np.ones((P, P))], 1)),
        "route": np.concatenate([merge] + [np.broadcast_to(r, (P, r.shape[-1])) for r in (
            np.arange(NX), P * np.arange(NT), np.arange(NTAB), np.arange(P),
            1 + T * np.arange(TOPK)[None, None, :] + P * np.arange(NT)[None, :, None] + np.arange(P)[:, None, None])
            for r in [np.asarray(r).reshape(-1 if np.ndim(r) == 1 else P, *([] if np.ndim(r) == 1 else [-1]))]],
            1).astype(np.float32),
    }


def on_partitions(ap, n):
    return bass.AP(ap.tensor, ap.offset, [[0, n]] + [list(a) for a in ap.ap])


def adaln_block(nc, a, out):
    with ExitStack() as ctx:
        def sb(name, shape, dt=F32):
            return ctx.enter_context(nc.sbuf_tensor(name, shape, dt))

        def sem(name):
            return ctx.enter_context(nc.semaphore(name))

        def dram(name, shape, dt):
            return nc.dram_tensor(name, shape, dt, kind="Internal").ap()

        q_rows = dram("q_rows", [6, H * D, T], BF16)
        k_rows = dram("k_rows", [6, H * D, T], BF16)
        al_rows = dram("al_rows", [6, H * NT, T], BF16)
        m_rows = dram("m_rows", [H, R_M, NT, P], BF16)
        xn_rows = dram("xn_rows", [T, E], F32)
        z_rows = dram("z_rows", [TOPK * T, E], F32)

        w_gu = sb("w_gu", [P, NX, KE, 2 * INTER])
        w_dn = sb("w_dn", [P, NX, 2, E])
        flat_gu = w_gu[:].rearrange("p x k n -> p (x k n)")
        flat_dn = w_dn[:].rearrange("p x k n -> p (x k n)")

        def carver(flat):
            used = [0]

            def carve(shape, dt=F32):
                n = int(np.prod(shape[1:])) * (1 if dt in (F32, U32, I32) else 2) // (1 if dt in (F32, U32, I32) else 4)
                v = flat[0:shape[0], used[0]:used[0] + n]
                used[0] += n
                assert used[0] <= flat.shape[1]
                v = v if dt == F32 else v.bitcast(dt)
                names = "abcdef"[:len(shape) - 1]
                return v.rearrange(f"p ({' '.join(names)}) -> p {' '.join(names)}",
                                   **{c: m for c, m in zip(names[1:], shape[2:])}) if len(shape) > 2 else v
            return carve

        early = carver(flat_gu)
        qk_part = early([P, 2, KE, 3, T], BF16)
        wmod = early([P, KE, 6 * E])
        al_part = early([P, 6, T], BF16)
        xh = early([P, NT, E])
        early = carver(flat_dn)
        w_raw = early([P, 4, KE, E])
        wT = early([P, 4, KE, E])
        al_key = early([P, T])
        gsign = al_key[:, 0:2 * E].rearrange("p (g e) -> p g e", g=2)
        gabs = al_key[:, 2 * E:].rearrange("p (g e) -> p g e", g=2)
        qk_f = early([P, 2, CH])
        qk_r = early([P, 2, CH])
        rw_raw = early([NX, E])

        x_sb = sb("x_sb", [P, NT, E])
        hT = sb("hT", [P, KE, T])
        wo_sb = sb("wo_sb", [P, KE, E])
        cond = sb("cond", [P, KE])
        cond_silu = sb("cond_silu", [P, KE])
        cond_bc = sb("cond_bc", [P, KE, P])
        modc = sb("modc", [P, 4, KE])
        gates = sb("gates", [P, 2, E])
        qk_bias = sb("qk_bias", [P, 2, KE])
        q_bias_s = sb("q_bias_s", [P, KE])
        v_bias = sb("v_bias", [P, E])
        o_bias = sb("o_bias", [P, E])
        x_bias = sb("x_bias", [P, NX])
        rwT = sb("rwT", [P, KE, NX])
        slopes = sb("slopes", [P, H])
        slope_hc = sb("slope_hc", [P, 1])
        ident = sb("ident", [P, P])
        triangle = sb("triangle", [P, 2, P], BF16)
        route = sb("route", [P, NCH * VW + NX + NT + NTAB + P + NT * TOPK])
        merge = route[:, 0:NCH * VW]
        dist = sb("dist", [P, W_DIST])
        table_call = sb("table_call", [1, 1])
        stats = sb("stats", [P, NT, 6])
        mv = sb("mv", [P, NT, 2])
        std = sb("std", [P, NT])
        rstd = sb("rstd", [P, NT])
        al_sign = sb("al_sign", [P, NT])
        sign_part = sb("sign_part", [P, 3, NT], BF16)
        v_all = sb("v_all", [P, NT, E])
        q_st = sb("q_st", [P, SLOTS, T], BF16)
        k_st = sb("k_st", [P, NCH, SLOTS, T], BF16)
        v_st = sb("v_st", [P, 2, NT, 32])
        bias_t = sb("bias_t", [P, 2, W_DIST])
        bias_d = sb("bias_d", [P, SLOTS, P])
        slope_now = sb("slope_now", [P, 2, 1])
        junk = sb("junk", [P, 2, CH], BF16)
        mx = sb("mx", [P, 2, NT, NCH])
        negm = sb("negm", [P, 2, NT])
        m_rest = sb("m_rest", [P, NT])
        m_part = sb("m_part", [P, 2, R_M, NT], BF16)
        m_row = sb("m_row", [R_M * NT, P], BF16)
        ident_b = sb("ident_b", [P, P], BF16)
        probs = sb("probs", [P, 4, T])
        o_sb = sb("o_sb", [P, CH])
        rsum = sb("rsum", [P, TC, NCH])
        attn = sb("attn", [P, NCH, TC, E])

        al_rest = attn[:].rearrange("p c t e -> p (c t e)")[:, 0:T]
        xn = v_all
        late = carver(bias_t[:].rearrange("p s n -> p (s n)"))
        attT = late([P, 2, KE, P])
        logits = late([P, NT, NX])
        top8 = late([P, NT, 8])
        top8_i = late([P, NT, 8], U32)
        top_i = late([P, NT, TOPK])
        top_w = late([P, NT, TOPK])
        top_e = late([P, NT, TOPK])
        top_s = late([P, NT])
        hot = late([P, NT, TOPK, NX])
        hot_a = late([P, NT, TOPK, NX])
        mask = late([P, NT, NX], BF16)
        before = late([P, NT, NX])
        over = late([P, NX, NT])
        n_tiles = late([P, NX])
        ends = late([P, NX])
        starts = late([P, NX])
        pos = late([P, NT, TOPK])
        pos_i = late([P, NT, TOPK], I32)
        lo_i = late([P, NT, TOPK], I32)
        hi_i = late([P, NT, TOPK], I32)
        lo_f = late([P, NT, TOPK])
        hi_f = late([P, NT, TOPK])
        hot_lo = late([P, 2, P])
        hot_hi = late([P, 2, NTAB])
        tab_f = late([P, NTAB])
        tab_e = late([P, NTAB])
        tab_i = late([P, NTAB, 2], I32)
        exp_f = late([1, NTAB])
        exp_i = late([1, NTAB], I32)
        late = carver(probs[:].rearrange("p s n -> p (s n)"))
        xg = late([P, 4, E])
        xT = late([P, 2, KE, P])
        silu = late([P, 2, INTER])
        hid = late([P, 2, INTER])
        hidT = late([P, 2, 2, P])
        y_sb = late([P, 4, E])
        idx = late([P, 4, 2], I32)
        idx_s = late([P, 4, 1], I32)
        ended = xg.rearrange("p s e -> p (s e)")[0:1, 0:NTAB * NX]
        z_sb = [k_st[:, s // 2].rearrange("p s n -> p (s n)").bitcast(F32)[:, (s % 2) * 1024:(s % 2) * 1024 + 1024]
                for s in range(4)] + [q_st[:].rearrange("p s n -> p (s n)").bitcast(F32)[:, s * 1024:s * 1024 + 1024]
                                      for s in range(2)]
        z_sb = [z.rearrange("p (j e) -> p j e", j=TOPK) for z in z_sb]

        ps = ctx.enter_context(nc.psum_tensor("ps", [P, 8, CH], F32))
        ps_max = [ps[:, 0, :], ps[:, 1, :]]
        ps_st = [ps[:, 2:4, :], ps[:, 4:6, :]]
        ps_o = ps[:, 6, :]
        ps_misc = ps[:, 7, :]
        ps_ot = ps_misc[:, 0:TC * NCH * VW].rearrange("p (t c d) -> p t c d", t=TC, c=NCH)

        x_in = [sem("x_in0"), sem("x_in1")]
        cond_in = sem("cond_in")
        wmod_in = [sem("wmod_in0"), sem("wmod_in1")]
        w_in = [sem(f"w_in{w}") for w in range(4)]
        ident_in = sem("ident_in")
        consts_in = sem("consts_in")
        dist_in = sem("dist_in")
        al_in = sem("al_in")
        sign_in = sem("sign_in")
        slopes_in = sem("slopes_in")
        router_in = sem("router_in")
        rows_in = sem("rows_in")
        silu_done = sem("silu_done")
        bc_done = sem("bc_done")
        var_done = sem("var_done")
        std_done = sem("std_done")
        xh_done = sem("xh_done")
        pe_group = sem("pe_group")
        dve_evac = sem("dve_evac")
        act_evac = sem("act_evac")
        mod_done = sem("mod_done")
        dve_chain = sem("dve_chain")
        q_bias_done = sem("q_bias_done")
        preload = sem("preload")
        sign_done = sem("sign_done")
        pool_chain = sem("pool_chain")
        raw_mod = sem("raw_mod")
        qk_first = sem("qk_first")
        qk_rest = sem("qk_rest")
        qk_second = sem("qk_second")
        qk_split = sem("qk_split")
        qk_stored = [sem(f"qk_stored{n}") for n in range(3)]
        al_done = sem("al_done")
        al_stored = sem("al_stored")
        v_done = sem("v_done")
        st_in = [sem(f"st_in{s}") for s in range(SLOTS)]
        al_ld = [sem(f"al_ld{s}") for s in range(SLOTS)]
        v_init = sem("v_init")
        slope_cp = sem("slope_cp")
        bias_t_done = sem("bias_t_done")
        bias_a_done = sem("bias_a_done")
        bias_p_done = sem("bias_p_done")
        bias_d_done = sem("bias_d_done")
        v_staged = sem("v_staged")
        max_ready = sem("max_ready")
        max_used = sem("max_used")
        negm_done = sem("negm_done")
        mT_ready = sem("mT_ready")
        m_chain = sem("m_chain")
        m_evac = sem("m_evac")
        m_stored = sem("m_stored")
        m_in = sem("m_in")
        st_ready = sem("st_ready")
        exp_done = sem("exp_done")
        pv_done = sem("pv_done")
        o_evac = sem("o_evac")
        ot_ready = sem("ot_ready")
        ot_recip = sem("ot_recip")
        ot_used = sem("ot_used")
        settled = sem("settled")
        fin = sem("fin")
        late_in = sem("late_in")
        wo_done = sem("wo_done")
        xg_done = sem("xg_done")
        w_stage = sem("w_stage")
        w_done = sem("w_done")
        attT_ready = sem("attT_ready")
        attT_evac = sem("attT_evac")
        y1_ready = sem("y1_ready")
        x2_done = sem("x2_done")
        var2_done = sem("var2_done")
        std2_done = sem("std2_done")
        xn_done = sem("xn_done")
        xn_stored = sem("xn_stored")
        xnT_ready = sem("xnT_ready")
        xnT_evac = sem("xnT_evac")
        logits_ready = sem("logits_ready")
        top_shift = sem("top_shift")
        top_exp = sem("top_exp")
        mask_done = sem("mask_done")
        before_ready = sem("before_ready")
        hot_done = sem("hot_done")
        hot_used = sem("hot_used")
        tab_done = sem("tab_done")
        idx_cp = sem("idx_cp")
        idx_s_cp = sem("idx_s_cp")
        gathered = [sem(f"gathered{s}") for s in range(4)]
        xgT_ready = sem("xgT_ready")
        xT_act = sem("xT_act")
        xT_dve = sem("xT_dve")
        gu_ready = sem("gu_ready")
        silu2_done = sem("silu2_done")
        hid_done = sem("hid_done")
        hidT_ready = sem("hidT_ready")
        hidT_evac = sem("hidT_evac")
        y_ready = sem("y_ready")
        y_evac = sem("y_evac")
        scattered = [sem(f"scattered{s}") for s in range(4)]
        z_in = [sem(f"z_in{s}") for s in range(6)]
        z_used = sem("z_used")
        acc_done = sem("acc_done")
        out_stored = sem("out_stored")

        block = ctx.enter_context(nc.Block())

        WQ, WK, MODA, XT, Q0, K0, WV, WO, MODB, GATE, V0, Q1, K1 = 0, 1, 2, 3, 7, 9, 11, 12, 13, 14, 15, 19, 21
        N_GROUPS = 23
        emptied_by = (["dve"] * 3 + ["act", "dve"] * 2 + ["act"] * 16)
        bank_of = [0, 1, 2, 3, 4, 5, 6, 7, 2, 3, 4, 5, 6, 2, 3, 4, 5, 6, 2, 3, 4, 5, 6]

        def count(group, engine):
            return sum(e == engine for e in emptied_by[:group + 1])

        def wait_emptied(eng, group):
            s = dve_evac if emptied_by[group] == "dve" else act_evac
            eng.wait_ge(s, count(group, emptied_by[group]))

        def settle(eng):
            eng.sem_inc(settled, 1)

        def at(i, c, per=SLOTS, k=1):
            return k * (4 * i + c)

        def is0(i):
            return isinstance(i, int) and i == 0

        def steps(eng, step):
            for c in (-2, -1, 0):
                step(0, c)
            with eng.Fori(0, 3) as i:
                for c in range(1, 1 + SLOTS):
                    step(i, c)
            for c in (1, 2, 3):
                step(3, c)

        def tiles(eng, tile, first, last):
            for k in range(first, 8):
                tile(0, k)
            with eng.Fori(2, MAX_TILES // 4) as i:
                for c in range(4):
                    tile(i, c)
            for k in range(MAX_TILES // 4 * 4, last):
                tile(MAX_TILES // 4, k - MAX_TILES // 4 * 4)

        def kind(i, c):
            if isinstance(i, int):
                h = 4 * i + c
                return h + 2 < H, 0 <= h + 1 < H, h >= 0, h >= 1
            return True, True, True, True

        @block.sync
        def _(sp):
            wm = a["wmod"].rearrange("(k p) m -> p k m", p=P)
            for k in range(2):
                sp.dma_start(x_sb[:, 4 * k:4 * k + 4, :],
                             a["x"].rearrange("(t p) e -> p t e", p=P)[:, 4 * k:4 * k + 4, :]).then_inc(x_in[k], 16)
            sp.dma_start(ident[:], a["ident"]).then_inc(ident_in, 16)

            def load_w(n):
                w = a[("Wq", "Wk", "Wv", "Wo")[n]]
                sp.dma_start(w_raw[:, n], w.rearrange("(k p) e -> p k e", p=P)).then_inc(w_in[n], 16)

            load_w(0)
            load_w(1)
            sp.dma_start(al_key[:], a["alibi_key"]).then_inc(al_in, 16)
            sp.dma_start(wmod[:, :, 2 * E:], wm[:, :, 2 * E:]).then_inc(wmod_in[1], 16)
            sp.dma_start(dist[:], a["dist"]).then_inc(dist_in, 16)
            load_w(2)
            load_w(3)
            sp.dma_start(rw_raw, a["router_w"]).then_inc(router_in, 16)
            sp.dma_start(q_st[R_QK:R_QK + R_AL], a["query_rows"].bitcast(BF16).unsqueeze(1).broadcast_to([R_AL, SLOTS, T])).then_inc(rows_in, 16)
            sp.dma_start(k_st[R_QK + R_AL:R_ALL].rearrange("p c s n -> p (c s) n"),
                         a["one_rows"].bitcast(BF16).unsqueeze(1).broadcast_to([R_M, NCH * SLOTS, T])).then_inc(rows_in, 16)

            def store_qk(n):
                f, first, last = ((0, 0, 2), (0, 2, HT), (1, 0, HT))[n]
                p0, p1 = D * first, D * last
                for w, rows in enumerate((q_rows, k_rows)):
                    sp.wait_ge(qk_split, 4 * f + 2 * w + 2)
                    g = 0
                    for k in (3, 2, 1):
                        src = (qk_part[p0:p1, w, f, 0:k, :] if w == 0 else
                               qk_part[p0:p1, w, f, 3 - k:4 - k, :].broadcast_to([p1 - p0, k, T]))
                        sp.dma_start(rows[g:g + k, P * f + p0:P * f + p1, :].rearrange("g r t -> r g t"),
                                     src).then_inc(qk_stored[n], 16)
                        g += k

            def load_qk(i, c):
                s, h = c % SLOTS, at(i, c)
                sp.dma_start(q_st[0:R_QK, s, :], q_rows[:, bass.ds(h * D, D), :]).then_inc(st_in[s], 16)
                for ch in range(NCH):
                    sp.dma_start(k_st[0:R_QK, ch, s, :], k_rows[:, bass.ds(h * D, D), :]).then_inc(st_in[s], 16)

            def load_al(i, c):
                s, h = c % SLOTS, at(i, c)
                for ch in range(NCH):
                    sp.dma_start(k_st[R_QK:R_QK + R_AL, ch, s, :], al_rows[:, bass.ds(h * NT + ch * TC, TC), :]).then_inc(al_ld[s], 16)

            store_qk(0)
            sp.wait_ge(qk_stored[0], 16 * 6)
            load_qk(0, 0)
            load_qk(0, 1)
            store_qk(1)
            sp.wait_ge(al_done, 1)
            sp.wait_ge(sign_done, 1)
            sp.dma_start(al_rows.rearrange("g r n -> r g n"), al_part[:]).then_inc(al_stored, 16)
            sp.wait_ge(al_stored, 16)
            load_al(0, 0)
            load_al(0, 1)
            sp.wait_ge(qk_stored[1], 16 * 6)

            def step(i, c):
                _, rows, _, _ = kind(i, c)
                if not isinstance(i, int) or 2 <= 4 * i + c + 3 < H:
                    if not isinstance(i, int) or 4 * i + c >= 1:
                        sp.wait_ge(st_ready, at(i, c, k=NT))
                    load_qk(i, c + 3)
                    load_al(i, c + 3)
                if is0(i) and c == 0:
                    store_qk(2)
                if rows:
                    g = c + 1
                    sp.wait_ge(m_evac, at(i, g) + 1)
                    sp.dma_start(m_rows[at(i, g)].rearrange("r i x -> (r i) x"), m_row[:]).then_inc(m_stored, 16)
                    sp.wait_ge(m_stored, at(i, g, k=16) + 16)
                    sp.dma_start(q_st[R_QK + R_AL:R_ALL, g % SLOTS, :],
                                 m_rows[at(i, g)].rearrange("r i x -> r (i x)")).then_inc(m_in, 16)
                if is0(i) and c == 0:
                    sp.wait_ge(qk_stored[2], 16 * 6)

            steps(sp, step)

            for hf in range(NCH):
                sp.wait_ge(xn_done, TC * hf + TC)
                sp.dma_start(xn_rows.rearrange("(t p) e -> p t e", p=P)[:, TC * hf:TC * hf + TC, :],
                             xn[:, TC * hf:TC * hf + TC, :]).then_inc(xn_stored, 16)
            for s in range(4):
                sp.wait_ge(scattered[s], 16 * len(range(s, MAX_TILES, 4)))
            for t in range(NT):
                s = t % 6
                if t >= 6:
                    sp.wait_ge(acc_done, t - 6 + 1)
                sp.dma_start(z_sb[s], z_rows.rearrange("(j t p) e -> p t j e", p=P, j=TOPK)[:, t]).then_inc(z_in[s], 16)
            for t in range(NT):
                sp.wait_ge(acc_done, t + 1)
                sp.dma_start(out[P * t:P * t + P, :], x_sb[:, t, :]).then_inc(out_stored, 16)
            sp.wait_ge(out_stored, 16 * NT)

        @block.scalar
        def _(act):
            act.dma_start(cond[:], a["c"].rearrange("o (k p) -> p (o k)", p=P), allow_slow_non_contiguous=True).then_inc(cond_in, 16)
            wm = a["wmod"].rearrange("(k p) m -> p k m", p=P)
            act.dma_start(wmod[:, :, 0:2 * E], wm[:, :, 0:2 * E]).then_inc(wmod_in[0], 16)
            act.wait_ge(preload, 1)
            act.activation(table_call[:], table_call[:], ACT.Sqrt)
            act.wait_ge(var_done, 1)
            act.activation(std[:], std[:], ACT.Sqrt).then_inc(std_done, 1)
            act.wait_ge(cond_in, 16)
            act.activation(cond_silu[:], cond[:], ACT.Silu).then_inc(silu_done, 1)
            act.wait_ge(mod_done, 1)
            for ch in range(NCH):
                g = XT + KE * ch
                act.wait_ge(pe_group, g + 1)
                act.activation(hT[:, 0, CH * ch:CH * ch + CH], ps[:, bank_of[g], :], ACT.Identity,
                               bias=modc[:, 0, 0:1], scale=modc[:, 1, 0:1]).then_inc(act_evac, 1)

            def evac_qk(n, g, w, f, ch):
                act.wait_ge(pe_group, g + 1)
                if n >= 2:
                    act.wait_ge(qk_rest, n - 1)
                bias = q_bias_s[:, f:f + 1] if w == 0 else qk_bias[:, 1, f:f + 1]
                act.activation(qk_f[:, n % 2], ps[:, bank_of[g], :], ACT.Identity, bias=bias,
                               scale=D ** -0.5 if w == 0 else 1.0).then_inc(act_evac, 1)
                act.wait_ge(act_evac, count(g, "act"))
                act.copy(qk_part[:, w, f, 0, CH * ch:CH * ch + CH], qk_f[:, n % 2]).then_inc(qk_first, 1)

            def second_part(n, w, f, ch):
                act.wait_ge(qk_rest, n + 1)
                act.copy(qk_part[:, w, f, 1, CH * ch:CH * ch + CH], qk_r[:, n % 2]).then_inc(qk_second, 1)

            def make_bias_t(i, c, third):
                if not (isinstance(i, int) and 4 * i + c < 2):
                    act.wait_ge(max_used, at(i, c - 1, k=16))
                settle(act)
                w = W_DIST // 3
                act.activation(bias_t[:, c % 2, w * third:w * third + w], dist[:, w * third:w * third + w], ACT.Identity,
                               scale=slopes[:, bass.ds(at(i, c), 1)]).then_inc(bias_t_done if third < 2 else bias_a_done, 1)

            act.wait_ge(consts_in, 16 * 4)
            act.wait_ge(q_bias_done, 1)
            for n in range(4):
                evac_qk(n, Q0 + n, n // 2, 0, n % 2)
            act.wait_ge(dist_in, 16)
            act.wait_ge(slopes_in, 16)
            for h in range(2):
                for third in range(3):
                    make_bias_t(0, h, third)
            act.activation(table_call[:], table_call[:], ACT.Exp)
            for w in range(2, 4):
                act.wait_ge(pe_group, WV + w - 1)
                act.copy(wT[:, w].rearrange("p k f -> p (k f)"), ps[:, bank_of[WV + w - 2], :]).then_inc(act_evac, 1)
            act.wait_ge(pe_group, MODB + 1)
            act.copy(modc[:, 2:4, :].rearrange("p m k -> p (m k)"), ps[:, bank_of[MODB], 0:2 * KE]).then_inc(raw_mod, 1)
            act.copy(rwT[:].rearrange("p k n -> p (k n)"), ps[:, bank_of[MODB], 32:32 + KE * NX]).then_inc(act_evac, 1)
            act.wait_ge(pe_group, GATE + 1)
            act.copy(gates[:].rearrange("p g e -> p (g e)"), ps[:, bank_of[GATE], :]).then_inc(act_evac, 1)
            for g in range(4):
                act.wait_ge(pe_group, V0 + g + 1)
                act.copy(v_all[:, 2 * g:2 * g + 2, :].rearrange("p t e -> p (t e)"), ps[:, bank_of[V0 + g], :]).then_inc(act_evac, 1)
            for n in range(4, 8):
                evac_qk(n, Q1 + n - 4, (n - 4) // 2, 1, n % 2)
                if n > 4:
                    second_part(n - 1, (n - 5) // 2, 1, (n - 1) % 2)
            second_part(7, 1, 1, 1)
            for third in range(3):
                make_bias_t(0, 2, third)

            def step(i, c):
                _, rows, probabilities, output = kind(i, c)
                for j in range(NT):
                    if probabilities:
                        first = is0(i) and c == 0
                        act.wait_ge(st_ready, at(i, c, k=NT) + j + 1)
                        if not first or j >= 4:
                            act.wait_ge(pv_done, at(i, c, k=4) + (j - 4) // 2 + 1)
                        act.activation(probs[:, j % 4, :], ps_st[j % 2].rearrange("p b n -> p (b n)"),
                                       ACT.Exp).then_inc(exp_done, 1)
                    if output and j == 1:
                        evac_o(i, c - 1)
                    if j in (3, 5) and (not isinstance(i, int) or 0 <= 4 * i + c and 4 * i + c + 3 < H):
                        make_bias_t(i, c + 3, (j - 3) // 2)
                    if rows and j == 4:
                        evac_rows(i, c + 1)

            def evac_o(i, c):
                act.wait_ge(pv_done, at(i, c, k=4) + 4)
                if not (is0(i) and c == 0):
                    act.wait_ge(ot_ready, at(i, c) + 1)
                act.copy(o_sb[:], ps_o).then_inc(o_evac, 1)

            def evac_rows(i, g):
                act.wait_ge(mT_ready, at(i, g) + 1)
                if not (is0(i) and g == 0):
                    act.wait_ge(m_stored, at(i, g, k=16))
                act.copy(m_row[:], ps_misc[0:R_M * NT, 256:256 + P]).then_inc(m_evac, 1)

            steps(act, step)
            evac_o(3, 3)

            for t in range(NT):
                act.wait_ge(attT_ready, t + 1)
                if t >= 2:
                    act.wait_ge(y1_ready, t - 1)
                act.copy(attT[:, t % 2], ps[:, t % 2, 0:E].rearrange("p (k n) -> p k n", k=KE)).then_inc(attT_evac, 1)
                if t % TC == TC - 1:
                    hf = t // TC
                    act.wait_ge(var2_done, hf + 1)
                    act.activation(std[:, TC * hf:TC * hf + TC], std[:, TC * hf:TC * hf + TC], ACT.Sqrt).then_inc(std2_done, 1)
            for g in range(4):
                hf, k = g // KE, g % KE
                act.wait_ge(xnT_ready, g + 1)
                act.activation(hT[:, k, CH * hf:CH * hf + CH], ps[:, 4 + g, :], ACT.Identity,
                               bias=modc[:, 2, k:k + 1], scale=modc[:, 3, k:k + 1]).then_inc(xnT_evac, 1)
            act.wait_ge(top_shift, 1)
            act.activation(top_e, top_w, ACT.Exp).then_inc(top_exp, 1)

            def tile(i, c):
                k = 4 * i + c if isinstance(i, int) else None
                if k is None or k + 1 < MAX_TILES:
                    act.wait_ge(xgT_ready, at(i, c + 1) + 1)
                    if k is None or k + 1 >= 2:
                        act.wait_ge(gu_ready, at(i, c + 1) - 1)
                    act.activation(xT[:, (c + 1) % 2, 0, :], ps[:, 0, 0:P], ACT.Identity,
                                   bias=modc[:, 2, 0:1], scale=modc[:, 3, 0:1]).then_inc(xT_act, 1)
                if k is None or 0 <= k - 1 < MAX_TILES:
                    act.wait_ge(hidT_ready, at(i, c - 1) + 1)
                    if k is None or k - 1 >= 2:
                        act.wait_ge(y_ready, at(i, c - 1) - 1)
                    act.copy(hidT[0:IH, (c - 1) % 2], ps[0:IH, 4 + (c - 1) % 2, 0:2 * P].rearrange("p (a n) -> p a n", a=2)).then_inc(hidT_evac, 1)
                if k is None or 0 <= k < MAX_TILES:
                    act.wait_ge(gu_ready, at(i, c) + 1)
                    if k is None or k >= 2:
                        act.wait_ge(hid_done, at(i, c) - 1)
                    act.activation(silu[:, c % 2, :], ps[:, 2 + c % 2, 0:INTER], ACT.Silu).then_inc(silu2_done, 1)

            tiles(act, tile, -1, MAX_TILES + 1)

        @block.gpsimd
        def _(pool):
            pool.dma_start(al_sign[:], a["alibi_sign"]).then_inc(sign_in, 16)
            pool.dma_start(slope_hc[:], bass.AP(a["slopes"].tensor, a["slopes"].offset, [[1, H], [0, NT], [1, 1]])).then_inc(sign_in, 16)
            pool.dma_start(slopes[:], on_partitions(a["slopes"], P)).then_inc(slopes_in, 16)
            for n, b in enumerate(("bq", "bk")):
                pool.dma_start(qk_bias[:, n, :], a[b].rearrange("(k p) -> p k", p=P), allow_slow_non_contiguous=True).then_inc(consts_in, 16)
            pool.dma_start(v_bias[:], on_partitions(a["bv"], P)).then_inc(consts_in, 16)
            pool.dma_start(o_bias[:], on_partitions(a["bo"], P)).then_inc(consts_in, 16)
            pool.dma_start(x_bias[:], on_partitions(a["expert_bias"], P)).then_inc(late_in, 16)
            pool.dma_start(triangle[:].rearrange("p a b -> p (a b)"), a["triangle"].bitcast(BF16)).then_inc(late_in, 16)
            pool.dma_start(route[:], a["route"]).then_inc(late_in, 16)
            pool.memset(v_st[:], 0.0).then_inc(v_init, 1)
            pool.wait_ge(v_init, 1)
            pool.memset(v_st[:, :, :, D:D + 1], 1.0).then_inc(v_init, 1)

            def take_slope(i, c):
                if not (isinstance(i, int) and 4 * i + c < 2):
                    pool.wait_ge(bias_d_done, at(i, c) - 1)
                pool.tensor_copy(slope_now[:, c % 2, :], slopes[:, bass.ds(at(i, c), 1)]).then_inc(slope_cp, 1)
                pool.wait_ge(slope_cp, at(i, c) + 1)

            def make_bias_p(i, c):
                s = c % 2
                w = 2 * W_DIST // 3
                pool.wait_ge(max_used, at(i, c - 1, k=16))
                settle(pool)
                pool.tensor_scalar(bias_t[:, s, w:], dist[:, w:], slope_now[:, s, :], None, ALU.mult).then_inc(bias_p_done, 1)

            def make_bias_d(i, c):
                s = c % 2
                if not isinstance(i, int) or 4 * i + c >= SLOTS:
                    pool.wait_ge(st_ready, at(i, c - 3, k=NT))
                settle(pool)
                pool.tensor_scalar(bias_d[:, c % SLOTS, :], dist[:, DIST0:DIST0 + P], slope_now[:, s, :], None,
                                   ALU.mult).then_inc(bias_d_done, 1)

            def stage_v(i, c):
                if not isinstance(i, int) or 4 * i + c >= 2:
                    pool.wait_ge(pv_done, at(i, c - 1, k=4))
                pool.tensor_copy(v_st[:, c % 2, :, 0:D], v_all[:, :, bass.ds(at(i, c, k=D), D)]).then_inc(v_staged, 1)

            chain = [0]

            def link(ins):
                chain[0] += 1
                ins.then_inc(pool_chain, 1)
                pool.wait_ge(pool_chain, chain[0])

            pool.wait_ge(al_in, 16)
            pool.wait_ge(sign_in, 32)
            link(pool.tensor_scalar(al_key[:], al_key[:], slope_hc[:, 0:1], None, ALU.mult))
            link(pool.tensor_copy(al_part[:, 0, :], al_key[:]))
            link(pool.tensor_tensor(al_rest[:], al_key[:], al_part[:, 0, :], ALU.subtract))

            def third_part(n, w, f, ch):
                pool.wait_ge(qk_second, n + 1)
                pool.tensor_tensor(qk_part[:, w, f, 2, CH * ch:CH * ch + CH], qk_r[:, n % 2],
                                   qk_part[:, w, f, 1, CH * ch:CH * ch + CH], ALU.subtract).then_inc(qk_split, 1)

            def rest_of(n, w, f, ch):
                pool.wait_ge(qk_first, n + 1)
                pool.wait_ge(qk_split, n - 1)
                pool.tensor_tensor(qk_r[:, n % 2], qk_f[:, n % 2], qk_part[:, w, f, 0, CH * ch:CH * ch + CH],
                                   ALU.subtract).then_inc(qk_rest, 1)

            for n in range(4):
                third_part(n, n // 2, 0, n % 2)
            link(pool.tensor_copy(al_part[:, 1, :], al_rest[:]))
            pool.tensor_tensor(al_part[:, 2, :], al_rest[:], al_part[:, 1, :], ALU.subtract).then_inc(al_done, 1)
            pool.wait_ge(dist_in, 16)
            pool.wait_ge(slopes_in, 16)
            for h in range(3):
                take_slope(0, h)
                make_bias_d(0, h)
            pool.wait_ge(consts_in, 16 * 4)
            for g in range(4):
                pool.wait_ge(act_evac, count(V0 + g, "act"))
                last = pool.tensor_tensor(v_all[:, 2 * g:2 * g + 2, :], v_all[:, 2 * g:2 * g + 2, :],
                                          v_bias[:].unsqueeze(1).broadcast_to([P, 2, E]), ALU.add)
                last.then_inc(v_done, 1)
            pool.wait_ge(v_init, 2)
            pool.wait_ge(v_done, 4)
            stage_v(0, 0)
            stage_v(0, 1)
            for n in range(4, 8):
                rest_of(n, (n - 4) // 2, 1, n % 2)
                if n > 4:
                    third_part(n - 1, (n - 5) // 2, 1, (n - 1) % 2)
            third_part(7, 1, 1, 1)
            pool.wait_ge(raw_mod, 1)
            pool.tensor_scalar(modc[:, 3, :], modc[:, 3, :], 1.0, None, ALU.add).then_inc(raw_mod, 1)
            pool.wait_ge(act_evac, count(GATE, "act"))
            link(pool.tensor_scalar(gsign[:], gates[:], 0.0, 2.0, ALU.is_ge, ALU.mult))
            link(pool.tensor_scalar(gsign[:], gsign[:], -1.0, None, ALU.add))
            link(pool.tensor_tensor(gabs[:], gates[:], gsign[:], ALU.mult))
            link(pool.tensor_scalar(gabs[:], gabs[:], GATE_MIN, None, ALU.max))
            link(pool.tensor_tensor(gates[:], gabs[:], gsign[:], ALU.mult))
            pool.wait_ge(act_evac, count(WO, "act"))
            pool.tensor_tensor(wo_sb[:], wT[:, 3], gates[:, 0:1, :].broadcast_to([P, KE, E]), ALU.mult).then_inc(wo_done, 1)
            link(pool.tensor_tensor(o_bias[:], o_bias[:], gates[:, 0, :], ALU.mult))
            pool.wait_ge(xh_done, NT)
            pool.tensor_tensor(x_sb[:], x_sb[:], o_bias[:].unsqueeze(1).broadcast_to([P, NT, E]), ALU.add).then_inc(xg_done, 1)

            def load_expert(i, c):
                n = at(i, c)
                for half, name in enumerate(("gate_proj", "up_proj")):
                    pool.dma_start(w_gu[:, bass.ds(n, 1), :, INTER * half:INTER * half + INTER],
                                   a[name][bass.ds(n, 1)].rearrange("x (k p) n -> p x k n", p=P)).then_inc(w_done, 16)
                pool.dma_start(w_dn[0:IH, bass.ds(n, 1), :, :],
                               a["down_proj"][bass.ds(n, 1)].rearrange("x (k p) n -> p x k n", p=IH)).then_inc(w_done, 16)

            def step(i, c):
                static = isinstance(i, int)
                h = 4 * i + c if static else None
                if not static or 1 <= h and h + 1 < H:
                    stage_v(i, c + 1)
                if not static or 0 <= h and h + 3 < H:
                    take_slope(i, c + 3)
                    make_bias_p(i, c + 3)
                    make_bias_d(i, c + 3)
                if static and h == 0:
                    for n in range(3):
                        pool.wait_ge(qk_stored[n], 16 * 6)
                    pool.wait_ge(al_stored, 16)
                    pool.wait_ge(wo_done, 1)
                    pool.wait_ge(pe_group, N_GROUPS)
                if not static or h >= 0:
                    load_expert(i, c)

            steps(pool, step)

            pool.wait_ge(tab_done, 1)
            pool.wait_ge(xn_stored, 32)

            def tile(i, c):
                k = 4 * i + c if isinstance(i, int) else None
                if k is None or 0 <= k + 3 < MAX_TILES:
                    s = (c + 3) % 4
                    if k is None or k + 3 >= 4:
                        pool.wait_ge(xgT_ready, at(i, c + 3) - 3)
                        pool.wait_ge(idx_cp, at(i, c + 3))
                    settle(pool)
                    pool.tensor_copy(idx[:, s, :].unsqueeze(1), tab_i[:, bass.ds(at(i, c + 3), 1), :]).then_inc(idx_cp, 1)
                    pool.wait_ge(idx_cp, at(i, c + 3) + 1)
                    settle(pool)
                    pool.indirect_dma_start(xg[:, s, :], None, xn_rows,
                                            bass.IndirectOffsetOnAxis(ap=idx[:, s, 0:1].bitcast(U32), axis=0),
                                            bounds_check=T - 1, oob_is_err=False).then_inc(gathered[s], 16)
                if k is None or 0 <= k - 3 < MAX_TILES:
                    s = (c - 3) % 4
                    pool.wait_ge(y_evac, at(i, c - 3) + 1)
                    settle(pool)
                    pool.tensor_copy(idx_s[:, s, :].unsqueeze(1), tab_i[:, bass.ds(at(i, c - 3), 1), 1:2]).then_inc(idx_s_cp, 1)
                    pool.wait_ge(idx_s_cp, at(i, c - 3) + 1)
                    settle(pool)
                    pool.indirect_dma_start(z_rows, bass.IndirectOffsetOnAxis(ap=idx_s[:, s, :].bitcast(U32), axis=0),
                                            y_sb[:, s, :], None, bounds_check=TOPK * T - 1,
                                            oob_is_err=False).then_inc(scattered[s], 16)

            tiles(pool, tile, -3, MAX_TILES + 3)

        @block.vector
        def _(dve):
            chain = [0]
            dve.sem_inc(ot_used, 1)
            dve.memset(table_call[:], 1.0).then_inc(preload, 1)

            def link(ins):
                chain[0] += 1
                ins.then_inc(dve_chain, 1)
                dve.wait_ge(dve_chain, chain[0])

            for t in range(NT):
                if t % 4 == 0:
                    dve.wait_ge(x_in[t // 4], 16)
                last = dve.bn_stats(stats[:, t, :], x_sb[:, t, :])
            link(last)
            for t in range(NT):
                last = dve.bn_aggr(mv[:, t, :], stats[:, t, :])
            link(last)
            dve.tensor_scalar(std[:], mv[:, :, 1], LN_EPS, None, ALU.add).then_inc(var_done, 1)
            dve.wait_ge(std_done, 1)
            link(dve.reciprocal(rstd[:], std[:]))
            for t in range(NT):
                dve.tensor_scalar(xh[:, t, :], x_sb[:, t, :], mv[:, t, 0:1], rstd[:, t:t + 1],
                                  ALU.subtract, ALU.mult).then_inc(xh_done, 1)
            for w in range(2):
                dve.wait_ge(pe_group, WQ + w + 1)
                dve.tensor_copy(wT[:, w].rearrange("p k f -> p (k f)"), ps[:, bank_of[WQ + w], :]).then_inc(dve_evac, 1)
            dve.wait_ge(sign_in, 32)
            link(dve.tensor_scalar(al_sign[:], al_sign[:], slope_hc[:, 0:1], None, ALU.mult))
            link(dve.tensor_copy(sign_part[:, 0, :], al_sign[:]))
            link(dve.tensor_tensor(al_sign[:], al_sign[:], sign_part[:, 0, :], ALU.subtract))
            link(dve.tensor_copy(sign_part[:, 1, :], al_sign[:]))
            link(dve.tensor_tensor(sign_part[:, 2, :], al_sign[:], sign_part[:, 1, :], ALU.subtract))
            dve.tensor_copy(al_part[:, 3:6, :].rearrange("p g (j n) -> p g j n", n=P),
                            sign_part[:].unsqueeze(3).broadcast_to([P, 3, NT, P])).then_inc(sign_done, 1)
            dve.wait_ge(pe_group, MODA + 1)
            dve.tensor_copy(modc[:, 0:2, :].rearrange("p m k -> p (m k)"), ps[:, bank_of[MODA], 0:2 * KE]).then_inc(dve_evac, 1)
            dve.wait_ge(dve_evac, MODA + 1)
            dve.tensor_scalar(modc[:, 1, :], modc[:, 1, :], 1.0, None, ALU.add).then_inc(mod_done, 1)
            dve.wait_ge(mod_done, 1)
            for ch in range(NCH):
                g = XT + KE * ch + 1
                dve.wait_ge(pe_group, g + 1)
                dve.tensor_scalar(hT[:, 1, CH * ch:CH * ch + CH], ps[:, bank_of[g], :], modc[:, 1, 1:2], modc[:, 0, 1:2],
                                  ALU.mult, ALU.add).then_inc(dve_evac, 1)
            dve.tensor_copy(cond_bc[:], cond_silu[:].unsqueeze(2).broadcast_to([P, KE, P])).then_inc(bc_done, 1)
            dve.tensor_copy(ident_b[:], ident[:])
            dve.wait_ge(consts_in, 16 * 4)
            dve.tensor_scalar(q_bias_s[:], qk_bias[:, 0, :], D ** -0.5, None, ALU.mult).then_inc(q_bias_done, 1)
            for n in range(4):
                w, ch = n // 2, n % 2
                dve.wait_ge(qk_first, n + 1)
                if n >= 2:
                    dve.wait_ge(qk_split, n - 1)
                dve.tensor_tensor(qk_r[:, n % 2], qk_f[:, n % 2], qk_part[:, w, 0, 0, CH * ch:CH * ch + CH],
                                  ALU.subtract).then_inc(qk_rest, 1)
                dve.wait_ge(qk_rest, n + 1)
                dve.tensor_copy(qk_part[:, w, 0, 1, CH * ch:CH * ch + CH], qk_r[:, n % 2]).then_inc(qk_second, 1)

            def step(i, c):
                maxima, rows, _, output = kind(i, c)
                g = c + 2
                for q in range(NT):
                    if maxima:
                        if q == 0:
                            dve.wait_ge(bias_t_done, at(i, g, k=2) + 2)
                            if is0(i):
                                dve.wait_ge(bias_a_done, g + 1)
                            else:
                                dve.wait_ge(bias_p_done, at(i, g) - 2)
                        for half in range(NCH):
                            n = 2 * q + half
                            dve.wait_ge(max_ready, at(i, g, k=16) + n + 1)
                            settle(dve)
                            off = DIST0 + CH * half - P * q
                            dve.tensor_tensor_reduce(
                                junk[:, half, :], ps_max[half], bias_t[:, g % 2, off:off + CH], 1.0, -3.0e38,
                                ALU.add, ALU.max, mx[:, g % 2, q, half:half + 1]).then_inc(max_used, 1)
                            if rows and n == 0:
                                total_max(i, c + 1)
                            elif rows and n < 5:
                                split_rows(i, c + 1, n - 1)
                    elif rows and q == 0:
                        total_max(i, c + 1)
                        for n in range(4):
                            split_rows(i, c + 1, n)
                    if output and q == 6:
                        normalise(i, c - 1)

            def total_max(i, g):
                dve.wait_ge(max_used, at(i, g, k=16) + 16)
                dve.tensor_reduce(negm[:, g % 2, :], mx[:, g % 2], AX_X, ALU.max, negate=True).then_inc(negm_done, 1)

            def split_rows(i, g, n):
                full, rest, part = negm[:, g % 2, :], m_rest[:], m_part[:, g % 2]
                if n == 0:
                    dve.wait_ge(negm_done, at(i, g) + 1)
                    settle(dve)
                else:
                    dve.wait_ge(m_chain, at(i, g, k=4) + n)
                (dve.tensor_copy(part[:, 0, :], full) if n == 0 else
                 dve.tensor_tensor(rest, full, part[:, 0, :], ALU.subtract) if n == 1 else
                 dve.tensor_copy(part[:, 1, :], rest) if n == 2 else
                 dve.tensor_tensor(part[:, 2, :], rest, part[:, 1, :], ALU.subtract)).then_inc(m_chain, 1)

            def normalise(i, c):
                dve.wait_ge(ot_ready, at(i, c) + 2)
                if not (is0(i) and c == 0):
                    dve.wait_ge(ot_used, at(i, c) + 1)
                dve.reciprocal(rsum[:], ps_ot[:, :, :, D]).then_inc(ot_recip, 1)
                dve.wait_ge(ot_recip, at(i, c) + 1)
                dve.tensor_tensor(attn[:, :, :, bass.ds(at(i, c, k=D), D)].rearrange("p c t d -> p t c d"),
                                  ps_ot[:, :, :, 0:D], rsum[:].unsqueeze(3).broadcast_to([P, TC, NCH, D]),
                                  ALU.mult).then_inc(ot_used, 1)

            steps(dve, step)
            normalise(3, 3)

            for t in range(NT):
                hf = t // TC
                dve.wait_ge(y1_ready, t + 1)
                dve.wait_ge(xg_done, 1)
                dve.tensor_tensor(x_sb[:, t, :], ps[:, 2 + t % 2, 0:E], x_sb[:, t, :], ALU.add).then_inc(x2_done, 1)
                dve.wait_ge(x2_done, t + 1)
                last = dve.bn_stats(stats[:, t, :], x_sb[:, t, :])
                if t % TC == TC - 1:
                    link(last)
                    for n in range(TC * hf, TC * hf + TC):
                        last = dve.bn_aggr(mv[:, n, :], stats[:, n, :])
                    link(last)
                    dve.tensor_scalar(std[:, TC * hf:TC * hf + TC], mv[:, TC * hf:TC * hf + TC, 1], LN_EPS, None,
                                      ALU.add).then_inc(var2_done, 1)
                    dve.wait_ge(std2_done, hf + 1)
                    link(dve.reciprocal(rstd[:, TC * hf:TC * hf + TC], std[:, TC * hf:TC * hf + TC]))
                    for n in range(TC * hf, TC * hf + TC):
                        dve.tensor_scalar(xn[:, n, :], x_sb[:, n, :], mv[:, n, 0:1], rstd[:, n:n + 1],
                                          ALU.subtract, ALU.mult).then_inc(xn_done, 1)
            dve.wait_ge(late_in, 16 * 3)
            for hf in range(NCH):
                dve.wait_ge(logits_ready, hf + 1)
                link(dve.tensor_tensor(logits[:, TC * hf:TC * hf + TC, :],
                                       ps[:, hf, 0:TC * NX].rearrange("p (t x) -> p t x", t=TC),
                                       x_bias[:].unsqueeze(1).broadcast_to([P, TC, NX]), ALU.add))
                for t in range(TC * hf, TC * hf + TC):
                    last = dve.max(top8[:, t, :], logits[:, t, :])
                link(last)
                for t in range(TC * hf, TC * hf + TC):
                    last = dve.max_index(top8_i[:, t, :], top8[:, t, :], logits[:, t, :])
            link(last)
            col = [NCH * VW]

            def consts(n):
                col[0] += n
                return route[:, col[0] - n:col[0]]
            c_experts, c_sizes, c_tiles, c_slots, c_rows = (consts(n) for n in (NX, NT, NTAB, P, NT * TOPK))
            link(dve.tensor_copy(top_i, top8_i[:, :, 0:TOPK]))
            link(dve.tensor_tensor(hot, top_i.unsqueeze(3).broadcast_to([P, NT, TOPK, NX]),
                                   c_experts.unsqueeze(1).unsqueeze(1).broadcast_to([P, NT, TOPK, NX]), ALU.is_equal))
            link(dve.tensor_reduce(before, hot.rearrange("p t j x -> p t x j"), AX_X, ALU.add))
            dve.tensor_copy(mask, before).then_inc(mask_done, 1)
            dve.tensor_tensor(top_w, top8[:, :, 0:TOPK], top8[:, :, 0:1].broadcast_to([P, NT, TOPK]),
                              ALU.subtract).then_inc(top_shift, 1)
            dve.wait_ge(top_exp, 1)
            link(dve.tensor_reduce(top_s, top_e, AX_X, ALU.add))
            link(dve.reciprocal(top_s, top_s))
            dve.tensor_tensor(top_w, top_e, top_s.unsqueeze(2).broadcast_to([P, NT, TOPK]), ALU.mult)
            dve.wait_ge(before_ready, 1)
            counts = ps[:, 3, 0:NX]
            link(dve.tensor_tensor(over, counts.unsqueeze(2).broadcast_to([P, NX, NT]),
                                   c_sizes.unsqueeze(1).broadcast_to([P, NX, NT]), ALU.is_gt))
            link(dve.tensor_reduce(n_tiles, over, AX_X, ALU.add))
            dve.memset(starts, 1.0)
            link(dve.tensor_copy(before, ps[:, 2, 0:P].rearrange("p (t x) -> p t x", t=NT)))
            link(dve.tensor_tensor_scan(ends, starts, n_tiles, 0.0, ALU.mult, ALU.add))
            link(dve.tensor_tensor(starts, ends, n_tiles, ALU.subtract))
            link(dve.tensor_scalar(starts, starts, float(P), None, ALU.mult))
            link(dve.tensor_tensor(before, before, starts.unsqueeze(1).broadcast_to([P, NT, NX]), ALU.add))
            link(dve.tensor_tensor(hot_a, hot, before.unsqueeze(2).broadcast_to([P, NT, TOPK, NX]), ALU.mult))
            link(dve.tensor_reduce(pos, hot_a, AX_X, ALU.add))
            link(dve.tensor_copy(pos_i, pos))
            dve.tensor_scalar(hi_i, pos_i, 7, None, ALU.logical_shift_right)
            link(dve.tensor_scalar(lo_i, pos_i, P - 1, None, ALU.bitwise_and))
            dve.tensor_copy(hi_f, hi_i)
            link(dve.tensor_copy(lo_f, lo_i))
            for n in range(NT * TOPK):
                t, j = n // TOPK, n % TOPK
                if n >= 2:
                    dve.wait_ge(hot_used, n - 1)
                dve.tensor_scalar(hot_lo[:, n % 2, :], c_slots, lo_f[:, t, j:j + 1], None, ALU.is_equal).then_inc(hot_done, 1)
                dve.tensor_scalar(hot_hi[:, n % 2, :], c_tiles, hi_f[:, t, j:j + 1], c_rows[:, n:n + 1],
                                  ALU.is_equal, ALU.mult).then_inc(hot_done, 1)
            link(dve.tensor_tensor(ended.rearrange("p (k x) -> p k x", k=NTAB), ends[0:1].unsqueeze(1).broadcast_to([1, NTAB, NX]),
                                   c_tiles[0:1].unsqueeze(2).broadcast_to([1, NTAB, NX]), ALU.is_le))
            link(dve.tensor_reduce(exp_f, ended.rearrange("p (k x) -> p k x", k=NTAB), AX_X, ALU.add))
            link(dve.tensor_scalar(exp_f, exp_f, float(NX - 1), None, ALU.min))
            link(dve.tensor_copy(exp_i, exp_f))
            dve.wait_ge(hot_used, NT * TOPK)
            link(dve.tensor_copy(tab_f, ps[:, 4, 0:NTAB]))
            link(dve.tensor_scalar(tab_e, tab_f, 0.0, 2.0 * TOPK * T, ALU.is_equal, ALU.mult))
            link(dve.scalar_tensor_tensor(out=tab_f, in0=tab_f, scalar=-1.0, in1=tab_e, op0=ALU.add, op1=ALU.add))
            link(dve.tensor_copy(tab_i[:, :, 1], tab_f))
            dve.tensor_scalar(tab_i[:, :, 0], tab_i[:, :, 1], T - 1, None, ALU.bitwise_and).then_inc(tab_done, 1)

            def tile(i, c):
                k = 4 * i + c if isinstance(i, int) else None
                if k is None or k + 1 < MAX_TILES:
                    dve.wait_ge(xgT_ready, at(i, c + 1) + 1)
                    if k is None or k + 1 >= 2:
                        dve.wait_ge(gu_ready, at(i, c + 1) - 1)
                    dve.tensor_scalar(xT[:, (c + 1) % 2, 1, :], ps[:, 1, 0:P], modc[:, 3, 1:2], modc[:, 2, 1:2],
                                      ALU.mult, ALU.add).then_inc(xT_dve, 1)
                if k is None or 0 <= k < MAX_TILES:
                    dve.wait_ge(silu2_done, at(i, c) + 1)
                    if k is None or k >= 2:
                        dve.wait_ge(hidT_ready, at(i, c) - 1)
                    dve.tensor_tensor(hid[:, c % 2, :], silu[:, c % 2, :], ps[:, 2 + c % 2, INTER:2 * INTER],
                                      ALU.mult).then_inc(hid_done, 1)
                if k is None or 0 <= k - 2 < MAX_TILES:
                    s = (c - 2) % 4
                    dve.wait_ge(y_ready, at(i, c - 2) + 1)
                    if k is None or k - 2 >= 4:
                        dve.wait_ge(scattered[s], (i + (c - 2) // 4) * 16)
                    dve.tensor_tensor(y_sb[:, s, :], ps[:, 6 + c % 2, 0:E], gates[:, 1, :], ALU.mult).then_inc(y_evac, 1)

            tiles(dve, tile, -1, MAX_TILES + 2)

            for t in range(NT):
                s = t % 6
                dve.wait_ge(z_in[s], 16 * (t // 6 + 1))
                for j in range(TOPK):
                    ins = dve.scalar_tensor_tensor(out=x_sb[:, t, :], in0=z_sb[s][:, j, :], scalar=top_w[:, t, j:j + 1],
                                                   in1=x_sb[:, t, :], op0=ALU.mult, op1=ALU.add)
                    if j < TOPK - 1:
                        link(ins)
                ins.then_inc(acc_done, 1)

        @block.tensor
        def _(pe):
            def group(g):
                b = bank_of[g]
                if b in bank_of[:g]:
                    wait_emptied(pe, max(n for n in range(g) if bank_of[n] == b))
                return ps[:, b, :]

            def transpose_w(w, g):
                pe.wait_ge(w_in[w], 16)
                b = group(g)
                for k in range(KE):
                    for f in range(KE):
                        last = pe.transpose(b[:, k * E + f * P:k * E + f * P + P],
                                            w_raw[:, w, f, k * P:k * P + P], ident[:])
                last.then_inc(pe_group, 1)

            def modulations(b, first, n):
                for m in range(KE * n):
                    for k in range(KE):
                        o = (KE * first + m) * P
                        last = pe.matmul(b[:, m:m + 1], wmod[:, k, o:o + P], cond_silu[:, k:k + 1],
                                         start=(k == 0), stop=(k == KE - 1))
                return last

            def project_t(g, w, f, ch, k):
                b = group(g) if k == 0 else ps[:, bank_of[g], :]
                ins = pe.matmul(b, wT[:, w, k, f * P:f * P + P], hT[:, k, CH * ch:CH * ch + CH],
                                start=(k == 0), stop=(k == KE - 1))
                if k == KE - 1:
                    ins.then_inc(pe_group, 1)

            def later_group(n):
                if n == 0:
                    pe.wait_ge(wmod_in[1], 16)
                    b = group(MODB)
                    modulations(b, 3, 2)
                    pe.wait_ge(router_in, 16)
                    for k in range(KE):
                        last = pe.transpose(b[:, 32 + k * NX:32 + k * NX + NX], rw_raw[:, k * P:k * P + P], ident[0:NX, 0:NX])
                    last.then_inc(pe_group, 1)
                elif n == 1:
                    pe.wait_ge(bc_done, 1)
                    b = group(GATE)
                    for n, m in enumerate((2, 5)):
                        for k in range(KE):
                            last = pe.matmul(b[:, n * E:n * E + E], cond_bc[:, k, :], wmod[:, k, m * E:m * E + E],
                                             start=(k == 0), stop=(k == KE - 1))
                    last.then_inc(pe_group, 1)
                else:
                    pe.wait_ge(act_evac, count(WV, "act"))
                    b = group(V0 + n - 2)
                    for half in range(2):
                        t = 2 * (n - 2) + half
                        for k in range(KE):
                            last = pe.matmul(b[:, half * E:half * E + E], hT[:, k, t * P:t * P + P], wT[:, 2, k, :],
                                             start=(k == 0), stop=(k == KE - 1))
                    last.then_inc(pe_group, 1)

            pe.wait_ge(ident_in, 16)
            for w in range(2):
                transpose_w(w, WQ + w)
            pe.wait_ge(wmod_in[0], 16)
            pe.wait_ge(silu_done, 1)
            modulations(group(MODA), 0, 2).then_inc(pe_group, 1)
            for n in range(4):
                ch, k = n // KE, n % KE
                pe.wait_ge(xh_done, TC * ch + TC)
                b = group(XT + n)
                for t in range(TC):
                    last = pe.transpose(b[:, t * P:t * P + P], xh[:, TC * ch + t, k * P:k * P + P], ident[:])
                last.then_inc(pe_group, 1)
            for g0, w in ((Q0, 0), (K0, 1)):
                for ch in range(NCH):
                    pe.wait_ge(act_evac, count(XT + KE * ch, "act"))
                    pe.wait_ge(dve_evac, count(XT + KE * ch + 1, "dve"))
                    for k in range(KE):
                        project_t(g0 + ch, w, 0, ch, k)
            for w in range(2, 4):
                transpose_w(w, WV - 2 + w)
            for n in range(6):
                later_group(n)

            def step(i, c):
                maxima, rows, probabilities, output = kind(i, c)
                if is0(i) and c == 0:
                    pe.wait_ge(act_evac, count(N_GROUPS - 1, "act"))
                    pe.wait_ge(rows_in, 16 * 2)
                    pe.wait_ge(late_in, 16 * 3)
                for j in range(NT):
                    if maxima:
                        scores(i, c + 2, j, 0)
                    if is0(i) and c == -2:
                        n = j // KE
                        project_t(Q1 + n, n // NCH, 1, n % NCH, j % KE)
                    if probabilities:
                        scores_t(i, c, j)
                    if maxima:
                        scores(i, c + 2, j, 1)
                    if probabilities:
                        own_tile(i, c, j)
                        if j % 2 == 1 and j >= 3:
                            sum_pv(i, c, (j - 3) // 2)
                    if output and j == 1:
                        sum_pv(i, c - 1, 3)
                    if rows and j == 3:
                        rows_t(i, c + 1)
                    if output and j == 5:
                        merge_o(i, c - 1)

            def loaded(i, c):
                pe.wait_ge(st_in[c % SLOTS], 48 * (i + c // SLOTS) + 48)

            def scores(i, c, q, half):
                s = c % SLOTS
                if q == 0 and half == 0:
                    loaded(i, c)
                n = 2 * q + half
                if n >= 2 or not (is0(i) and c == 0):
                    pe.wait_ge(max_used, at(i, c, k=16) + n - 1)
                pe.matmul(ps_max[half], q_st[0:R_QK, s, q * P:q * P + P],
                          k_st[0:R_QK, 0, s, CH * half:CH * half + CH], start=True, stop=True).then_inc(max_ready, 1)

            def scores_t(i, c, j):
                s = c % SLOTS
                if j == 0:
                    pe.wait_ge(m_in, at(i, c, k=16) + 16)
                    pe.wait_ge(al_ld[s], 32 * (i + c // SLOTS) + 32)
                    pe.wait_ge(bias_d_done, at(i, c) + 1)
                if j >= 2 or not (is0(i) and c == 0):
                    pe.wait_ge(exp_done, at(i, c, k=NT) + j - 1)
                for ch in range(NCH):
                    pe.matmul(ps_st[j % 2][:, ch, :], k_st[0:R_ALL, ch, s, j * P:j * P + P],
                              q_st[0:R_ALL, s, CH * ch:CH * ch + CH], start=True, stop=j // TC != ch)

            def own_tile(i, c, j):
                t = j % TC
                pe.matmul(ps_st[j % 2][:, j // TC, t * P:t * P + P], ident[:], bias_d[:, c % SLOTS, :],
                          start=False, stop=True).then_inc(st_ready, 1)

            def sum_pv(i, c, pair):
                if pair == 0:
                    pe.wait_ge(v_staged, at(i, c) + 1)
                    if not (is0(i) and c == 0):
                        pe.wait_ge(o_evac, at(i, c))
                pe.wait_ge(exp_done, at(i, c, k=NT) + 2 * pair + 2)
                for n in range(2):
                    j = 2 * pair + n
                    for ch in range(NCH):
                        r = 32 * (2 * n + ch)
                        last = pe.matmul(ps_o[r:r + 32], v_st[:, c % 2, j, :], probs[:, j % 4, CH * ch:CH * ch + CH],
                                         start=(pair == 0), stop=(pair == 3))
                last.then_inc(pv_done, 1)

            def rows_t(i, g):
                pe.wait_ge(m_chain, at(i, g, k=4) + 4)
                if not (is0(i) and g < 2):
                    pe.wait_ge(ot_used, at(i, g) - 1)
                if is0(i) and g == 0:
                    pe.wait_ge(act_evac, count(Q0, "act"))
                pe.matmul(ps_misc[0:R_M * NT, 256:256 + P], m_part[:, g % 2].rearrange("p r i -> p (r i)"), ident_b[:],
                          start=True, stop=True).then_inc(mT_ready, 1)

            def merge_o(i, c):
                pe.wait_ge(o_evac, at(i, c) + 1)
                if not (is0(i) and c == 0):
                    pe.wait_ge(ot_used, at(i, c) + 1)
                nr = c + 2
                if not (isinstance(i, int) and 4 * i + nr >= H):
                    pe.wait_ge(m_evac, at(i, nr) + 1)
                for t in range(TC):
                    last = pe.matmul(ps_ot[:, t].rearrange("p c d -> p (c d)"), o_sb[:, t * P:t * P + P], merge[:],
                                     start=True, stop=True)
                last.then_inc(ot_ready, 1)

            pe.sem_inc(ot_ready, 1)
            steps(pe, step)
            sum_pv(3, 3, 3)
            merge_o(3, 3)

            pe.wait_ge(wo_done, 1)
            for t in range(NT + 1):
                if t < NT:
                    pe.wait_ge(ot_used, H + 1)
                    if t >= 2:
                        pe.wait_ge(attT_evac, t - 1)
                    for k in range(KE):
                        last = pe.transpose(ps[:, t % 2, k * P:k * P + P], attn[:, t // TC, t % TC, k * P:k * P + P], ident[:])
                    last.then_inc(attT_ready, 1)
                if t >= 1:
                    n = t - 1
                    pe.wait_ge(attT_evac, n + 1)
                    if n >= 2:
                        pe.wait_ge(x2_done, n - 1)
                    for k in range(KE):
                        last = pe.matmul(ps[:, 2 + n % 2, 0:E], attT[:, n % 2, k, :], wo_sb[:, k, :],
                                         start=(k == 0), stop=(k == KE - 1))
                    last.then_inc(y1_ready, 1)
            for g in range(4):
                hf, k = g // KE, g % KE
                pe.wait_ge(xn_done, TC * hf + TC)
                for t in range(TC):
                    last = pe.transpose(ps[:, 4 + g, t * P:t * P + P], xn[:, TC * hf + t, k * P:k * P + P], ident[:])
                last.then_inc(xnT_ready, 1)
            for hf in range(NCH):
                pe.wait_ge(xnT_evac, KE * hf + KE)
                for t in range(TC):
                    for k in range(KE):
                        last = pe.matmul(ps[:, hf, t * NX:t * NX + NX], hT[:, k, (TC * hf + t) * P:(TC * hf + t) * P + P],
                                         rwT[:, k, :], start=(k == 0), stop=(k == KE - 1))
                last.then_inc(logits_ready, 1)
            pe.wait_ge(mask_done, 1)
            flat_mask = mask.rearrange("p t x -> p (t x)")
            for n in range(1, NT):
                pe.matmul(ps[:, 2, n * NX:P], triangle[:, 1, :], flat_mask[:, 0:P - n * NX], start=(n == 1), stop=False,
                          skip_group_check=True)
            pe.matmul(ps[:, 2, 0:P], triangle[:, 0, :], flat_mask, start=False, stop=True, skip_group_check=True)
            for n in range(NT):
                last = pe.matmul(ps[:, 3, 0:NX], triangle[:, 1, :], mask[:, n, :], start=(n == 0), stop=(n == NT - 1))
            last.then_inc(before_ready, 1)
            for n in range(NT * TOPK):
                pe.wait_ge(hot_done, 2 * n + 2)
                pe.matmul(ps[:, 4, 0:NTAB], hot_lo[:, n % 2, :], hot_hi[:, n % 2, :], start=(n == 0),
                          stop=(n == NT * TOPK - 1)).then_inc(hot_used, 1)
            pe.wait_ge(tab_done, 1)
            pe.wait_ge(w_done, 16 * 3 * NX)

            def expert(i, c):
                return pe.value_load(exp_i[0:1, bass.ds(at(i, c), 1)], min_val=0, max_val=NX - 1)

            def tile(i, c):
                k = 4 * i + c if isinstance(i, int) else None
                if k is None or 0 <= k < MAX_TILES:
                    e = expert(i, c)
                if k is None or k + 1 < MAX_TILES:
                    s = (c + 1) % 4
                    pe.wait_ge(gathered[s], (i + (c + 1) // 4) * 16 + 16)
                    if k is None or k + 1 >= 1:
                        pe.wait_ge(xT_act, at(i, c + 1))
                        pe.wait_ge(xT_dve, at(i, c + 1))
                    for kk in range(KE):
                        last = pe.transpose(ps[:, kk, 0:P], xg[:, s, kk * P:kk * P + P], ident[:])
                    last.then_inc(xgT_ready, 1)
                if k is None or 0 <= k - 1 < MAX_TILES:
                    pe.wait_ge(hid_done, at(i, c - 1) + 1)
                    if k is None or k - 1 >= 2:
                        pe.wait_ge(hidT_evac, at(i, c - 1) - 1)
                    for kk in range(2):
                        last = pe.transpose(ps[0:IH, 4 + (c - 1) % 2, kk * P:kk * P + P],
                                            hid[:, (c - 1) % 2, kk * IH:kk * IH + IH], ident[:])
                    last.then_inc(hidT_ready, 1)
                if k is None or 0 <= k < MAX_TILES:
                    pe.wait_ge(xT_act, at(i, c) + 1)
                    pe.wait_ge(xT_dve, at(i, c) + 1)
                    if k is None or k >= 2:
                        pe.wait_ge(hid_done, at(i, c) - 1)
                    for kk in range(KE):
                        last = pe.matmul(ps[:, 2 + c % 2, 0:2 * INTER], xT[:, c % 2, kk, :],
                                         w_gu[:, bass.ds(e, 1), kk, :].rearrange("p x n -> p (x n)"),
                                         start=(kk == 0), stop=(kk == KE - 1))
                    last.then_inc(gu_ready, 1)
                if k is None or 0 <= k - 2 < MAX_TILES:
                    e2 = expert(i, c - 2)
                    pe.wait_ge(hidT_evac, at(i, c - 2) + 1)
                    if k is None or k - 2 >= 2:
                        pe.wait_ge(y_evac, at(i, c - 2) - 1)
                    for kk in range(2):
                        last = pe.matmul(ps[:, 6 + c % 2, 0:E], hidT[0:IH, c % 2, kk, :],
                                         w_dn[0:IH, bass.ds(e2, 1), kk, :].rearrange("p x n -> p (x n)"),
                                         start=(kk == 0), stop=(kk == 1))
                    last.then_inc(y_ready, 1)

            tiles(pe, tile, -1, MAX_TILES + 2)


_INPUTS = {"x": "L0_attn_x", "Wq": "L0_attn_Wq", "Wk": "L0_attn_Wk", "Wv": "L0_attn_Wv", "Wo": "L0_attn_Wo",
           "bq": "L0_attn_bq", "bk": "L0_attn_bk", "bv": "L0_attn_bv", "bo": "L0_attn_bo",
           "slopes": "L0_attn_slopes", "router_w": "L0_ffn_router_w", "expert_bias": "L0_ffn_expert_bias",
           "gate_proj": "L0_ffn_gate_proj", "up_proj": "L0_ffn_up_proj", "down_proj": "L0_ffn_down_proj",
           "c": "L0_c", "wmod": "L0_wmod"}


def kernel(**inputs):
    import concourse.bacc as bacc
    from concourse.bass_utils import run_bass_kernel_spmd

    nc = bacc.Bacc("TRN2", target_bir_lowering=False, num_devices=1)
    arrays = {short: np.ascontiguousarray(inputs[name]) for short, name in _INPUTS.items()}
    arrays["x"] = arrays["x"].reshape(T, E)
    arrays.update(host_constants())
    aps = {n: nc.dram_tensor(f"in_{n}", v.shape, mybir.dt.from_np(v.dtype), kind="ExternalInput").ap()
           for n, v in arrays.items()}
    out = nc.dram_tensor("out_0", (T, E), F32, kind="ExternalOutput").ap()
    adaln_block(nc, aps, out)
    r = run_bass_kernel_spmd(nc, [{f"in_{n}": v for n, v in arrays.items()}], core_ids=[0])
    return r.results[0]["out_0"].reshape(1, T, E)
```

```python
from contextlib import ExitStack

import numpy as np

import concourse.bass as bass
from concourse import mybir

F32 = mybir.dt.float32
BF16 = mybir.dt.bfloat16
U32 = mybir.dt.uint32
I32 = mybir.dt.int32
ALU = mybir.AluOpType
ACT = mybir.ActivationFunctionType
AX_X = mybir.AxisListType.X

P = 128
T = 1024
NT = T // P
E = 256
KE = E // P
H = 16
D = E // H
VW = D + 1
CH = 512
NCH = T // CH
TC = CH // P
LN_EPS = 1e-5
GATE_MIN = 0.25
HT = P // D

Q_PARTS = (0, 1, 2, 0, 1, 0)
K_PARTS = (0, 0, 0, 1, 1, 2)
R_QK = 6 * D
R_AL = 6 * TC
R_M = 3
R_ALL = R_QK + R_AL + R_M

W_DIST = T + (NT - 1) * P
DIST0 = (NT - 1) * P

SLOTS = 4
NX = 16
TOPK = 4
INTER = 224
IH = INTER // 2
WARM_LOAD = 14
WARM_GATHER = 10
NTAB = 48
OWN_DVE = (1, 3, 5, 7)
SUM_DVE = (0, 1, 3, 4, 6, 7)
SUM_POOL = (2, 5)
MAX_TILES = (T * TOPK + NX * (P - 1)) // P


def host_constants():
    def bf16_bits(a):
        return (np.ascontiguousarray(a, np.float32).view(np.uint32) >> 16).astype(np.uint16)

    i = np.arange(P)[:, None]
    dist = -np.abs(i - (np.arange(W_DIST)[None, :] - DIST0)).astype(np.float32)
    c = (np.arange(P) % NT)[:, None]
    j = np.arange(T)[None, :]
    same = (j // P) == c
    alibi_key = np.where(same, 0, -np.abs(j - P * c)).astype(np.float32)
    alibi_sign = np.sign(np.arange(NT)[None, :] - c).astype(np.float32)
    t = np.arange(T)
    rows = [((t // P) % TC == k) * 1.0 for k in range(TC)]
    qrows = np.stack(rows * 3 + [r * (t % P) for r in rows] * 3)
    merge = np.zeros((P, NCH * VW), np.float32)
    for g in range(4):
        for d in range(VW):
            merge[32 * g + d, (g % NCH) * VW + d] = 1.0
    return {
        "ident": np.eye(P, dtype=np.float32),
        "dist": dist,
        "alibi_key": alibi_key,
        "alibi_sign": alibi_sign,
        "query_rows": bf16_bits(qrows),
        "one_rows": bf16_bits(np.ones((R_M, T))),
        "triangle": bf16_bits(np.concatenate([np.triu(np.ones((P, P)), 1), np.ones((P, P))], 1)),
        "route": np.concatenate([merge] + [np.broadcast_to(r, (P, r.shape[-1])) for r in (
            np.arange(NX), P * np.arange(NT), np.arange(NTAB), np.arange(P),
            np.arange(1, P + 1)[:, None], (NT * np.arange(TOPK)[None, :] + np.arange(NT)[:, None]).reshape(-1))
            for r in [np.asarray(r).reshape(-1 if np.ndim(r) == 1 else P, *([] if np.ndim(r) == 1 else [-1]))]],
            1).astype(np.float32),
    }


def on_partitions(ap, n):
    return bass.AP(ap.tensor, ap.offset, [[0, n]] + [list(a) for a in ap.ap])


def adaln_block(nc, a, out):
    with ExitStack() as ctx:
        def sb(name, shape, dt=F32):
            return ctx.enter_context(nc.sbuf_tensor(name, shape, dt))

        def sem(name):
            return ctx.enter_context(nc.semaphore(name))

        def dram(name, shape, dt):
            return nc.dram_tensor(name, shape, dt, kind="Internal").ap()

        q_rows = dram("q_rows", [6, H * D, T], BF16)
        k_rows = dram("k_rows", [6, H * D, T], BF16)
        al_rows = dram("al_rows", [6, H * NT, T], BF16)
        m_rows = dram("m_rows", [H, R_M, NT, P], BF16)
        xn_rows = dram("xn_rows", [T, E], F32)
        z_rows = dram("z_rows", [TOPK * T, E], F32)

        w_gu = sb("w_gu", [P, NX, KE, 2 * INTER])
        w_dn = sb("w_dn", [P, NX, 2, E])
        flat_gu = w_gu[:].rearrange("p x k n -> p (x k n)")
        flat_dn = w_dn[:].rearrange("p x k n -> p (x k n)")

        def carver(flat):
            used = [0]

            def carve(shape, dt=F32):
                n = int(np.prod(shape[1:])) * (1 if dt in (F32, U32, I32) else 2) // (1 if dt in (F32, U32, I32) else 4)
                v = flat[0:shape[0], used[0]:used[0] + n]
                used[0] += n
                assert used[0] <= flat.shape[1]
                v = v if dt == F32 else v.bitcast(dt)
                names = "abcdef"[:len(shape) - 1]
                return v.rearrange(f"p ({' '.join(names)}) -> p {' '.join(names)}",
                                   **{c: m for c, m in zip(names[1:], shape[2:])}) if len(shape) > 2 else v
            return carve

        early = carver(flat_gu)
        qk_part = early([P, 2, KE, 3, T], BF16)
        wmod = early([P, KE, 6 * E])
        al_part = early([P, 6, T], BF16)
        xh = early([P, NT, E])
        early = carver(flat_dn)
        w_raw = early([P, 4, KE, E])
        wT = early([P, 4, KE, E])
        al_key = early([P, T])
        gsign = al_key[:, 0:2 * E].rearrange("p (g e) -> p g e", g=2)
        gabs = al_key[:, 2 * E:].rearrange("p (g e) -> p g e", g=2)
        qk_f = early([P, 2, CH])
        qk_r = early([P, 2, CH])
        rw_raw = early([NX, E])

        x_sb = sb("x_sb", [P, NT, E])
        hT = sb("hT", [P, KE, T])
        wo_sb = sb("wo_sb", [P, KE, E])
        cond = sb("cond", [P, KE])
        cond_silu = sb("cond_silu", [P, KE])
        cond_bc = sb("cond_bc", [P, KE, P])
        modc = sb("modc", [P, 4, KE])
        gates = sb("gates", [P, 2, E])
        qk_bias = sb("qk_bias", [P, 2, KE])
        q_bias_s = sb("q_bias_s", [P, KE])
        v_bias = sb("v_bias", [P, E])
        o_bias = sb("o_bias", [P, E])
        x_bias = sb("x_bias", [P, NX])
        rwT = sb("rwT", [P, KE, NX])
        slopes = sb("slopes", [P, H])
        slope_hc = sb("slope_hc", [P, 1])
        ident = sb("ident", [P, P])
        triangle = sb("triangle", [P, 2, P], BF16)
        route = sb("route", [P, NCH * VW + NX + NT + NTAB + P + 1 + NT * TOPK])
        merge = route[:, 0:NCH * VW]
        dist = sb("dist", [P, W_DIST])
        table_call = sb("table_call", [1, 8])
        stats = sb("stats", [P, NT, 6])
        mv = sb("mv", [P, NT, 2])
        std = sb("std", [P, NT])
        rstd = sb("rstd", [P, NT])
        al_sign = sb("al_sign", [P, NT])
        sign_part = sb("sign_part", [P, 3, NT], BF16)
        v_all = sb("v_all", [P, NT, E])
        q_st = sb("q_st", [P, SLOTS, T], BF16)
        k_st = sb("k_st", [P, NCH, SLOTS, T], BF16)
        v_st = sb("v_st", [P, 2, NT, 32])
        bias_t = sb("bias_t", [P, 2, W_DIST])
        bias_d = sb("bias_d", [P, SLOTS, P])
        slope_now = sb("slope_now", [P, 2, 1])
        junk = sb("junk", [P, 2, CH], BF16)
        mx = sb("mx", [P, 2, NT, NCH])
        negm = sb("negm", [P, 2, NT])
        m_rest = sb("m_rest", [P, NT])
        m_part = sb("m_part", [P, 2, R_M, NT], BF16)
        m_row = sb("m_row", [R_M * NT, P], BF16)
        ident_b = sb("ident_b", [P, P], BF16)
        probs = sb("probs", [P, 4, T])
        o_sb = sb("o_sb", [P, CH])
        rsum = sb("rsum", [P, TC, NCH])
        attn = sb("attn", [P, NCH, TC, E])

        al_rest = attn[:].rearrange("p c t e -> p (c t e)")[:, 0:T]
        xn = v_all
        late = carver(bias_t[:].rearrange("p s n -> p (s n)"))
        attT = late([P, 3, KE, P])
        shift2 = late([P, TC])
        logits = late([P, NT, NX])
        top8 = late([P, NT, 8])
        top8_i = late([P, NT, 8], U32)
        top_i = late([P, NT, TOPK])
        top_w = late([P, NT, TOPK])
        top_e = late([P, NT, TOPK])
        top_s = late([P, NT])
        hot = late([P, NT, TOPK, NX])
        hot_a = late([P, NT, TOPK, NX])
        mask = late([P, NT, NX], BF16)
        before = late([P, NT, NX])
        over = late([P, NX, NT])
        n_tiles = late([P, NX])
        ends = late([P, NX])
        starts = late([P, NX])
        pos = late([P, NT, TOPK])
        pos_i = late([P, NT, TOPK], I32)
        lo_i = late([P, NT, TOPK], I32)
        hi_i = late([P, NT, TOPK], I32)
        lo_f = late([P, NT, TOPK])
        hi_f = late([P, NT, TOPK])
        tab_f = late([P, NTAB])
        tab_e = late([P, NTAB])
        slots_b = late([P, P], BF16)
        tab_i = late([P, NTAB, 2], I32)
        ended = late([NTAB, NX])
        exp_f = late([NTAB, 1])
        exp_i = late([1, NTAB], I32)
        late = carver(probs[:].rearrange("p s n -> p (s n)"))
        xg = late([P, 4, E])
        xT = late([P, 2, KE, P])
        silu = late([P, 2, INTER])
        hid = late([P, 2, INTER])
        hidT = late([P, 2, 2, P])
        y_sb = late([P, 4, E])
        idx = late([P, 4, 2], I32)
        idx_s = late([P, 4, 1], I32)
        tab_n = NT * TOPK
        late = carver(probs[:].rearrange("p s n -> p (s n)"))
        hot_lo = late([P, tab_n, P], BF16)
        hot_hi = late([P, 2, tab_n, NTAB], BF16)
        z_sb = [k_st[:, s // 2].rearrange("p s n -> p (s n)").bitcast(F32)[:, (s % 2) * 1024:(s % 2) * 1024 + 1024]
                for s in range(4)] + [q_st[:].rearrange("p s n -> p (s n)").bitcast(F32)[:, s * 1024:s * 1024 + 1024]
                                      for s in range(2)]
        z_sb += [hT[:, k, :] for k in range(KE)]
        z_sb = [z.rearrange("p (j e) -> p j e", j=TOPK) for z in z_sb]

        ps = ctx.enter_context(nc.psum_tensor("ps", [P, 8, CH], F32))
        ps_max = [ps[:, 0, :], ps[:, 1, :]]
        ps_st = [ps[:, 2:4, :], ps[:, 4:6, :]]
        ps_o = ps[:, 6, :]
        ps_misc = ps[:, 7, :]
        att_banks, y1_banks = (0, 1, 6), (2, 3, 7)
        ps_ot = ps_misc[:, 0:TC * NCH * VW].rearrange("p (t c d) -> p t c d", t=TC, c=NCH)

        x_in = [sem("x_in0"), sem("x_in1")]
        cond_in = sem("cond_in")
        wmod_in = [sem("wmod_in0"), sem("wmod_in1")]
        w_in = [sem(f"w_in{w}") for w in range(4)]
        ident_in = sem("ident_in")
        consts_in = sem("consts_in")
        dist_in = sem("dist_in")
        al_in = sem("al_in")
        sign_in = sem("sign_in")
        slopes_in = sem("slopes_in")
        router_in = sem("router_in")
        rows_in = sem("rows_in")
        silu_done = sem("silu_done")
        bc_done = sem("bc_done")
        var_done = sem("var_done")
        std_done = sem("std_done")
        xh_done = sem("xh_done")
        pe_group = sem("pe_group")
        dve_evac = sem("dve_evac")
        act_evac = sem("act_evac")
        mod_done = sem("mod_done")
        dve_chain = sem("dve_chain")
        q_bias_done = sem("q_bias_done")
        preload = sem("preload")
        sign_done = sem("sign_done")
        pool_chain = sem("pool_chain")
        raw_mod = sem("raw_mod")
        qk_first = sem("qk_first")
        qk_rest = sem("qk_rest")
        qk_second = sem("qk_second")
        qk_split = sem("qk_split")
        qk_stored = [sem(f"qk_stored{n}") for n in range(3)]
        al_done = sem("al_done")
        al_stored = sem("al_stored")
        v_done = sem("v_done")
        st_in = [sem(f"st_in{s}") for s in range(SLOTS)]
        al_ld = [sem(f"al_ld{s}") for s in range(SLOTS)]
        v_init = sem("v_init")
        slope_cp = sem("slope_cp")
        bias_t_done = sem("bias_t_done")
        bias_a_done = sem("bias_a_done")
        bias_p_done = sem("bias_p_done")
        bias_d_done = sem("bias_d_done")
        v_staged = sem("v_staged")
        max_ready = sem("max_ready")
        max_used = sem("max_used")
        negm_done = sem("negm_done")
        mT_ready = sem("mT_ready")
        m_chain = sem("m_chain")
        m_evac = sem("m_evac")
        m_stored = sem("m_stored")
        m_in = sem("m_in")
        st_ready = sem("st_ready")
        own_done = sem("own_done")
        exp_done = sem("exp_done")
        pv_done = sem("pv_done")
        o_evac = sem("o_evac")
        ot_ready = sem("ot_ready")
        ot_recip = sem("ot_recip")
        ot_used = sem("ot_used")
        settled = sem("settled")
        late_in = sem("late_in")
        wo_done = sem("wo_done")
        xg_done = sem("xg_done")
        w_done = sem("w_done")
        attT_ready = sem("attT_ready")
        attT_evac = sem("attT_evac")
        y1_ready = sem("y1_ready")
        x2_done = sem("x2_done")
        var2_done = sem("var2_done")
        stats_done = sem("stats_done")
        std2_done = sem("std2_done")
        rstd2_done = sem("rstd2_done")
        xn_done = [sem("xn_done0"), sem("xn_done1")]
        xn_stored = sem("xn_stored")
        xnT_ready = sem("xnT_ready")
        xnT_evac = sem("xnT_evac")
        logits_ready = sem("logits_ready")
        top_shift = sem("top_shift")
        top_exp = sem("top_exp")
        w_top_done = sem("w_top_done")
        mask_done = sem("mask_done")
        before_ready = sem("before_ready")
        hot_done = sem("hot_done")
        table_ready = sem("table_ready")
        exp_col = sem("exp_col")
        exp_row = sem("exp_row")
        tab_parts = sem("tab_parts")
        tab_done = sem("tab_done")
        idx_cp = sem("idx_cp")
        idx_s_cp = sem("idx_s_cp")
        gathered = [sem(f"gathered{s}") for s in range(4)]
        xgT_ready = sem("xgT_ready")
        xT_act = sem("xT_act")
        xT_dve = sem("xT_dve")
        gu_ready = sem("gu_ready")
        silu2_done = sem("silu2_done")
        hid_done = sem("hid_done")
        hidT_ready = sem("hidT_ready")
        hidT_evac = sem("hidT_evac")
        y_ready = sem("y_ready")
        y_evac = sem("y_evac")
        scattered = [sem(f"scattered{s}") for s in range(4)]
        z_in = [sem(f"z_in{t}") for t in range(NT)]
        z_scaled = sem("z_scaled")
        acc_pool = sem("acc_pool")
        acc_done = sem("acc_done")
        out_stored = sem("out_stored")

        block = ctx.enter_context(nc.Block())

        WQ, WK, MODA, XT, Q0, K0, WV, WO, MODB, GATE, V0, Q1, K1 = 0, 1, 2, 3, 7, 9, 11, 12, 13, 14, 15, 19, 21
        N_GROUPS = 23
        emptied_by = (["dve"] * 3 + ["act", "dve"] * 2 + ["act"] * 16)
        bank_of = [0, 1, 2, 3, 4, 5, 6, 7, 2, 3, 4, 5, 6, 2, 3, 4, 5, 6, 2, 3, 4, 5, 6]

        def count(group, engine):
            return sum(e == engine for e in emptied_by[:group + 1])

        def wait_emptied(eng, group):
            s = dve_evac if emptied_by[group] == "dve" else act_evac
            eng.wait_ge(s, count(group, emptied_by[group]))

        def settle(eng):
            eng.sem_inc(settled, 1)

        def at(i, c, per=SLOTS, k=1):
            return k * (4 * i + c)

        def is0(i):
            return isinstance(i, int) and i == 0

        def steps(eng, step):
            for c in (-2, -1, 0):
                step(0, c)
            with eng.Fori(0, 3) as i:
                for c in range(1, 1 + SLOTS):
                    step(i, c)
            for c in (1, 2, 3):
                step(3, c)

        def tiles(eng, tile, first, last):
            for k in range(first, 8):
                tile(0, k)
            with eng.Fori(2, MAX_TILES // 4) as i:
                for c in range(4):
                    tile(i, c)
            for k in range(MAX_TILES // 4 * 4, last):
                tile(MAX_TILES // 4, k - MAX_TILES // 4 * 4)

        def kind(i, c):
            if isinstance(i, int):
                h = 4 * i + c
                return h + 2 < H, 0 <= h + 1 < H, h >= 0, h >= 1
            return True, True, True, True

        @block.sync
        def _(sp):
            wm = a["wmod"].rearrange("(k p) m -> p k m", p=P)
            for k in range(2):
                sp.dma_start(x_sb[:, 4 * k:4 * k + 4, :],
                             a["x"].rearrange("(t p) e -> p t e", p=P)[:, 4 * k:4 * k + 4, :]).then_inc(x_in[k], 16)
            sp.dma_start(ident[:], a["ident"]).then_inc(ident_in, 16)

            def load_w(n):
                w = a[("Wq", "Wk", "Wv", "Wo")[n]]
                sp.dma_start(w_raw[:, n], w.rearrange("(k p) e -> p k e", p=P)).then_inc(w_in[n], 16)

            load_w(0)
            load_w(1)
            sp.dma_start(al_key[:], a["alibi_key"]).then_inc(al_in, 16)
            sp.dma_start(wmod[:, :, 2 * E:], wm[:, :, 2 * E:]).then_inc(wmod_in[1], 16)
            sp.dma_start(dist[:], a["dist"]).then_inc(dist_in, 16)
            load_w(2)
            load_w(3)
            sp.dma_start(rw_raw, a["router_w"]).then_inc(router_in, 16)
            sp.dma_start(q_st[R_QK:R_QK + R_AL], a["query_rows"].bitcast(BF16).unsqueeze(1).broadcast_to([R_AL, SLOTS, T])).then_inc(rows_in, 16)
            sp.dma_start(k_st[R_QK + R_AL:R_ALL].rearrange("p c s n -> p (c s) n"),
                         a["one_rows"].bitcast(BF16).unsqueeze(1).broadcast_to([R_M, NCH * SLOTS, T])).then_inc(rows_in, 16)

            def store_qk(n):
                f, first, last = ((0, 0, 2), (0, 2, HT), (1, 0, HT))[n]
                p0, p1 = D * first, D * last
                for w, rows in enumerate((q_rows, k_rows)):
                    sp.wait_ge(qk_split, 4 * f + 2 * w + 2)
                    g = 0
                    for k in (3, 2, 1):
                        src = (qk_part[p0:p1, w, f, 0:k, :] if w == 0 else
                               qk_part[p0:p1, w, f, 3 - k:4 - k, :].broadcast_to([p1 - p0, k, T]))
                        sp.dma_start(rows[g:g + k, P * f + p0:P * f + p1, :].rearrange("g r t -> r g t"),
                                     src).then_inc(qk_stored[n], 16)
                        g += k

            def load_qk(i, c):
                s, h = c % SLOTS, at(i, c)
                sp.dma_start(q_st[0:R_QK, s, :], q_rows[:, bass.ds(h * D, D), :]).then_inc(st_in[s], 16)
                for ch in range(NCH):
                    sp.dma_start(k_st[0:R_QK, ch, s, :], k_rows[:, bass.ds(h * D, D), :]).then_inc(st_in[s], 16)

            def load_al(i, c):
                s, h = c % SLOTS, at(i, c)
                for ch in range(NCH):
                    sp.dma_start(k_st[R_QK:R_QK + R_AL, ch, s, :], al_rows[:, bass.ds(h * NT + ch * TC, TC), :]).then_inc(al_ld[s], 16)

            store_qk(0)
            sp.wait_ge(qk_stored[0], 16 * 6)
            load_qk(0, 0)
            load_qk(0, 1)
            store_qk(1)
            sp.wait_ge(al_done, 1)
            sp.wait_ge(sign_done, 1)
            sp.dma_start(al_rows.rearrange("g r n -> r g n"), al_part[:]).then_inc(al_stored, 16)
            sp.wait_ge(al_stored, 16)
            load_al(0, 0)
            load_al(0, 1)
            sp.wait_ge(qk_stored[1], 16 * 6)

            def step(i, c):
                _, rows, _, _ = kind(i, c)
                if not isinstance(i, int) or 2 <= 4 * i + c + 3 < H:
                    if not isinstance(i, int) or 4 * i + c >= 1:
                        sp.wait_ge(st_ready, at(i, c, k=NT))
                    load_qk(i, c + 3)
                    load_al(i, c + 3)
                if is0(i) and c == 0:
                    store_qk(2)
                if rows:
                    g = c + 1
                    sp.wait_ge(m_evac, at(i, g) + 1)
                    sp.dma_start(m_rows[at(i, g)].rearrange("r i x -> (r i) x"), m_row[:]).then_inc(m_stored, 16)
                    sp.wait_ge(m_stored, at(i, g, k=16) + 16)
                    sp.dma_start(q_st[R_QK + R_AL:R_ALL, g % SLOTS, :],
                                 m_rows[at(i, g)].rearrange("r i x -> r (i x)")).then_inc(m_in, 16)
                if is0(i) and c == 0:
                    sp.wait_ge(qk_stored[2], 16 * 6)

            steps(sp, step)

            for hf in range(NCH):
                sp.wait_ge(xn_done[hf], TC)
                sp.dma_start(xn_rows.rearrange("(t p) e -> p t e", p=P)[:, TC * hf:TC * hf + TC, :],
                             xn[:, TC * hf:TC * hf + TC, :]).then_inc(xn_stored, 16)
            for s in range(4):
                sp.wait_ge(scattered[s], 16 * len(range(s, MAX_TILES, 4)))
            for t in range(NT):
                sp.dma_start(z_sb[t], z_rows.rearrange("(j t p) e -> p t j e", p=P, j=TOPK)[:, t]).then_inc(z_in[t], 16)
            for t in range(NT):
                if t in SUM_DVE:
                    sp.wait_ge(acc_done, SUM_DVE.index(t) + 1)
                else:
                    sp.wait_ge(acc_pool, SUM_POOL.index(t) + 1)
                sp.dma_start(out[P * t:P * t + P, :], x_sb[:, t, :]).then_inc(out_stored, 16)
            sp.wait_ge(out_stored, 16 * NT)

        @block.scalar
        def _(act):
            calls = [0]

            def call_table(func):
                calls[0] += 1
                act.activation(table_call[:, calls[0]:calls[0] + 1], table_call[:, 0:1], func)

            act.dma_start(cond[:], a["c"].rearrange("o (k p) -> p (o k)", p=P), allow_slow_non_contiguous=True).then_inc(cond_in, 16)
            wm = a["wmod"].rearrange("(k p) m -> p k m", p=P)
            act.dma_start(wmod[:, :, 0:2 * E], wm[:, :, 0:2 * E]).then_inc(wmod_in[0], 16)
            act.wait_ge(preload, 1)
            call_table(ACT.Sqrt)
            act.wait_ge(var_done, 1)
            act.activation(std[:], std[:], ACT.Sqrt).then_inc(std_done, 1)
            act.wait_ge(cond_in, 16)
            act.activation(cond_silu[:], cond[:], ACT.Silu).then_inc(silu_done, 1)
            act.wait_ge(mod_done, 1)
            for ch in range(NCH):
                g = XT + KE * ch
                act.wait_ge(pe_group, g + 1)
                act.activation(hT[:, 0, CH * ch:CH * ch + CH], ps[:, bank_of[g], :], ACT.Identity,
                               bias=modc[:, 0, 0:1], scale=modc[:, 1, 0:1]).then_inc(act_evac, 1)

            def evac_qk(n, g, w, f, ch):
                act.wait_ge(pe_group, g + 1)
                if n >= 2:
                    act.wait_ge(qk_rest, n - 1)
                bias = q_bias_s[:, f:f + 1] if w == 0 else qk_bias[:, 1, f:f + 1]
                act.activation(qk_f[:, n % 2], ps[:, bank_of[g], :], ACT.Identity, bias=bias,
                               scale=D ** -0.5 if w == 0 else 1.0).then_inc(act_evac, 1)
                act.wait_ge(act_evac, count(g, "act"))
                act.copy(qk_part[:, w, f, 0, CH * ch:CH * ch + CH], qk_f[:, n % 2]).then_inc(qk_first, 1)

            def second_part(n, w, f, ch):
                act.wait_ge(qk_rest, n + 1)
                act.copy(qk_part[:, w, f, 1, CH * ch:CH * ch + CH], qk_r[:, n % 2]).then_inc(qk_second, 1)

            def make_bias_t(i, c, third):
                if not (isinstance(i, int) and 4 * i + c < 2):
                    act.wait_ge(max_used, at(i, c - 1, k=16))
                settle(act)
                w = W_DIST // 3
                act.activation(bias_t[:, c % 2, w * third:w * third + w], dist[:, w * third:w * third + w], ACT.Identity,
                               scale=slopes[:, bass.ds(at(i, c), 1)]).then_inc(bias_t_done if third < 2 else bias_a_done, 1)

            act.wait_ge(consts_in, 16 * 4)
            act.wait_ge(q_bias_done, 1)
            for n in range(4):
                evac_qk(n, Q0 + n, n // 2, 0, n % 2)
            for w in range(2, 4):
                act.wait_ge(pe_group, WV + w - 1)
                act.copy(wT[:, w].rearrange("p k f -> p (k f)"), ps[:, bank_of[WV + w - 2], :]).then_inc(act_evac, 1)
            act.wait_ge(dist_in, 16)
            act.wait_ge(slopes_in, 16)
            for third in range(3):
                make_bias_t(0, 0, third)
            act.wait_ge(pe_group, MODB + 1)
            act.copy(modc[:, 2:4, :].rearrange("p m k -> p (m k)"), ps[:, bank_of[MODB], 0:2 * KE]).then_inc(raw_mod, 1)
            act.copy(rwT[:].rearrange("p k n -> p (k n)"), ps[:, bank_of[MODB], 32:32 + KE * NX]).then_inc(act_evac, 1)
            act.wait_ge(pe_group, GATE + 1)
            act.copy(gates[:].rearrange("p g e -> p (g e)"), ps[:, bank_of[GATE], :]).then_inc(act_evac, 1)
            for g in range(4):
                act.wait_ge(pe_group, V0 + g + 1)
                act.copy(v_all[:, 2 * g:2 * g + 2, :].rearrange("p t e -> p (t e)"), ps[:, bank_of[V0 + g], :]).then_inc(act_evac, 1)
            for third in range(3):
                make_bias_t(0, 1, third)
            call_table(ACT.Exp)
            for n in range(4, 8):
                evac_qk(n, Q1 + n - 4, (n - 4) // 2, 1, n % 2)
                if n > 4:
                    second_part(n - 1, (n - 5) // 2, 1, (n - 1) % 2)
            second_part(7, 1, 1, 1)
            for third in range(3):
                make_bias_t(0, 2, third)

            def step(i, c):
                _, rows, probabilities, output = kind(i, c)
                for j in range(NT):
                    if probabilities:
                        first = is0(i) and c == 0
                        if j in OWN_DVE:
                            act.wait_ge(own_done, at(i, c, k=len(OWN_DVE)) + OWN_DVE.index(j) + 1)
                        else:
                            act.wait_ge(st_ready, at(i, c, k=NT) + j + 1)
                        if not first or j >= 4:
                            act.wait_ge(pv_done, at(i, c, k=4) + (j - 4) // 2 + 1)
                        act.activation(probs[:, j % 4, :], ps_st[j % 2].rearrange("p b n -> p (b n)"),
                                       ACT.Exp).then_inc(exp_done, 1)
                    if output and j == 1:
                        evac_o(i, c - 1)
                    if j in (3, 5) and (not isinstance(i, int) or 0 <= 4 * i + c and 4 * i + c + 3 < H):
                        make_bias_t(i, c + 3, (j - 3) // 2)
                    if rows and j == 4:
                        evac_rows(i, c + 1)

            def evac_o(i, c):
                act.wait_ge(pv_done, at(i, c, k=4) + 4)
                if not (is0(i) and c == 0):
                    act.wait_ge(ot_ready, at(i, c) + 1)
                act.copy(o_sb[:], ps_o).then_inc(o_evac, 1)

            def evac_rows(i, g):
                act.wait_ge(mT_ready, at(i, g) + 1)
                if not (is0(i) and g == 0):
                    act.wait_ge(m_stored, at(i, g, k=16))
                act.copy(m_row[:], ps_misc[0:R_M * NT, 256:256 + P]).then_inc(m_evac, 1)

            steps(act, step)
            evac_o(3, 3)

            def evac_att(t):
                act.wait_ge(attT_ready, t + 1)
                if t >= 3:
                    act.wait_ge(y1_ready, t - 2)
                act.copy(attT[:, t % 3], ps[:, att_banks[t % 3], 0:E].rearrange("p (k n) -> p k n", k=KE)).then_inc(attT_evac, 1)

            def root(hf):
                act.wait_ge(var2_done, hf + 1)
                act.activation(std[:, TC * hf:TC * hf + TC], std[:, TC * hf:TC * hf + TC], ACT.Sqrt).then_inc(std2_done, 1)

            call_table(ACT.Sqrt)
            for t in range(6):
                evac_att(t)
            root(0)
            for t in range(6, NT):
                evac_att(t)
            act.wait_ge(rstd2_done, 1)
            for t in range(TC):
                act.activation(xn[:, t, :], x_sb[:, t, :], ACT.Identity, bias=shift2[:, t:t + 1],
                               scale=rstd[:, t:t + 1]).then_inc(xn_done[0], 1)
            root(1)
            for g in range(4):
                hf, k = g // KE, g % KE
                act.wait_ge(xnT_ready, g + 1)
                act.activation(hT[:, k, CH * hf:CH * hf + CH], ps[:, 4 + g, :], ACT.Identity,
                               bias=modc[:, 2, k:k + 1], scale=modc[:, 3, k:k + 1]).then_inc(xnT_evac, 1)
            call_table(ACT.Exp)
            act.wait_ge(top_shift, 1)
            act.activation(top_e, top_w, ACT.Exp).then_inc(top_exp, 1)
            call_table(ACT.Silu)

            def tile(i, c):
                k = 4 * i + c if isinstance(i, int) else None
                if k is None or k + 1 < MAX_TILES:
                    act.wait_ge(xgT_ready, at(i, c + 1) + 1)
                    if k is None or k + 1 >= 2:
                        act.wait_ge(gu_ready, at(i, c + 1) - 1)
                    act.activation(xT[:, (c + 1) % 2, 0, :], ps[:, 0, 0:P], ACT.Identity,
                                   bias=modc[:, 2, 0:1], scale=modc[:, 3, 0:1]).then_inc(xT_act, 1)
                if k is None or 0 <= k - 1 < MAX_TILES:
                    act.wait_ge(hidT_ready, at(i, c - 1) + 1)
                    if k is None or k - 1 >= 2:
                        act.wait_ge(y_ready, at(i, c - 1) - 1)
                    act.copy(hidT[0:IH, (c - 1) % 2], ps[0:IH, 4 + (c - 1) % 2, 0:2 * P].rearrange("p (a n) -> p a n", a=2)).then_inc(hidT_evac, 1)
                if k is None or 0 <= k < MAX_TILES:
                    act.wait_ge(gu_ready, at(i, c) + 1)
                    if k is None or k >= 2:
                        act.wait_ge(hid_done, at(i, c) - 1)
                    act.activation(silu[:, c % 2, :], ps[:, 2 + c % 2, 0:INTER], ACT.Silu).then_inc(silu2_done, 1)

            tiles(act, tile, -1, MAX_TILES + 1)

            act.wait_ge(w_top_done, 1)
            for t in SUM_POOL:
                act.wait_ge(z_in[t], 16)
                for j in range(TOPK):
                    act.activation(z_sb[t][:, j, :], z_sb[t][:, j, :], ACT.Identity,
                                   scale=top_w[:, t, j:j + 1]).then_inc(z_scaled, 1)

        @block.gpsimd
        def _(pool):
            pool.dma_start(al_sign[:], a["alibi_sign"]).then_inc(sign_in, 16)
            pool.dma_start(slope_hc[:], bass.AP(a["slopes"].tensor, a["slopes"].offset, [[1, H], [0, NT], [1, 1]])).then_inc(sign_in, 16)
            pool.dma_start(slopes[:], on_partitions(a["slopes"], P)).then_inc(slopes_in, 16)
            for n, b in enumerate(("bq", "bk")):
                pool.dma_start(qk_bias[:, n, :], a[b].rearrange("(k p) -> p k", p=P), allow_slow_non_contiguous=True).then_inc(consts_in, 16)
            pool.dma_start(v_bias[:], on_partitions(a["bv"], P)).then_inc(consts_in, 16)
            pool.dma_start(o_bias[:], on_partitions(a["bo"], P)).then_inc(consts_in, 16)
            pool.dma_start(x_bias[:], on_partitions(a["expert_bias"], P)).then_inc(late_in, 16)
            pool.dma_start(triangle[:].rearrange("p a b -> p (a b)"), a["triangle"].bitcast(BF16)).then_inc(late_in, 16)
            pool.dma_start(route[:], a["route"]).then_inc(late_in, 16)
            pool.memset(v_st[:], 0.0).then_inc(v_init, 1)
            pool.wait_ge(v_init, 1)
            pool.memset(v_st[:, :, :, D:D + 1], 1.0).then_inc(v_init, 1)

            def take_slope(i, c):
                if not (isinstance(i, int) and 4 * i + c < 2):
                    pool.wait_ge(bias_d_done, at(i, c) - 1)
                pool.tensor_copy(slope_now[:, c % 2, :], slopes[:, bass.ds(at(i, c), 1)]).then_inc(slope_cp, 1)
                pool.wait_ge(slope_cp, at(i, c) + 1)

            def make_bias_p(i, c):
                s = c % 2
                w = 2 * W_DIST // 3
                pool.wait_ge(max_used, at(i, c - 1, k=16))
                settle(pool)
                pool.tensor_scalar(bias_t[:, s, w:], dist[:, w:], slope_now[:, s, :], None, ALU.mult).then_inc(bias_p_done, 1)

            def make_bias_d(i, c):
                s = c % 2
                if not isinstance(i, int) or 4 * i + c >= SLOTS:
                    pool.wait_ge(exp_done, at(i, c - 3, k=NT))
                settle(pool)
                pool.tensor_scalar(bias_d[:, c % SLOTS, :], dist[:, DIST0:DIST0 + P], slope_now[:, s, :], None,
                                   ALU.mult).then_inc(bias_d_done, 1)

            def stage_v(i, c):
                if not isinstance(i, int) or 4 * i + c >= 2:
                    pool.wait_ge(pv_done, at(i, c - 1, k=4))
                pool.tensor_copy(v_st[:, c % 2, :, 0:D], v_all[:, :, bass.ds(at(i, c, k=D), D)]).then_inc(v_staged, 1)

            chain = [0]

            def link(ins):
                chain[0] += 1
                ins.then_inc(pool_chain, 1)
                pool.wait_ge(pool_chain, chain[0])

            pool.wait_ge(al_in, 16)
            pool.wait_ge(sign_in, 32)
            link(pool.tensor_scalar(al_key[:], al_key[:], slope_hc[:, 0:1], None, ALU.mult))
            link(pool.tensor_copy(al_part[:, 0, :], al_key[:]))
            link(pool.tensor_tensor(al_rest[:], al_key[:], al_part[:, 0, :], ALU.subtract))

            def third_part(n, w, f, ch):
                pool.wait_ge(qk_second, n + 1)
                pool.tensor_tensor(qk_part[:, w, f, 2, CH * ch:CH * ch + CH], qk_r[:, n % 2],
                                   qk_part[:, w, f, 1, CH * ch:CH * ch + CH], ALU.subtract).then_inc(qk_split, 1)

            def rest_of(n, w, f, ch):
                pool.wait_ge(qk_first, n + 1)
                pool.wait_ge(qk_split, n - 1)
                pool.tensor_tensor(qk_r[:, n % 2], qk_f[:, n % 2], qk_part[:, w, f, 0, CH * ch:CH * ch + CH],
                                   ALU.subtract).then_inc(qk_rest, 1)

            for n in range(4):
                third_part(n, n // 2, 0, n % 2)
            link(pool.tensor_copy(al_part[:, 1, :], al_rest[:]))
            pool.tensor_tensor(al_part[:, 2, :], al_rest[:], al_part[:, 1, :], ALU.subtract).then_inc(al_done, 1)
            pool.wait_ge(dist_in, 16)
            pool.wait_ge(slopes_in, 16)
            for h in range(3):
                take_slope(0, h)
                make_bias_d(0, h)
            pool.wait_ge(consts_in, 16 * 4)
            for g in range(4):
                pool.wait_ge(act_evac, count(V0 + g, "act"))
                last = pool.tensor_tensor(v_all[:, 2 * g:2 * g + 2, :], v_all[:, 2 * g:2 * g + 2, :],
                                          v_bias[:].unsqueeze(1).broadcast_to([P, 2, E]), ALU.add)
                last.then_inc(v_done, 1)
            pool.wait_ge(v_init, 2)
            pool.wait_ge(v_done, 4)
            stage_v(0, 0)
            stage_v(0, 1)
            for n in range(4, 8):
                rest_of(n, (n - 4) // 2, 1, n % 2)
                if n > 4:
                    third_part(n - 1, (n - 5) // 2, 1, (n - 1) % 2)
            third_part(7, 1, 1, 1)
            pool.wait_ge(raw_mod, 1)
            pool.tensor_scalar(modc[:, 3, :], modc[:, 3, :], 1.0, None, ALU.add).then_inc(raw_mod, 1)
            pool.wait_ge(act_evac, count(GATE, "act"))
            link(pool.tensor_scalar(gsign[:], gates[:], 0.0, 2.0, ALU.is_ge, ALU.mult))
            link(pool.tensor_scalar(gsign[:], gsign[:], -1.0, None, ALU.add))
            link(pool.tensor_tensor(gabs[:], gates[:], gsign[:], ALU.mult))
            link(pool.tensor_scalar(gabs[:], gabs[:], GATE_MIN, None, ALU.max))
            link(pool.tensor_tensor(gates[:], gabs[:], gsign[:], ALU.mult))
            pool.wait_ge(act_evac, count(WO, "act"))
            pool.tensor_tensor(wo_sb[:], wT[:, 3], gates[:, 0:1, :].broadcast_to([P, KE, E]), ALU.mult).then_inc(wo_done, 1)
            link(pool.tensor_tensor(o_bias[:], o_bias[:], gates[:, 0, :], ALU.mult))
            pool.wait_ge(xh_done, NT)
            pool.tensor_tensor(x_sb[:], x_sb[:], o_bias[:].unsqueeze(1).broadcast_to([P, NT, E]), ALU.add).then_inc(xg_done, 1)

            def load_expert(i, c):
                n = at(i, c)
                for half, name in enumerate(("gate_proj", "up_proj")):
                    pool.dma_start(w_gu[:, bass.ds(n, 1), :, INTER * half:INTER * half + INTER],
                                   a[name][bass.ds(n, 1)].rearrange("x (k p) n -> p x k n", p=P)).then_inc(w_done, 16)
                pool.dma_start(w_dn[0:IH, bass.ds(n, 1), :, :],
                               a["down_proj"][bass.ds(n, 1)].rearrange("x (k p) n -> p x k n", p=IH)).then_inc(w_done, 16)

            def step(i, c):
                static = isinstance(i, int)
                h = 4 * i + c if static else None
                if not static or 1 <= h and h + 1 < H:
                    stage_v(i, c + 1)
                if not static or 0 <= h and h + 3 < H:
                    take_slope(i, c + 3)
                    make_bias_p(i, c + 3)
                    make_bias_d(i, c + 3)
                if static and h == 0:
                    for n in range(3):
                        pool.wait_ge(qk_stored[n], 16 * 6)
                    pool.wait_ge(al_stored, 16)
                    pool.wait_ge(wo_done, 1)
                    pool.wait_ge(pe_group, N_GROUPS)
                if not static or h >= 0:
                    load_expert(i, c)

            steps(pool, step)

            pool.wait_ge(tab_done, 1)
            pool.wait_ge(xn_stored, 32)

            def tile(i, c):
                k = 4 * i + c if isinstance(i, int) else None
                if k is None or 0 <= k + 3 < MAX_TILES:
                    s = (c + 3) % 4
                    if k is None or k + 3 >= 4:
                        pool.wait_ge(xgT_ready, at(i, c + 3) - 3)
                        pool.wait_ge(idx_cp, at(i, c + 3))
                    settle(pool)
                    pool.tensor_copy(idx[:, s, :].unsqueeze(1), tab_i[:, bass.ds(at(i, c + 3), 1), :]).then_inc(idx_cp, 1)
                    pool.wait_ge(idx_cp, at(i, c + 3) + 1)
                    settle(pool)
                    pool.indirect_dma_start(xg[:, s, :], None, xn_rows,
                                            bass.IndirectOffsetOnAxis(ap=idx[:, s, 0:1].bitcast(U32), axis=0),
                                            bounds_check=T - 1, oob_is_err=False).then_inc(gathered[s], 16)
                if k is None or 0 <= k - 3 < MAX_TILES:
                    s = (c - 3) % 4
                    pool.wait_ge(y_evac, at(i, c - 3) + 1)
                    settle(pool)
                    pool.tensor_copy(idx_s[:, s, :].unsqueeze(1), tab_i[:, bass.ds(at(i, c - 3), 1), 1:2]).then_inc(idx_s_cp, 1)
                    pool.wait_ge(idx_s_cp, at(i, c - 3) + 1)
                    settle(pool)
                    pool.indirect_dma_start(z_rows, bass.IndirectOffsetOnAxis(ap=idx_s[:, s, :].bitcast(U32), axis=0),
                                            y_sb[:, s, :], None, bounds_check=TOPK * T - 1,
                                            oob_is_err=False).then_inc(scattered[s], 16)

            tiles(pool, tile, -3, MAX_TILES + 3)

            for n, t in enumerate(SUM_POOL):
                for j in range(TOPK):
                    pool.wait_ge(z_scaled, TOPK * n + j + 1)
                    ins = pool.tensor_tensor(x_sb[:, t, :], x_sb[:, t, :], z_sb[t][:, j, :], ALU.add)
                    if j < TOPK - 1:
                        link(ins)
                ins.then_inc(acc_pool, 1)

        @block.vector
        def _(dve):
            chain = [0]
            dve.sem_inc(ot_used, 1)
            dve.memset(table_call[:, 0:1], 1.0).then_inc(preload, 1)
            dve.memset(junk[:], 0.0).then_inc(preload, 1)

            def link(ins):
                chain[0] += 1
                ins.then_inc(dve_chain, 1)
                dve.wait_ge(dve_chain, chain[0])

            for t in range(NT):
                if t % 4 == 0:
                    dve.wait_ge(x_in[t // 4], 16)
                last = dve.bn_stats(stats[:, t, :], x_sb[:, t, :])
            link(last)
            for t in range(NT):
                last = dve.bn_aggr(mv[:, t, :], stats[:, t, :])
            link(last)
            dve.tensor_scalar(std[:], mv[:, :, 1], LN_EPS, None, ALU.add).then_inc(var_done, 1)
            dve.wait_ge(std_done, 1)
            link(dve.reciprocal(rstd[:], std[:]))
            for t in range(NT):
                dve.tensor_scalar(xh[:, t, :], x_sb[:, t, :], mv[:, t, 0:1], rstd[:, t:t + 1],
                                  ALU.subtract, ALU.mult).then_inc(xh_done, 1)
            for w in range(2):
                dve.wait_ge(pe_group, WQ + w + 1)
                dve.tensor_copy(wT[:, w].rearrange("p k f -> p (k f)"), ps[:, bank_of[WQ + w], :]).then_inc(dve_evac, 1)
            dve.wait_ge(sign_in, 32)
            link(dve.tensor_scalar(al_sign[:], al_sign[:], slope_hc[:, 0:1], None, ALU.mult))
            link(dve.tensor_copy(sign_part[:, 0, :], al_sign[:]))
            link(dve.tensor_tensor(al_sign[:], al_sign[:], sign_part[:, 0, :], ALU.subtract))
            link(dve.tensor_copy(sign_part[:, 1, :], al_sign[:]))
            link(dve.tensor_tensor(sign_part[:, 2, :], al_sign[:], sign_part[:, 1, :], ALU.subtract))
            dve.tensor_copy(al_part[:, 3:6, :].rearrange("p g (j n) -> p g j n", n=P),
                            sign_part[:].unsqueeze(3).broadcast_to([P, 3, NT, P])).then_inc(sign_done, 1)
            dve.wait_ge(pe_group, MODA + 1)
            dve.tensor_copy(modc[:, 0:2, :].rearrange("p m k -> p (m k)"), ps[:, bank_of[MODA], 0:2 * KE]).then_inc(dve_evac, 1)
            dve.wait_ge(dve_evac, MODA + 1)
            dve.tensor_scalar(modc[:, 1, :], modc[:, 1, :], 1.0, None, ALU.add).then_inc(mod_done, 1)
            dve.wait_ge(mod_done, 1)
            for ch in range(NCH):
                g = XT + KE * ch + 1
                dve.wait_ge(pe_group, g + 1)
                dve.tensor_scalar(hT[:, 1, CH * ch:CH * ch + CH], ps[:, bank_of[g], :], modc[:, 1, 1:2], modc[:, 0, 1:2],
                                  ALU.mult, ALU.add).then_inc(dve_evac, 1)
            dve.tensor_copy(cond_bc[:], cond_silu[:].unsqueeze(2).broadcast_to([P, KE, P])).then_inc(bc_done, 1)
            dve.tensor_copy(ident_b[:], ident[:])
            dve.wait_ge(consts_in, 16 * 4)
            dve.tensor_scalar(q_bias_s[:], qk_bias[:, 0, :], D ** -0.5, None, ALU.mult).then_inc(q_bias_done, 1)
            for n in range(4):
                w, ch = n // 2, n % 2
                dve.wait_ge(qk_first, n + 1)
                if n >= 2:
                    dve.wait_ge(qk_split, n - 1)
                dve.tensor_tensor(qk_r[:, n % 2], qk_f[:, n % 2], qk_part[:, w, 0, 0, CH * ch:CH * ch + CH],
                                  ALU.subtract).then_inc(qk_rest, 1)
                dve.wait_ge(qk_rest, n + 1)
                dve.tensor_copy(qk_part[:, w, 0, 1, CH * ch:CH * ch + CH], qk_r[:, n % 2]).then_inc(qk_second, 1)

            def step(i, c):
                maxima, rows, probabilities, output = kind(i, c)
                g = c + 2
                for q in range(NT):
                    if maxima:
                        if q == 0:
                            dve.wait_ge(bias_t_done, at(i, g, k=2) + 2)
                            if is0(i):
                                dve.wait_ge(bias_a_done, g + 1)
                            else:
                                dve.wait_ge(bias_p_done, at(i, g) - 2)
                        for half in range(NCH):
                            n = 2 * q + half
                            dve.wait_ge(max_ready, at(i, g, k=16) + n + 1)
                            settle(dve)
                            off = DIST0 + CH * half - P * q
                            dve.tensor_tensor_reduce(
                                junk[:, half, :], ps_max[half], bias_t[:, g % 2, off:off + CH], 1.0, -3.0e38,
                                ALU.add, ALU.max, mx[:, g % 2, q, half:half + 1]).then_inc(max_used, 1)
                            if probabilities and half == 0 and q in OWN_DVE:
                                own_tile(i, c, q)
                            if rows and n == 0:
                                total_max(i, c + 1)
                            elif rows and n < 5:
                                split_rows(i, c + 1, n - 1)
                    elif rows and q == 0:
                        total_max(i, c + 1)
                        for n in range(4):
                            split_rows(i, c + 1, n)
                    if not maxima and probabilities and q in OWN_DVE:
                        own_tile(i, c, q)
                    if output and q == 6:
                        normalise(i, c - 1)

            def own_tile(i, c, j):
                t, bank = j % TC, ps_st[j % 2][:, j // TC, :]
                if j == OWN_DVE[0]:
                    dve.wait_ge(bias_d_done, at(i, c) + 1)
                dve.wait_ge(st_ready, at(i, c, k=NT) + j + 1)
                dve.tensor_tensor(bank[:, t * P:t * P + P], bank[:, t * P:t * P + P], bias_d[:, c % SLOTS, :],
                                  ALU.add).then_inc(own_done, 1)

            def total_max(i, g):
                dve.wait_ge(max_used, at(i, g, k=16) + 16)
                dve.tensor_reduce(negm[:, g % 2, :], mx[:, g % 2], AX_X, ALU.max, negate=True).then_inc(negm_done, 1)

            def split_rows(i, g, n):
                full, rest, part = negm[:, g % 2, :], m_rest[:], m_part[:, g % 2]
                if n == 0:
                    dve.wait_ge(negm_done, at(i, g) + 1)
                    settle(dve)
                else:
                    dve.wait_ge(m_chain, at(i, g, k=4) + n)
                (dve.tensor_copy(part[:, 0, :], full) if n == 0 else
                 dve.tensor_tensor(rest, full, part[:, 0, :], ALU.subtract) if n == 1 else
                 dve.tensor_copy(part[:, 1, :], rest) if n == 2 else
                 dve.tensor_tensor(part[:, 2, :], rest, part[:, 1, :], ALU.subtract)).then_inc(m_chain, 1)

            def normalise(i, c):
                dve.wait_ge(ot_ready, at(i, c) + 2)
                if not (is0(i) and c == 0):
                    dve.wait_ge(ot_used, at(i, c) + 1)
                dve.reciprocal(rsum[:], ps_ot[:, :, :, D]).then_inc(ot_recip, 1)
                dve.wait_ge(ot_recip, at(i, c) + 1)
                dve.tensor_tensor(attn[:, :, :, bass.ds(at(i, c, k=D), D)].rearrange("p c t d -> p t c d"),
                                  ps_ot[:, :, :, 0:D], rsum[:].unsqueeze(3).broadcast_to([P, TC, NCH, D]),
                                  ALU.mult).then_inc(ot_used, 1)

            steps(dve, step)
            normalise(3, 3)

            dve.wait_ge(xg_done, 1)

            def residual(t):
                dve.wait_ge(y1_ready, t + 1)
                dve.tensor_tensor(x_sb[:, t, :], ps[:, y1_banks[t % 3], 0:E], x_sb[:, t, :], ALU.add).then_inc(x2_done, 1)
                dve.wait_ge(x2_done, t + 1)
                dve.bn_stats(stats[:, t, :], x_sb[:, t, :]).then_inc(stats_done, 1)

            def variance(hf):
                dve.wait_ge(stats_done, TC * hf + TC)
                for n in range(TC * hf, TC * hf + TC):
                    last = dve.bn_aggr(mv[:, n, :], stats[:, n, :])
                link(last)
                dve.tensor_scalar(std[:, TC * hf:TC * hf + TC], mv[:, TC * hf:TC * hf + TC, 1], LN_EPS, None,
                                  ALU.add).then_inc(var2_done, 1)

            for t in range(TC):
                residual(t)
            variance(0)
            residual(4)
            residual(5)
            dve.wait_ge(std2_done, 1)
            link(dve.reciprocal(rstd[:, 0:TC], std[:, 0:TC]))
            dve.scalar_tensor_tensor(out=shift2, in0=mv[:, 0:TC, 0], scalar=-1.0, in1=rstd[:, 0:TC],
                                     op0=ALU.mult, op1=ALU.mult).then_inc(rstd2_done, 1)
            residual(6)
            residual(7)
            variance(1)
            dve.wait_ge(std2_done, 2)
            link(dve.reciprocal(rstd[:, TC:NT], std[:, TC:NT]))
            for t in range(TC, NT):
                dve.tensor_scalar(xn[:, t, :], x_sb[:, t, :], mv[:, t, 0:1], rstd[:, t:t + 1],
                                  ALU.subtract, ALU.mult).then_inc(xn_done[1], 1)
            col = [NCH * VW]

            def consts(n):
                col[0] += n
                return route[:, col[0] - n:col[0]]
            c_experts, c_sizes, c_tiles, c_slots, c_token, c_code = (consts(n) for n in (NX, NT, NTAB, P, 1, NT * TOPK))
            dve.wait_ge(late_in, 16 * 3)
            for hf in range(NCH):
                dve.wait_ge(logits_ready, hf + 1)
                link(dve.tensor_tensor(logits[:, TC * hf:TC * hf + TC, :],
                                       ps[:, hf, 0:TC * NX].rearrange("p (t x) -> p t x", t=TC),
                                       x_bias[:].unsqueeze(1).broadcast_to([P, TC, NX]), ALU.add))
                for t in range(TC * hf, TC * hf + TC):
                    last = dve.max(top8[:, t, :], logits[:, t, :])
                link(last)
                for t in range(TC * hf, TC * hf + TC):
                    last = dve.max_index(top8_i[:, t, :], top8[:, t, :], logits[:, t, :])
                link(last)
                r = slice(TC * hf, TC * hf + TC)
                link(dve.tensor_copy(top_i[:, r], top8_i[:, r, 0:TOPK]))
                link(dve.tensor_tensor(hot[:, r], top_i[:, r].unsqueeze(3).broadcast_to([P, TC, TOPK, NX]),
                                       c_experts.unsqueeze(1).unsqueeze(1).broadcast_to([P, TC, TOPK, NX]), ALU.is_equal))
                link(dve.tensor_reduce(before[:, r], hot[:, r].rearrange("p t j x -> p t x j"), AX_X, ALU.add))
                dve.tensor_copy(mask[:, r], before[:, r]).then_inc(mask_done, 1)
            dve.tensor_tensor(top_w, top8[:, :, 0:TOPK], top8[:, :, 0:1].broadcast_to([P, NT, TOPK]),
                              ALU.subtract).then_inc(top_shift, 1)
            dve.wait_ge(top_exp, 1)
            link(dve.tensor_reduce(top_s, top_e, AX_X, ALU.add))
            link(dve.reciprocal(top_s, top_s))
            dve.tensor_tensor(top_w, top_e, top_s.unsqueeze(2).broadcast_to([P, NT, TOPK]), ALU.mult).then_inc(w_top_done, 1)
            dve.wait_ge(before_ready, 1)
            counts = ps[:, 3, 0:NX]
            link(dve.tensor_tensor(over, counts.unsqueeze(2).broadcast_to([P, NX, NT]),
                                   c_sizes.unsqueeze(1).broadcast_to([P, NX, NT]), ALU.is_gt))
            link(dve.tensor_reduce(n_tiles, over, AX_X, ALU.add))
            dve.memset(starts, 1.0)
            link(dve.tensor_copy(before, ps[:, 2, 0:P].rearrange("p (t x) -> p t x", t=NT)))
            link(dve.tensor_tensor_scan(ends, starts, n_tiles, 0.0, ALU.mult, ALU.add))
            link(dve.tensor_tensor(starts, ends, n_tiles, ALU.subtract))
            link(dve.tensor_scalar(starts, starts, float(P), None, ALU.mult))
            link(dve.tensor_scalar(ended, ends[0:NTAB], c_token[0:NTAB], None, ALU.is_lt))
            link(dve.tensor_reduce(exp_f, ended, AX_X, ALU.add))
            dve.tensor_scalar(exp_f, exp_f, float(NX - 1), None, ALU.min).then_inc(exp_col, 1)
            link(dve.tensor_tensor(before, before, starts.unsqueeze(1).broadcast_to([P, NT, NX]), ALU.add))
            link(dve.tensor_tensor(hot_a, hot, before.unsqueeze(2).broadcast_to([P, NT, TOPK, NX]), ALU.mult))
            link(dve.tensor_reduce(pos, hot_a, AX_X, ALU.add))
            link(dve.tensor_copy(pos_i, pos))
            dve.tensor_scalar(hi_i, pos_i, 7, None, ALU.logical_shift_right)
            link(dve.tensor_scalar(lo_i, pos_i, P - 1, None, ALU.bitwise_and))
            dve.tensor_copy(hi_f, hi_i)
            link(dve.tensor_copy(lo_f, lo_i))
            link(dve.tensor_copy(slots_b, c_slots))
            dve.tensor_tensor(hot_hi[:, 0], hi_f.rearrange("p t j -> p (t j)").unsqueeze(2).broadcast_to([P, tab_n, NTAB]),
                              c_tiles.unsqueeze(1).broadcast_to([P, tab_n, NTAB]), ALU.is_equal).then_inc(hot_done, 1)
            dve.wait_ge(hot_done, 1)
            dve.tensor_tensor(hot_hi[:, 1], hot_hi[:, 0], c_code.unsqueeze(2).broadcast_to([P, tab_n, NTAB]),
                              ALU.mult).then_inc(hot_done, 1)
            dve.wait_ge(hot_done, 2)
            dve.tensor_scalar(hot_hi[:, 0], hot_hi[:, 0], c_token, None, ALU.mult).then_inc(hot_done, 1)
            for n in range(tab_n):
                dve.tensor_scalar(hot_lo[:, n, :], slots_b, lo_f[:, n // TOPK, n % TOPK:n % TOPK + 1], None,
                                  ALU.is_equal).then_inc(hot_done, 1)
            dve.wait_ge(exp_row, 1)
            dve.tensor_copy(exp_i, ps[0:1, 5, 0:NTAB])
            dve.wait_ge(table_ready, 1)
            dve.tensor_copy(tab_f, ps[:, 4, 0:NTAB])
            dve.tensor_scalar(tab_e, ps[:, 4, 0:NTAB], 0.0, 2.0 * TOPK * T, ALU.is_equal, ALU.mult).then_inc(tab_parts, 1)
            dve.wait_ge(tab_parts, 1)
            link(dve.scalar_tensor_tensor(out=tab_f, in0=ps[:, 4, NTAB:2 * NTAB], scalar=float(P), in1=tab_f,
                                          op0=ALU.mult, op1=ALU.add))
            link(dve.scalar_tensor_tensor(out=tab_i[:, :, 1], in0=tab_f, scalar=-1.0, in1=tab_e, op0=ALU.add, op1=ALU.add))
            dve.tensor_scalar(tab_i[:, :, 0], tab_i[:, :, 1], T - 1, None, ALU.bitwise_and).then_inc(tab_done, 1)

            def tile(i, c):
                k = 4 * i + c if isinstance(i, int) else None
                if k is None or k + 1 < MAX_TILES:
                    dve.wait_ge(xgT_ready, at(i, c + 1) + 1)
                    if k is None or k + 1 >= 2:
                        dve.wait_ge(gu_ready, at(i, c + 1) - 1)
                    dve.tensor_scalar(xT[:, (c + 1) % 2, 1, :], ps[:, 1, 0:P], modc[:, 3, 1:2], modc[:, 2, 1:2],
                                      ALU.mult, ALU.add).then_inc(xT_dve, 1)
                if k is None or 0 <= k < MAX_TILES:
                    dve.wait_ge(silu2_done, at(i, c) + 1)
                    if k is None or k >= 2:
                        dve.wait_ge(hidT_ready, at(i, c) - 1)
                    dve.tensor_tensor(hid[:, c % 2, :], silu[:, c % 2, :], ps[:, 2 + c % 2, INTER:2 * INTER],
                                      ALU.mult).then_inc(hid_done, 1)
                if k is None or 0 <= k - 2 < MAX_TILES:
                    s = (c - 2) % 4
                    dve.wait_ge(y_ready, at(i, c - 2) + 1)
                    if k is None or k - 2 >= 4:
                        dve.wait_ge(scattered[s], (i + (c - 2) // 4) * 16)
                    dve.tensor_tensor(y_sb[:, s, :], ps[:, 6 + c % 2, 0:E], gates[:, 1, :], ALU.mult).then_inc(y_evac, 1)

            tiles(dve, tile, -1, MAX_TILES + 2)

            for t in SUM_DVE:
                dve.wait_ge(z_in[t], 16)
                for j in range(TOPK):
                    ins = dve.scalar_tensor_tensor(out=x_sb[:, t, :], in0=z_sb[t][:, j, :], scalar=top_w[:, t, j:j + 1],
                                                   in1=x_sb[:, t, :], op0=ALU.mult, op1=ALU.add)
                    if j < TOPK - 1:
                        link(ins)
                ins.then_inc(acc_done, 1)

        @block.tensor
        def _(pe):
            def group(g):
                b = bank_of[g]
                if b in bank_of[:g]:
                    wait_emptied(pe, max(n for n in range(g) if bank_of[n] == b))
                return ps[:, b, :]

            def transpose_w(w, g):
                pe.wait_ge(w_in[w], 16)
                b = group(g)
                for k in range(KE):
                    for f in range(KE):
                        last = pe.transpose(b[:, k * E + f * P:k * E + f * P + P],
                                            w_raw[:, w, f, k * P:k * P + P], ident[:])
                last.then_inc(pe_group, 1)

            def modulations(b, first, n):
                for m in range(KE * n):
                    for k in range(KE):
                        o = (KE * first + m) * P
                        last = pe.matmul(b[:, m:m + 1], wmod[:, k, o:o + P], cond_silu[:, k:k + 1],
                                         start=(k == 0), stop=(k == KE - 1))
                return last

            def project_t(g, w, f, ch, k):
                b = group(g) if k == 0 else ps[:, bank_of[g], :]
                ins = pe.matmul(b, wT[:, w, k, f * P:f * P + P], hT[:, k, CH * ch:CH * ch + CH],
                                start=(k == 0), stop=(k == KE - 1))
                if k == KE - 1:
                    ins.then_inc(pe_group, 1)

            def later_group(n):
                if n == 0:
                    pe.wait_ge(wmod_in[1], 16)
                    b = group(MODB)
                    modulations(b, 3, 2)
                    pe.wait_ge(router_in, 16)
                    for k in range(KE):
                        last = pe.transpose(b[:, 32 + k * NX:32 + k * NX + NX], rw_raw[:, k * P:k * P + P], ident[0:NX, 0:NX])
                    last.then_inc(pe_group, 1)
                elif n == 1:
                    pe.wait_ge(bc_done, 1)
                    b = group(GATE)
                    for n, m in enumerate((2, 5)):
                        for k in range(KE):
                            last = pe.matmul(b[:, n * E:n * E + E], cond_bc[:, k, :], wmod[:, k, m * E:m * E + E],
                                             start=(k == 0), stop=(k == KE - 1))
                    last.then_inc(pe_group, 1)
                else:
                    pe.wait_ge(act_evac, count(WV, "act"))
                    b = group(V0 + n - 2)
                    for half in range(2):
                        t = 2 * (n - 2) + half
                        for k in range(KE):
                            last = pe.matmul(b[:, half * E:half * E + E], hT[:, k, t * P:t * P + P], wT[:, 2, k, :],
                                             start=(k == 0), stop=(k == KE - 1))
                    last.then_inc(pe_group, 1)

            def keep_warm(n, bank):
                for _ in range(n):
                    pe.matmul(ps[:, bank, :], junk[:, 0, 0:P], junk[:, 1, :], start=True, stop=True)

            pe.wait_ge(preload, 2)
            keep_warm(WARM_LOAD, bank_of[Q0])
            pe.wait_ge(ident_in, 16)
            for w in range(2):
                transpose_w(w, WQ + w)
            pe.wait_ge(wmod_in[0], 16)
            pe.wait_ge(silu_done, 1)
            modulations(group(MODA), 0, 2).then_inc(pe_group, 1)
            for n in range(4):
                ch, k = n // KE, n % KE
                pe.wait_ge(xh_done, TC * ch + TC)
                b = group(XT + n)
                for t in range(TC):
                    last = pe.transpose(b[:, t * P:t * P + P], xh[:, TC * ch + t, k * P:k * P + P], ident[:])
                last.then_inc(pe_group, 1)
            for g0, w in ((Q0, 0), (K0, 1)):
                for ch in range(NCH):
                    pe.wait_ge(act_evac, count(XT + KE * ch, "act"))
                    pe.wait_ge(dve_evac, count(XT + KE * ch + 1, "dve"))
                    for k in range(KE):
                        project_t(g0 + ch, w, 0, ch, k)
            for w in range(2, 4):
                transpose_w(w, WV - 2 + w)
            for n in range(6):
                later_group(n)

            def step(i, c):
                maxima, rows, probabilities, output = kind(i, c)
                if is0(i) and c == 0:
                    pe.wait_ge(act_evac, count(N_GROUPS - 1, "act"))
                    pe.wait_ge(rows_in, 16 * 2)
                    pe.wait_ge(late_in, 16 * 3)
                for j in range(NT):
                    if maxima:
                        scores(i, c + 2, j, 0)
                    if is0(i) and c == -2:
                        n = j // KE
                        project_t(Q1 + n, n // NCH, 1, n % NCH, j % KE)
                    if probabilities:
                        scores_t(i, c, j)
                    if maxima:
                        scores(i, c + 2, j, 1)
                    if probabilities:
                        if j not in OWN_DVE:
                            own_tile(i, c, j)
                        if j % 2 == 1 and j >= 3:
                            sum_pv(i, c, (j - 3) // 2)
                    if output and j == 1:
                        sum_pv(i, c - 1, 3)
                    if rows and j == 3:
                        rows_t(i, c + 1)
                    if output and j == 5:
                        merge_o(i, c - 1)

            def loaded(i, c):
                pe.wait_ge(st_in[c % SLOTS], 48 * (i + c // SLOTS) + 48)

            def scores(i, c, q, half):
                s = c % SLOTS
                if q == 0 and half == 0:
                    loaded(i, c)
                n = 2 * q + half
                if n >= 2 or not (is0(i) and c == 0):
                    pe.wait_ge(max_used, at(i, c, k=16) + n - 1)
                pe.matmul(ps_max[half], q_st[0:R_QK, s, q * P:q * P + P],
                          k_st[0:R_QK, 0, s, CH * half:CH * half + CH], start=True, stop=True).then_inc(max_ready, 1)

            def scores_t(i, c, j):
                s = c % SLOTS
                if j == 0:
                    pe.wait_ge(m_in, at(i, c, k=16) + 16)
                    pe.wait_ge(al_ld[s], 32 * (i + c // SLOTS) + 32)
                    pe.wait_ge(bias_d_done, at(i, c) + 1)
                if j >= 2 or not (is0(i) and c == 0):
                    pe.wait_ge(exp_done, at(i, c, k=NT) + j - 1)
                for ch in range(NCH):
                    last = pe.matmul(ps_st[j % 2][:, ch, :], k_st[0:R_ALL, ch, s, j * P:j * P + P],
                                     q_st[0:R_ALL, s, CH * ch:CH * ch + CH], start=True,
                                     stop=j // TC != ch or j in OWN_DVE)
                if j in OWN_DVE:
                    last.then_inc(st_ready, 1)

            def own_tile(i, c, j):
                t = j % TC
                pe.matmul(ps_st[j % 2][:, j // TC, t * P:t * P + P], ident[:], bias_d[:, c % SLOTS, :],
                          start=False, stop=True).then_inc(st_ready, 1)

            def sum_pv(i, c, pair):
                if pair == 0:
                    pe.wait_ge(v_staged, at(i, c) + 1)
                    if not (is0(i) and c == 0):
                        pe.wait_ge(o_evac, at(i, c))
                pe.wait_ge(exp_done, at(i, c, k=NT) + 2 * pair + 2)
                for n in range(2):
                    j = 2 * pair + n
                    for ch in range(NCH):
                        r = 32 * (2 * n + ch)
                        last = pe.matmul(ps_o[r:r + 32], v_st[:, c % 2, j, :], probs[:, j % 4, CH * ch:CH * ch + CH],
                                         start=(pair == 0), stop=(pair == 3))
                last.then_inc(pv_done, 1)

            def rows_t(i, g):
                pe.wait_ge(m_chain, at(i, g, k=4) + 4)
                if not (is0(i) and g < 2):
                    pe.wait_ge(ot_used, at(i, g) - 1)
                if is0(i) and g == 0:
                    pe.wait_ge(act_evac, count(Q0, "act"))
                pe.matmul(ps_misc[0:R_M * NT, 256:256 + P], m_part[:, g % 2].rearrange("p r i -> p (r i)"), ident_b[:],
                          start=True, stop=True).then_inc(mT_ready, 1)

            def merge_o(i, c):
                pe.wait_ge(o_evac, at(i, c) + 1)
                if not (is0(i) and c == 0):
                    pe.wait_ge(ot_used, at(i, c) + 1)
                nr = c + 2
                if not (isinstance(i, int) and 4 * i + nr >= H):
                    pe.wait_ge(m_evac, at(i, nr) + 1)
                for t in range(TC):
                    last = pe.matmul(ps_ot[:, t].rearrange("p c d -> p (c d)"), o_sb[:, t * P:t * P + P], merge[:],
                                     start=True, stop=True)
                last.then_inc(ot_ready, 1)

            pe.sem_inc(ot_ready, 1)
            steps(pe, step)
            sum_pv(3, 3, 3)
            merge_o(3, 3)

            pe.wait_ge(wo_done, 1)
            for t in range(NT + 1):
                if t < NT:
                    pe.wait_ge(ot_used, H + 1)
                    if t >= 3:
                        pe.wait_ge(attT_evac, t - 2)
                    for k in range(KE):
                        last = pe.transpose(ps[:, att_banks[t % 3], k * P:k * P + P],
                                            attn[:, t // TC, t % TC, k * P:k * P + P], ident[:])
                    last.then_inc(attT_ready, 1)
                if t >= 1:
                    n = t - 1
                    pe.wait_ge(attT_evac, n + 1)
                    if n >= 3:
                        pe.wait_ge(x2_done, n - 2)
                    for k in range(KE):
                        last = pe.matmul(ps[:, y1_banks[n % 3], 0:E], attT[:, n % 3, k, :], wo_sb[:, k, :],
                                         start=(k == 0), stop=(k == KE - 1))
                    last.then_inc(y1_ready, 1)
            for hf in range(NCH):
                pe.wait_ge(xn_done[hf], TC)
                for k in range(KE):
                    for t in range(TC):
                        last = pe.transpose(ps[:, 4 + KE * hf + k, t * P:t * P + P], xn[:, TC * hf + t, k * P:k * P + P], ident[:])
                    last.then_inc(xnT_ready, 1)
            for hf in range(NCH):
                pe.wait_ge(xnT_evac, KE * hf + KE)
                for t in range(TC):
                    for k in range(KE):
                        last = pe.matmul(ps[:, hf, t * NX:t * NX + NX], hT[:, k, (TC * hf + t) * P:(TC * hf + t) * P + P],
                                         rwT[:, k, :], start=(k == 0), stop=(k == KE - 1))
                last.then_inc(logits_ready, 1)
            pe.wait_ge(mask_done, NCH)
            flat_mask = mask.rearrange("p t x -> p (t x)")
            for n in range(1, NT):
                pe.matmul(ps[:, 2, n * NX:P], triangle[:, 1, :], flat_mask[:, 0:P - n * NX], start=(n == 1), stop=False,
                          skip_group_check=True)
            pe.matmul(ps[:, 2, 0:P], triangle[:, 0, :], flat_mask, start=False, stop=True, skip_group_check=True)
            for n in range(NT):
                last = pe.matmul(ps[:, 3, 0:NX], triangle[:, 1, :], mask[:, n, :], start=(n == 0), stop=(n == NT - 1))
            last.then_inc(before_ready, 1)
            pe.wait_ge(exp_col, 1)
            pe.transpose(ps[0:1, 5, 0:NTAB], exp_f, ident[0:NTAB, 0:NTAB]).then_inc(exp_row, 1)
            for n in range(tab_n):
                pe.wait_ge(hot_done, 4 + n)
                last = pe.matmul(ps[:, 4, 0:2 * NTAB], hot_lo[:, n, :], hot_hi[:, :, n, :], start=(n == 0),
                                 stop=(n == tab_n - 1))
            last.then_inc(table_ready, 1)
            keep_warm(WARM_GATHER, 6)
            pe.wait_ge(tab_done, 1)
            pe.wait_ge(w_done, 16 * 3 * NX)

            def expert(i, c):
                return pe.value_load(exp_i[0:1, bass.ds(at(i, c), 1)], min_val=0, max_val=NX - 1)

            def tile(i, c):
                k = 4 * i + c if isinstance(i, int) else None
                if k is None or 0 <= k < MAX_TILES:
                    e = expert(i, c)
                if k is None or k + 1 < MAX_TILES:
                    s = (c + 1) % 4
                    pe.wait_ge(gathered[s], (i + (c + 1) // 4) * 16 + 16)
                    if k is None or k + 1 >= 1:
                        pe.wait_ge(xT_act, at(i, c + 1))
                        pe.wait_ge(xT_dve, at(i, c + 1))
                    for kk in range(KE):
                        last = pe.transpose(ps[:, kk, 0:P], xg[:, s, kk * P:kk * P + P], ident[:])
                    last.then_inc(xgT_ready, 1)
                if k is None or 0 <= k - 1 < MAX_TILES:
                    pe.wait_ge(hid_done, at(i, c - 1) + 1)
                    if k is None or k - 1 >= 2:
                        pe.wait_ge(hidT_evac, at(i, c - 1) - 1)
                    for kk in range(2):
                        last = pe.transpose(ps[0:IH, 4 + (c - 1) % 2, kk * P:kk * P + P],
                                            hid[:, (c - 1) % 2, kk * IH:kk * IH + IH], ident[:])
                    last.then_inc(hidT_ready, 1)
                if k is None or 0 <= k < MAX_TILES:
                    pe.wait_ge(xT_act, at(i, c) + 1)
                    pe.wait_ge(xT_dve, at(i, c) + 1)
                    if k is None or k >= 2:
                        pe.wait_ge(hid_done, at(i, c) - 1)
                    for kk in range(KE):
                        last = pe.matmul(ps[:, 2 + c % 2, 0:2 * INTER], xT[:, c % 2, kk, :],
                                         w_gu[:, bass.ds(e, 1), kk, :].rearrange("p x n -> p (x n)"),
                                         start=(kk == 0), stop=(kk == KE - 1))
                    last.then_inc(gu_ready, 1)
                if k is None or 0 <= k - 2 < MAX_TILES:
                    e2 = expert(i, c - 2)
                    pe.wait_ge(hidT_evac, at(i, c - 2) + 1)
                    if k is None or k - 2 >= 2:
                        pe.wait_ge(y_evac, at(i, c - 2) - 1)
                    for kk in range(2):
                        last = pe.matmul(ps[:, 6 + c % 2, 0:E], hidT[0:IH, c % 2, kk, :],
                                         w_dn[0:IH, bass.ds(e2, 1), kk, :].rearrange("p x n -> p (x n)"),
                                         start=(kk == 0), stop=(kk == 1))
                    last.then_inc(y_ready, 1)

            tiles(pe, tile, -1, MAX_TILES + 2)


_INPUTS = {"x": "L0_attn_x", "Wq": "L0_attn_Wq", "Wk": "L0_attn_Wk", "Wv": "L0_attn_Wv", "Wo": "L0_attn_Wo",
           "bq": "L0_attn_bq", "bk": "L0_attn_bk", "bv": "L0_attn_bv", "bo": "L0_attn_bo",
           "slopes": "L0_attn_slopes", "router_w": "L0_ffn_router_w", "expert_bias": "L0_ffn_expert_bias",
           "gate_proj": "L0_ffn_gate_proj", "up_proj": "L0_ffn_up_proj", "down_proj": "L0_ffn_down_proj",
           "c": "L0_c", "wmod": "L0_wmod"}


def kernel(**inputs):
    import concourse.bacc as bacc
    from concourse.bass_utils import run_bass_kernel_spmd

    nc = bacc.Bacc("TRN2", target_bir_lowering=False, num_devices=1)
    arrays = {short: np.ascontiguousarray(inputs[name]) for short, name in _INPUTS.items()}
    arrays["x"] = arrays["x"].reshape(T, E)
    arrays.update(host_constants())
    aps = {n: nc.dram_tensor(f"in_{n}", v.shape, mybir.dt.from_np(v.dtype), kind="ExternalInput").ap()
           for n, v in arrays.items()}
    out = nc.dram_tensor("out_0", (T, E), F32, kind="ExternalOutput").ap()
    adaln_block(nc, aps, out)
    r = run_bass_kernel_spmd(nc, [{f"in_{n}": v for n, v in arrays.items()}], core_ids=[0])
    return r.results[0]["out_0"].reshape(1, T, E)
```
